# Optimizing a Trainium2 kernel written in Bass

```python
import numpy as np
import jax
import jax.numpy as jnp

def _softmax(x, axis=-1):
    return jax.nn.softmax(x, axis=axis)
def _gelu(x):
    return jax.nn.gelu(x, approximate=True)
def _silu(x):
    return jax.nn.silu(x)
def _sigmoid(x):
    return jax.nn.sigmoid(x)
def _layernorm(x, axis=-1, eps=1e-5):
    m = jnp.mean(x, axis=axis, keepdims=True)
    v = jnp.var(x, axis=axis, keepdims=True)
    return (x - m) / jnp.sqrt(v + eps)
def _scatter_add(tgt, idx, src, axis=0):
    return tgt.at[idx].add(src)
def _segment_sum(src, seg, n):
    return jax.ops.segment_sum(src, seg, n)

kernel_name = 'mk_conv_seq_d4_conv_nhwc256_1ae12a'

def setup_inputs(seed: int = 0):
    np.random.seed(seed)
    _w = jnp.asarray
    def _rec_inputs():
        import jax
        import jax.numpy as jnp
        _gk = jax.random.key(seed)
        x = -0.0005207 + 1.001 * jax.random.normal(jax.random.fold_in(_gk, 1), (2, 64, 64, 256), jnp.float32)
        return x
    x = _rec_inputs()
    def _L0_conv_setup():
        import jax, jax.numpy as jnp
        import numpy as np
        key = jax.random.key(seed)
        ks = jax.random.split(key, 8)
        B, S, K, D = (2, 64, 64, 256)
        C = D // 8
        return {'x': jax.random.normal(ks[0], (B, S, K, D), dtype=jnp.float32), 'Wq': jax.random.normal(ks[1], (C, D), dtype=jnp.float32) * (1.0 / np.sqrt(D)), 'bq': jax.random.normal(ks[2], (C,), dtype=jnp.float32) * 0.01, 'Wk': jax.random.normal(ks[3], (C, D), dtype=jnp.float32) * (1.0 / np.sqrt(D)), 'bk': jax.random.normal(ks[4], (C,), dtype=jnp.float32) * 0.01, 'Wv': jax.random.normal(ks[5], (D, D), dtype=jnp.float32) * (1.0 / np.sqrt(D)), 'bv': jax.random.normal(ks[6], (D,), dtype=jnp.float32) * 0.01, 'gamma': jax.random.uniform(ks[7], (1,), dtype=jnp.float32)}
    _L0_conv_all = _L0_conv_setup()
    _L0_conv_in = {k: v for k, v in _L0_conv_all.items() if k in ('Wq', 'bq', 'Wk', 'bk', 'Wv', 'bv', 'gamma', )}
    del _L0_conv_all

    def _L1_conv_setup():
        import jax, jax.numpy as jnp
        import numpy as np
        BN_EPS = 0.001

        def conv1x1(x, w):
            return jnp.einsum('nchw,oc->nohw', x, w)

        def bn(x, gamma, beta, mean, var):
            scale = gamma / jnp.sqrt(var + BN_EPS)
            shift = beta - mean * scale
            return x * scale[None, :, None, None] + shift[None, :, None, None]

        def fourier_unit(x, w, gamma, beta, mean, var):
            N, C, H, W = x.shape
            norm = jnp.sqrt(jnp.float32(W))
            f = jnp.fft.rfft(x / norm, axis=-1)
            Wf = f.shape[-1]
            ff = jnp.stack([jnp.real(f), jnp.imag(f)], axis=2).reshape(N, 2 * C, H, Wf)
            y = jax.nn.relu(bn(conv1x1(ff, w), gamma, beta, mean, var))
            Co = y.shape[1] // 2
            y = y.reshape(N, Co, 2, H, Wf)
            c = jax.lax.complex(y[:, :, 0], y[:, :, 1])
            return jnp.fft.irfft(c, n=W, axis=-1) * norm
        key = jax.random.key(seed)
        ks = jax.random.split(key, 20)
        N, H, W, Cin = (8, 128, 128, 256)
        fmaps = 256
        half = fmaps // 2

        def nrm(k, shape, s=0.05):
            return jax.random.normal(k, shape, dtype=jnp.float32) * s

        def bn_params(k, c):
            k1, k2, k3, k4 = jax.random.split(k, 4)
            gamma = jax.random.uniform(k1, (c,), dtype=jnp.float32) + 0.5
            beta = nrm(k2, (c,), 0.1)
            mean = nrm(k3, (c,), 0.1)
            var = jax.random.uniform(k4, (c,), dtype=jnp.float32) + 0.5
            return (gamma, beta, mean, var)
        x = jax.random.normal(ks[0], (N, H, W, Cin), dtype=jnp.float32)
        w1 = nrm(ks[1], (half, Cin))
        g1, b1, m1, v1 = bn_params(ks[2], half)
        fu_w = nrm(ks[3], (2 * half, 2 * half))
        fu_g, fu_b, fu_m, fu_v = bn_params(ks[4], 2 * half)
        lfu_w = nrm(ks[5], (2 * half, 2 * half))
        lfu_g, lfu_b, lfu_m, lfu_v = bn_params(ks[6], 2 * half)
        w2 = nrm(ks[7], (fmaps, half))
        return {'x': x, 'w1': w1, 'g1': g1, 'b1': b1, 'm1': m1, 'v1': v1, 'fu_w': fu_w, 'fu_g': fu_g, 'fu_b': fu_b, 'fu_m': fu_m, 'fu_v': fu_v, 'lfu_w': lfu_w, 'lfu_g': lfu_g, 'lfu_b': lfu_b, 'lfu_m': lfu_m, 'lfu_v': lfu_v, 'w2': w2}
    _L1_conv_all = _L1_conv_setup()
    _L1_conv_in = {k: v for k, v in _L1_conv_all.items() if k in ('w1', 'g1', 'b1', 'm1', 'v1', 'fu_w', 'fu_g', 'fu_b', 'fu_m', 'fu_v', 'lfu_w', 'lfu_g', 'lfu_b', 'lfu_m', 'lfu_v', 'w2', )}
    del _L1_conv_all

    def _L2_conv_setup():
        import jax, jax.numpy as jnp
        import numpy as np
        EPS = 1e-05
        D_CONV = 4

        def rmsnorm(x, w):
            return x * jax.lax.rsqrt(jnp.mean(x * x, axis=-1, keepdims=True) + EPS) * w

        def layernorm(x, w, b):
            m = jnp.mean(x, axis=-1, keepdims=True)
            v = jnp.mean((x - m) ** 2, axis=-1, keepdims=True)
            return (x - m) * jax.lax.rsqrt(v + EPS) * w + b

        def mamba_mixer(x, W_in, conv_w, conv_b, W_x, W_dt, b_dt, A_log, Dp, W_out):
            B, L, C = x.shape
            I = W_out.shape[1]
            N = A_log.shape[1]
            R = W_dt.shape[1]
            proj = x @ W_in.T
            hs, gate = jnp.split(proj, 2, axis=-1)
            hs_c = jax.lax.conv_general_dilated(hs.transpose(0, 2, 1), conv_w, (1,), [(D_CONV - 1, 0)], dimension_numbers=('NCH', 'OIH', 'NCH'), feature_group_count=I)
            hs = jax.nn.silu(hs_c.transpose(0, 2, 1) + conv_b)
            ssm_in = hs @ W_x.T
            dt_r, Bm, Cm = jnp.split(ssm_in, [R, R + N], axis=-1)
            dt = jax.nn.softplus(dt_r @ W_dt.T + b_dt)
            A = -jnp.exp(A_log)

            def step(state, inp):
                dt_t, B_t, C_t, u_t = inp
                dA = jnp.exp(dt_t[:, :, None] * A)
                state = dA * state + dt_t[:, :, None] * B_t[:, None, :] * u_t[:, :, None]
                y = jnp.einsum('bin,bn->bi', state, C_t)
                return (state, y)
            xs = (dt.transpose(1, 0, 2), Bm.transpose(1, 0, 2), Cm.transpose(1, 0, 2), hs.transpose(1, 0, 2))
            state0 = jnp.zeros((B, I, N), x.dtype)
            _, ys = jax.lax.scan(step, state0, xs)
            y = ys.transpose(1, 0, 2) + hs * Dp
            y = y * jax.nn.silu(gate)
            return y @ W_out.T

        def forward_scan(x, W_in, conv_w, conv_b, W_x, W_dt, b_dt, A_log, Dp, W_out, rms_w1, rms_wf):
            h = x + mamba_mixer(rmsnorm(x, rms_w1), W_in, conv_w, conv_b, W_x, W_dt, b_dt, A_log, Dp, W_out)
            return rmsnorm(h, rms_wf)
        key = jax.random.key(seed)
        ks = jax.random.split(key, 12)
        BT, H, W, C = (8, 32, 32, 256)
        I, N, R = (2 * C, 16, 16)
        s = 0.02
        x = jax.random.normal(ks[0], (BT, H, W, C), jnp.float32)
        W_in = jax.random.normal(ks[1], (2 * I, C), jnp.float32) * s
        conv_w = jax.random.normal(ks[2], (I, 1, D_CONV), jnp.float32) * s
        conv_b = jax.random.normal(ks[3], (I,), jnp.float32) * s
        W_x = jax.random.normal(ks[4], (R + 2 * N, I), jnp.float32) * s
        W_dt = jax.random.normal(ks[5], (I, R), jnp.float32) * s
        b_dt = jax.random.normal(ks[6], (I,), jnp.float32) * 0.1
        A_log = jnp.log(jnp.broadcast_to(jnp.arange(1, N + 1, dtype=jnp.float32), (I, N)))
        Dp = jnp.ones((I,), jnp.float32)
        W_out = jax.random.normal(ks[7], (C, I), jnp.float32) * s
        rms_w1 = jnp.ones((C,), jnp.float32)
        rms_wf = jnp.ones((C,), jnp.float32)
        ln_w = jnp.ones((C,), jnp.float32)
        ln_b = jnp.zeros((C,), jnp.float32)
        return {'x': x, 'W_in': W_in, 'conv_w': conv_w, 'conv_b': conv_b, 'W_x': W_x, 'W_dt': W_dt, 'b_dt': b_dt, 'A_log': A_log, 'Dp': Dp, 'W_out': W_out, 'rms_w1': rms_w1, 'rms_wf': rms_wf, 'ln_w': ln_w, 'ln_b': ln_b}
    _L2_conv_all = _L2_conv_setup()
    _L2_conv_in = {k: v for k, v in _L2_conv_all.items() if k in ('W_in', 'conv_w', 'conv_b', 'W_x', 'W_dt', 'b_dt', 'A_log', 'Dp', 'W_out', 'rms_w1', 'rms_wf', 'ln_w', 'ln_b', )}
    del _L2_conv_all

    def _L3_conv_setup():
        import jax, jax.numpy as jnp
        import numpy as np
        EPS = 1e-05
        M_PER_GROUP = 16
        key = jax.random.key(seed)
        k1, = jax.random.split(key, 1)
        N, H, W, C = (128, 32, 32, 256)
        x = jax.random.normal(k1, (N, H, W, C), dtype=jnp.float32)
        gamma = jnp.ones((1, 1, 1, C), dtype=jnp.float32)
        beta = jnp.zeros((1, 1, 1, C), dtype=jnp.float32)
        return {'x': x, 'gamma': gamma, 'beta': beta}
    _L3_conv_all = _L3_conv_setup()
    _L3_conv_in = {k: v for k, v in _L3_conv_all.items() if k in ('gamma', 'beta', )}
    del _L3_conv_all

    return {
        "x": x,
        "L0_conv_Wq": _L0_conv_in["Wq"],
        "L0_conv_bq": _L0_conv_in["bq"],
        "L0_conv_Wk": _L0_conv_in["Wk"],
        "L0_conv_bk": _L0_conv_in["bk"],
        "L0_conv_Wv": _L0_conv_in["Wv"],
        "L0_conv_bv": _L0_conv_in["bv"],
        "L0_conv_gamma": _L0_conv_in["gamma"],
        "L1_conv_w1": _L1_conv_in["w1"],
        "L1_conv_g1": _L1_conv_in["g1"],
        "L1_conv_b1": _L1_conv_in["b1"],
        "L1_conv_m1": _L1_conv_in["m1"],
        "L1_conv_v1": _L1_conv_in["v1"],
        "L1_conv_fu_w": _L1_conv_in["fu_w"],
        "L1_conv_fu_g": _L1_conv_in["fu_g"],
        "L1_conv_fu_b": _L1_conv_in["fu_b"],
        "L1_conv_fu_m": _L1_conv_in["fu_m"],
        "L1_conv_fu_v": _L1_conv_in["fu_v"],
        "L1_conv_lfu_w": _L1_conv_in["lfu_w"],
        "L1_conv_lfu_g": _L1_conv_in["lfu_g"],
        "L1_conv_lfu_b": _L1_conv_in["lfu_b"],
        "L1_conv_lfu_m": _L1_conv_in["lfu_m"],
        "L1_conv_lfu_v": _L1_conv_in["lfu_v"],
        "L1_conv_w2": _L1_conv_in["w2"],
        "L2_conv_W_in": _L2_conv_in["W_in"],
        "L2_conv_conv_w": _L2_conv_in["conv_w"],
        "L2_conv_conv_b": _L2_conv_in["conv_b"],
        "L2_conv_W_x": _L2_conv_in["W_x"],
        "L2_conv_W_dt": _L2_conv_in["W_dt"],
        "L2_conv_b_dt": _L2_conv_in["b_dt"],
        "L2_conv_A_log": _L2_conv_in["A_log"],
        "L2_conv_Dp": _L2_conv_in["Dp"],
        "L2_conv_W_out": _L2_conv_in["W_out"],
        "L2_conv_rms_w1": _L2_conv_in["rms_w1"],
        "L2_conv_rms_wf": _L2_conv_in["rms_wf"],
        "L2_conv_ln_w": _L2_conv_in["ln_w"],
        "L2_conv_ln_b": _L2_conv_in["ln_b"],
        "L3_conv_gamma": _L3_conv_in["gamma"],
        "L3_conv_beta": _L3_conv_in["beta"],
    }

def reference(x, L0_conv_Wq, L0_conv_bq, L0_conv_Wk, L0_conv_bk, L0_conv_Wv, L0_conv_bv, L0_conv_gamma, L1_conv_w1, L1_conv_g1, L1_conv_b1, L1_conv_m1, L1_conv_v1, L1_conv_fu_w, L1_conv_fu_g, L1_conv_fu_b, L1_conv_fu_m, L1_conv_fu_v, L1_conv_lfu_w, L1_conv_lfu_g, L1_conv_lfu_b, L1_conv_lfu_m, L1_conv_lfu_v, L1_conv_w2, L2_conv_W_in, L2_conv_conv_w, L2_conv_conv_b, L2_conv_W_x, L2_conv_W_dt, L2_conv_b_dt, L2_conv_A_log, L2_conv_Dp, L2_conv_W_out, L2_conv_rms_w1, L2_conv_rms_wf, L2_conv_ln_w, L2_conv_ln_b, L3_conv_gamma, L3_conv_beta):
    import jax
    import jax.numpy as jnp
    def _L0_conv_ref(x, Wq, bq, Wk, bk, Wv, bv, gamma):
        import jax, jax.numpy as jnp
        import numpy as np
        B, S, K, D = x.shape
        N = K * S
        xp = jnp.transpose(x, (0, 3, 2, 1)).reshape(B, D, N)
        q = jnp.einsum('cd,bdn->bnc', Wq, xp) + bq
        k = jnp.einsum('cd,bdn->bcn', Wk, xp) + bk[:, None]
        energy = jnp.einsum('bnc,bcm->bnm', q, k)
        attention = jax.nn.softmax(energy, axis=-1)
        v = jnp.einsum('ed,bdn->ben', Wv, xp) + bv[:, None]
        out = jnp.einsum('bdj,bij->bdi', v, attention)
        out = gamma * out + xp
        out = out.reshape(B, D, K, S)
        return jnp.transpose(out, (0, 3, 2, 1))

    def _L1_conv_ref(x, w1, g1, b1, m1, v1, fu_w, fu_g, fu_b, fu_m, fu_v, lfu_w, lfu_g, lfu_b, lfu_m, lfu_v, w2):
        import jax, jax.numpy as jnp
        import numpy as np
        BN_EPS = 0.001

        def conv1x1(x, w):
            return jnp.einsum('nchw,oc->nohw', x, w)

        def bn(x, gamma, beta, mean, var):
            scale = gamma / jnp.sqrt(var + BN_EPS)
            shift = beta - mean * scale
            return x * scale[None, :, None, None] + shift[None, :, None, None]

        def fourier_unit(x, w, gamma, beta, mean, var):
            N, C, H, W = x.shape
            norm = jnp.sqrt(jnp.float32(W))
            f = jnp.fft.rfft(x / norm, axis=-1)
            Wf = f.shape[-1]
            ff = jnp.stack([jnp.real(f), jnp.imag(f)], axis=2).reshape(N, 2 * C, H, Wf)
            y = jax.nn.relu(bn(conv1x1(ff, w), gamma, beta, mean, var))
            Co = y.shape[1] // 2
            y = y.reshape(N, Co, 2, H, Wf)
            c = jax.lax.complex(y[:, :, 0], y[:, :, 1])
            return jnp.fft.irfft(c, n=W, axis=-1) * norm
        x = jnp.transpose(x, (0, 3, 1, 2))
        x = jax.nn.relu(bn(conv1x1(x, w1), g1, b1, m1, v1))
        out = fourier_unit(x, fu_w, fu_g, fu_b, fu_m, fu_v)
        C = x.shape[1]
        xs = x[:, :C // 4]
        xs = jnp.concatenate(jnp.split(xs, 2, axis=2), axis=1)
        xs = jnp.concatenate(jnp.split(xs, 2, axis=3), axis=1)
        xs = fourier_unit(xs, lfu_w, lfu_g, lfu_b, lfu_m, lfu_v)
        xs = jnp.tile(xs, (1, 1, 2, 2))
        out = conv1x1(x + out + xs, w2)
        return jnp.transpose(out, (0, 2, 3, 1))

    def _L2_conv_ref(x, W_in, conv_w, conv_b, W_x, W_dt, b_dt, A_log, Dp, W_out, rms_w1, rms_wf, ln_w, ln_b):
        import jax, jax.numpy as jnp
        import numpy as np
        EPS = 1e-05
        D_CONV = 4

        def rmsnorm(x, w):
            return x * jax.lax.rsqrt(jnp.mean(x * x, axis=-1, keepdims=True) + EPS) * w

        def layernorm(x, w, b):
            m = jnp.mean(x, axis=-1, keepdims=True)
            v = jnp.mean((x - m) ** 2, axis=-1, keepdims=True)
            return (x - m) * jax.lax.rsqrt(v + EPS) * w + b

        def mamba_mixer(x, W_in, conv_w, conv_b, W_x, W_dt, b_dt, A_log, Dp, W_out):
            B, L, C = x.shape
            I = W_out.shape[1]
            N = A_log.shape[1]
            R = W_dt.shape[1]
            proj = x @ W_in.T
            hs, gate = jnp.split(proj, 2, axis=-1)
            hs_c = jax.lax.conv_general_dilated(hs.transpose(0, 2, 1), conv_w, (1,), [(D_CONV - 1, 0)], dimension_numbers=('NCH', 'OIH', 'NCH'), feature_group_count=I)
            hs = jax.nn.silu(hs_c.transpose(0, 2, 1) + conv_b)
            ssm_in = hs @ W_x.T
            dt_r, Bm, Cm = jnp.split(ssm_in, [R, R + N], axis=-1)
            dt = jax.nn.softplus(dt_r @ W_dt.T + b_dt)
            A = -jnp.exp(A_log)

            def step(state, inp):
                dt_t, B_t, C_t, u_t = inp
                dA = jnp.exp(dt_t[:, :, None] * A)
                state = dA * state + dt_t[:, :, None] * B_t[:, None, :] * u_t[:, :, None]
                y = jnp.einsum('bin,bn->bi', state, C_t)
                return (state, y)
            xs = (dt.transpose(1, 0, 2), Bm.transpose(1, 0, 2), Cm.transpose(1, 0, 2), hs.transpose(1, 0, 2))
            state0 = jnp.zeros((B, I, N), x.dtype)
            _, ys = jax.lax.scan(step, state0, xs)
            y = ys.transpose(1, 0, 2) + hs * Dp
            y = y * jax.nn.silu(gate)
            return y @ W_out.T

        def forward_scan(x, W_in, conv_w, conv_b, W_x, W_dt, b_dt, A_log, Dp, W_out, rms_w1, rms_wf):
            h = x + mamba_mixer(rmsnorm(x, rms_w1), W_in, conv_w, conv_b, W_x, W_dt, b_dt, A_log, Dp, W_out)
            return rmsnorm(h, rms_wf)
        BT, H, W, C = x.shape
        xs = jnp.stack([x, x[:, :, ::-1], x[:, ::-1], x[:, ::-1, ::-1]], axis=0)
        xs = xs.reshape(4 * BT, H * W, C)
        out = forward_scan(xs, W_in, conv_w, conv_b, W_x, W_dt, b_dt, A_log, Dp, W_out, rms_w1, rms_wf)
        out = out.reshape(4, BT, H, W, C)
        o = (out[0] + out[1][:, :, ::-1] + out[2][:, ::-1] + out[3][:, ::-1, ::-1]) / 4.0
        return layernorm(o, ln_w, ln_b)

    def _L3_conv_ref(x, gamma, beta):
        import jax, jax.numpy as jnp
        import numpy as np
        EPS = 1e-05
        M_PER_GROUP = 16
        N, H, W, C = x.shape
        m = M_PER_GROUP
        G = C // m
        xf = x.reshape(-1, G, m)
        n_rows = xf.shape[0]
        mean = jnp.mean(xf, axis=0, keepdims=True)
        centered = xf - mean
        sigma = jnp.einsum('ngi,ngj->gij', centered, centered) / n_rows
        lam, U = jnp.linalg.eigh(sigma)
        inv_sqrt = 1.0 / jnp.sqrt(lam + EPS)
        proj = jnp.einsum('gik,gk,gjk->gij', U, inv_sqrt, U)
        out = jnp.einsum('ngi,gij->ngj', centered, proj)
        out = out.reshape(N, H, W, C)
        return out * gamma + beta

    def _gn(v, G=32, eps=1e-5):
        B_, H_, W_, C_ = v.shape
        g = v.reshape(B_, H_, W_, G, C_ // G)
        m = jnp.mean(g, axis=(1, 2, 4), keepdims=True)
        s = jnp.var(g, axis=(1, 2, 4), keepdims=True)
        return ((g - m) / jnp.sqrt(s + eps)).reshape(v.shape)

    def _ln_c(v, eps=1e-6):
        m = jnp.mean(v, axis=-1, keepdims=True)
        s = jnp.var(v, axis=-1, keepdims=True)
        return (v - m) / jnp.sqrt(s + eps)

    def _ln_t(v, eps=1e-5):
        m = jnp.mean(v, axis=-1, keepdims=True)
        s = jnp.var(v, axis=-1, keepdims=True)
        return (v - m) / jnp.sqrt(s + eps)

    def _to_tokens(v):
        B_, H_, W_, C_ = v.shape
        return v.reshape(B_, H_ * W_, C_)
    def _from_tokens(t, like):
        return t.reshape(like.shape)

    x = _L0_conv_ref(x, L0_conv_Wq, L0_conv_bq, L0_conv_Wk, L0_conv_bk, L0_conv_Wv, L0_conv_bv, L0_conv_gamma)
    x = _L1_conv_ref(x, L1_conv_w1, L1_conv_g1, L1_conv_b1, L1_conv_m1, L1_conv_v1, L1_conv_fu_w, L1_conv_fu_g, L1_conv_fu_b, L1_conv_fu_m, L1_conv_fu_v, L1_conv_lfu_w, L1_conv_lfu_g, L1_conv_lfu_b, L1_conv_lfu_m, L1_conv_lfu_v, L1_conv_w2)
    x = _L2_conv_ref(x, L2_conv_W_in, L2_conv_conv_w, L2_conv_conv_b, L2_conv_W_x, L2_conv_W_dt, L2_conv_b_dt, L2_conv_A_log, L2_conv_Dp, L2_conv_W_out, L2_conv_rms_w1, L2_conv_rms_wf, L2_conv_ln_w, L2_conv_ln_b)
    x = _L3_conv_ref(x, L3_conv_gamma, L3_conv_beta)
    return x


_drawn_inputs = setup_inputs


def setup_inputs(seed=0):
    import zlib

    import numpy as np

    out = dict(_drawn_inputs(seed))
    spreads = {'L2_conv_Dp': (1.0, 0.6),
     'L2_conv_rms_w1': (1.0, 0.6),
     'L2_conv_rms_wf': (1.0, 0.2),
     'L2_conv_ln_w': (1.0, 0.563),
     'L2_conv_ln_b': (0.0, 0.8),
     'L3_conv_gamma': (1.0, 0.2),
     'L3_conv_beta': (0.0, 0.1)}
    factors = {'L0_conv_bq': 6.403,
     'L0_conv_bk': 8.0,
     'L0_conv_bv': 8.0,
     'L2_conv_W_in': 8.0,
     'L2_conv_conv_w': 8.0,
     'L2_conv_conv_b': 8.0,
     'L2_conv_W_x': 8.0,
     'L2_conv_W_dt': 8.0,
     'L2_conv_b_dt': 8.0,
     'L2_conv_A_log': 8.0,
     'L2_conv_W_out': 8.0}
    for name, (base, spread) in spreads.items():
        noise = np.random.default_rng([zlib.crc32(name.encode()), seed]).standard_normal(out[name].shape)
        drawn = base * np.exp(spread * noise) if base else spread * noise
        out[name] = jnp.asarray(drawn.astype(out[name].dtype))
    for name, factor in factors.items():
        out[name] = (out[name] * factor).astype(out[name].dtype)
    return out
```

```python
from contextlib import ExitStack

import concourse.bass as bass
from concourse import mybir

F32 = mybir.dt.float32
BF16 = mybir.dt.bfloat16
ALU = mybir.AluOpType
ACT = mybir.ActivationFunctionType
AX = mybir.AxisListType

P = 128
B, H, W, C = 2, 64, 64, 256
N = H * W
KC = C // P
TILES = N // P
CQ = C // 8
ROW2 = 64

I = 2 * C
IB = I // P
NS = 16
RK = 16
TAPS = 4
T = 512
CHUNKS = N // T
SEQS = 4 * B

M = 16


class Pool_:

    def __init__(self, nc, ctx, tag):
        self.nc, self.ctx, self.tag = nc, ctx, tag

    def sb(self, name, shape, dt=F32):
        return self.ctx.enter_context(self.nc.sbuf_tensor(f"{self.tag}_{name}", shape, dt))

    def ps(self, name, shape, dt=F32):
        return self.ctx.enter_context(self.nc.psum_tensor(f"{self.tag}_p_{name}", shape, dt))

    def sem(self, name):
        return self.ctx.enter_context(self.nc.semaphore(f"{self.tag}_s_{name}"))


def attention(nc, xT, x, wqT, wkT, bq, bk, wvT, bv, gamma, ident, x0):
    QR = ROW2 + CQ + 1
    IT = 512
    JP = TILES // 2
    with ExitStack() as ctx:
        m = Pool_(nc, ctx, "at")
        xT_sb = m.sb("xT", [P, KC, N])
        wq_sb, wk_sb = m.sb("wq", [P, KC, QR]), m.sb("wk", [P, KC, QR])
        wv_sb = m.sb("wv", [P, KC, C])
        bq_sb, bk_sb = m.sb("bq", [QR, 1]), m.sb("bk", [QR, 1])
        bv_sb, ones_row = m.sb("bv", [1, C]), m.sb("ones", [1, P])
        gamma_sb, ident_sb = m.sb("gamma", [P, 1]), m.sb("ident", [P, P])
        q_sb, k_sb = m.sb("q", [QR, N]), m.sb("k", [QR, N])
        q_now = m.sb("qnow", [QR, 2, IT])
        v_sb = m.sb("v", [P, TILES, C + 1])
        part_max = m.sb("pmax", [P, TILES, 2])
        max_sb = m.sb("max", [P, TILES])
        negmax = m.sb("negmax", [P, TILES])
        probs = m.sb("probs", [P, 2, 2, IT])
        x_now = m.sb("xnow", [P, 2, 4, C])
        recip = m.sb("recip", [P, 4])
        rg = m.sb("rg", [P, 4])
        out_sb = m.sb("out", [P, 2, 4, C])
        ps = m.ps("all", [P, 8, 512])

        s_w, s_xT = m.sem("weights"), m.sem("xT_loaded")
        s_const = m.sem("consts_set")
        s_proj = m.sem("projected")
        s_proj_free = [m.sem("even_projection_copied"), m.sem("odd_projection_copied")]
        s_mx, s_mx_free = m.sem("scores_for_max"), m.sem("max_taken")
        s_neg, s_negT, s_negrow = m.sem("negmax"), m.sem("negmax_row"), m.sem("negmax_row_in_q")
        s_pm = m.sem("partial_max_done")
        s_qn, s_qn_free = m.sem("q_now"), m.sem("q_now_free")
        s_sc, s_pr, s_pv = m.sem("scores"), m.sem("probs"), m.sem("pair_summed")
        s_x = [m.sem("x_now0"), m.sem("x_now1")]
        s_rc, s_rg, s_o = m.sem("recip"), m.sem("recip_gamma"), m.sem("out_ready")
        s_st = [m.sem("stored0"), m.sem("stored1")]
        s_acc_free = m.sem("acc_free")
        block = ctx.enter_context(nc.Block())
        PROJ = 2 * (N // 512) + TILES // 2
        MAXS = 2 * TILES

        xv = x.rearrange("b (t g p) c -> b t p g c", p=P, g=4)
        ov = x0.rearrange("b (t g p) c -> b t p g c", p=P, g=4)

        @block.sync
        def _(sp):
            for dst, src in ((wq_sb, wqT), (wk_sb, wkT), (wv_sb, wvT)):
                sp.dma_start(dst[:, :, :], src.rearrange("(k p) o -> p k o", p=P)).then_inc(s_w, 16)
            for dst, src in ((bq_sb, bq), (bk_sb, bk), (bv_sb, bv), (gamma_sb, gamma), (ident_sb, ident)):
                sp.dma_start(dst[:, :], src).then_inc(s_w, 16)
            sp.sem_inc(s_st[0], 16)
            sp.sem_inc(s_st[1], 16)
            for b in range(B):
                if b:
                    sp.wait_ge(s_proj, PROJ * b)
                sp.dma_start(xT_sb[:, :, :], xT[b].rearrange("(k p) n -> p k n", p=P)).then_inc(s_xT, 16)
                for t in range(N // IT):
                    n = b * (N // IT) + t
                    if n >= 2:
                        sp.wait_ge(s_o, 4 * (n - 1))
                    sp.dma_start(x_now[:, n % 2, :, :], xv[b, t]).then_inc(s_x[n % 2], 16)
                    if n >= 1:
                        sp.wait_ge(s_o, 4 * n)
                        sp.dma_start(ov[(n - 1) // 8, (n - 1) % 8], out_sb[:, (n - 1) % 2, :, :]).then_inc(s_st[(n - 1) % 2], 16)
            n = B * (N // IT)
            sp.wait_ge(s_o, 4 * n)
            sp.dma_start(ov[B - 1, 7], out_sb[:, (n - 1) % 2, :, :]).then_inc(s_st[(n - 1) % 2], 16)
            for par in range(2):
                sp.wait_ge(s_st[par], 8 * n + 16)

        @block.tensor
        def _(pe):
            pe.sem_inc(s_sc, 2 * JP)
            pe.wait_ge(s_w, 16 * 8)
            pe.wait_ge(s_const, 2)
            with pe.Fori(0, B) as b:
                pe.wait_ge(s_xT, b * 16 + 16)
                pe.wait_ge(s_acc_free, b * 8 + 1)
                step = 0

                def bank_free(step):
                    if step >= 8:
                        pe.wait_ge(s_proj_free[step % 2], b * (PROJ // 2) + (step - 8) // 2 + 1)

                for w in (wq_sb, wk_sb):
                    for t in range(N // 512):
                        bank_free(step)
                        for kc in range(KC):
                            mm = nc.tensor.matmul(ps[0:QR, step % 8, :], w[:, kc, :], xT_sb[:, kc, t * 512:(t + 1) * 512],
                                                  start=(kc == 0), stop=(kc == KC - 1))
                        mm.then_inc(s_proj, 1)
                        step += 1
                for t in range(TILES // 2):
                    bank_free(step)
                    for g in range(2):
                        o = ps[:, step % 8, g * C:(g + 1) * C]
                        tok = (2 * t + g) * P
                        for kc in range(KC):
                            nc.tensor.matmul(o, xT_sb[:, kc, tok:tok + P], wv_sb[:, kc, :], start=(kc == 0), stop=False)
                        mm = nc.tensor.matmul(o, ones_row[:, :], bv_sb[:, :], start=False, stop=True)
                    mm.then_inc(s_proj, 1)
                    step += 1
                for par in range(2):
                    pe.wait_ge(s_proj_free[par], b * (PROJ // 2) + PROJ // 2)
                for it in range(TILES):
                    for half in range(2):
                        n = 2 * it + half
                        if n >= 2:
                            pe.wait_ge(s_mx_free, b * MAXS + (n - 1))
                        for j in range(4):
                            r = ROW2 * (j % 2)
                            jj = (4 * half + j) * 512
                            mm = nc.tensor.matmul(ps[:, 4 * half + j, :], q_sb[r:r + CQ + 1, it * P:(it + 1) * P],
                                                  k_sb[r:r + CQ + 1, jj:jj + 512], start=True, stop=True)
                        mm.then_inc(s_mx, 1)
                pe.wait_ge(s_neg, b + 1)
                pe.wait_ge(s_mx_free, b * MAXS + MAXS)
                for it in range(TILES):
                    for r in (CQ, ROW2 + CQ):
                        mm = nc.tensor.matmul(ps[r:r + 1, it // 4, (it % 4) * P:(it % 4 + 1) * P],
                                              negmax[:, it:it + 1], ident_sb[:, :], start=True, stop=True)
                mm.then_inc(s_negT, 1)
                with pe.Fori(0, N // IT // 2) as th:
                    pe.wait_ge(s_negrow, b * 2 + 2)
                    for par in range(2):
                        q = b * (N // IT) + th * 2 + par

                        def scores(j):
                            pe.wait_ge(s_pr, q * JP + (j + 1))
                            for r in range(2):
                                jb, lo = 2 * j + r, ROW2 * r
                                mm = nc.tensor.matmul(ps[:, 2 * (j % 2) + r, :], k_sb[lo:lo + CQ + 1, jb * P:(jb + 1) * P],
                                                      q_now[lo:lo + CQ + 1, par, :], start=True, stop=True)
                            mm.then_inc(s_sc, 1)

                        pe.wait_ge(s_qn, q + 1)
                        scores(0)
                        for j in range(JP):
                            if j + 1 < JP:
                                scores(j + 1)
                            if j == 0:
                                pe.wait_ge(s_acc_free, q + 1)
                            pe.wait_ge(s_pr, q * JP + (j + 3))
                            for r in range(2):
                                jb = 2 * j + r
                                for g in range(4):
                                    mm = nc.tensor.matmul(ps[:, 4 + g, 0:C + 1], probs[:, j % 2, r, g * P:(g + 1) * P],
                                                          v_sb[:, jb, :], start=(jb == 0), stop=(jb == TILES - 1))
                            mm.then_inc(s_pv, 1)

        @block.vector
        def _(dve):
            dve.sem_inc(s_acc_free, 1)
            nc.vector.memset(ones_row[:, :], 1.0).then_inc(s_const, 1)
            nc.vector.memset(v_sb[:, :, C:C + 1], 1.0).then_inc(s_const, 1)
            dve.wait_ge(s_w, 16 * 8)
            with dve.Fori(0, B) as b:
                dve.wait_ge(s_pv, b * (8 * JP) + 2)
                for t in range(1, PROJ, 2):
                    dve.wait_ge(s_proj, b * PROJ + (t + 1))
                    if t < 16:
                        dst, bias = (q_sb, bq_sb) if t < 8 else (k_sb, bk_sb)
                        nc.vector.tensor_scalar(dst[:, (t % 8) * 512:(t % 8 + 1) * 512], ps[0:QR, t % 8, :], bias[:, 0:1],
                                                None, ALU.add).then_inc(s_proj_free[1], 1)
                    else:
                        tt = 2 * (t - 16)
                        nc.vector.tensor_copy(v_sb[:, tt:tt + 2, 0:C], ps[:, t % 8, :].rearrange("p (g c) -> p g c", g=2)
                                              ).then_inc(s_proj_free[1], 1)
                for n in range(MAXS):
                    dve.wait_ge(s_mx, b * MAXS + (n + 1))
                    half = n % 2
                    nc.vector.tensor_reduce(part_max[:, n // 2, half:half + 1], ps[:, 4 * half:4 * half + 4, :],
                                            AX.XY, ALU.max).then_inc(s_mx_free, 1)
                dve.wait_ge(s_mx_free, b * MAXS + MAXS)
                nc.vector.tensor_tensor(max_sb[:, :], part_max[:, :, 0], part_max[:, :, 1], ALU.max).then_inc(s_pm, 1)
                dve.wait_ge(s_pm, b + 1)
                nc.vector.tensor_scalar(negmax[:, :], max_sb[:, :], -1.0, None, ALU.mult).then_inc(s_neg, 1)
                dve.wait_ge(s_negT, b + 1)
                r = CQ
                nc.vector.tensor_copy(q_sb[r:r + 1, :].rearrange("p (a n) -> p a n", a=8), ps[r:r + 1, :, :]).then_inc(s_negrow, 1)
                with dve.Fori(0, N // IT // 2) as th:
                    for par in range(2):
                        q = b * (N // IT) + th * 2 + par
                        dve.wait_ge(s_pv, q * JP + (JP + 2))
                        dve.wait_ge(s_x[par], b * 64 + th * 16 + 16)
                        dve.wait_ge(s_st[par], b * 64 + th * 16 + 16)
                        nc.vector.reciprocal(recip[:, :], ps[:, 4:8, C]).then_inc(s_rc, 1)
                        dve.wait_ge(s_rc, q + 1)
                        nc.vector.tensor_scalar(rg[:, :], recip[:, :], gamma_sb[:, 0:1], None, ALU.mult).then_inc(s_rg, 1)
                        dve.wait_ge(s_rg, q + 1)
                        for g in range(4):
                            nc.vector.scalar_tensor_tensor(out_sb[:, par, g, :], ps[:, 4 + g, 0:C], rg[:, g:g + 1],
                                                           x_now[:, par, g, :], ALU.mult, ALU.add).then_inc(s_o, 1)
                        dve.wait_ge(s_o, q * 4 + 4)
                        dve.sem_inc(s_acc_free, 1)

        @block.scalar
        def _(act):
            act.wait_ge(s_w, 16 * 8)
            act.sem_inc(s_pr, 2)
            with act.Fori(0, B) as b:
                act.wait_ge(s_pv, b * (8 * JP) + 2)
                for t in range(0, PROJ, 2):
                    act.wait_ge(s_proj, b * PROJ + (t + 1))
                    if t < 16:
                        dst, bias = (q_sb, bq_sb) if t < 8 else (k_sb, bk_sb)
                        nc.scalar.activation(dst[:, (t % 8) * 512:(t % 8 + 1) * 512], ps[0:QR, t % 8, :], ACT.Identity,
                                             bias=bias[:, 0:1]).then_inc(s_proj_free[0], 1)
                    else:
                        tt = 2 * (t - 16)
                        nc.scalar.copy(v_sb[:, tt:tt + 2, 0:C], ps[:, t % 8, :].rearrange("p (g c) -> p g c", g=2)
                                       ).then_inc(s_proj_free[0], 1)
                act.wait_ge(s_negT, b + 1)
                r = ROW2 + CQ
                nc.scalar.copy(q_sb[r:r + 1, :].rearrange("p (a n) -> p a n", a=8), ps[r:r + 1, :, :]).then_inc(s_negrow, 1)
                with act.Fori(0, N // IT) as t:
                    for j in range(JP):
                        n = b * (8 * JP) + t * JP + j
                        act.wait_ge(s_sc, n + (1 + 2 * JP))
                        act.wait_ge(s_pv, n + 1)
                        nc.scalar.activation(probs[:, j % 2, :, :], ps[:, 2 * (j % 2):2 * (j % 2) + 2, :], ACT.Exp
                                             ).then_inc(s_pr, 1)

        @block.gpsimd
        def _(pool):
            pool.sem_inc(s_pv, 2)
            with pool.Fori(0, B) as b:
                with pool.Fori(0, N // IT // 2) as th:
                    pool.wait_ge(s_negrow, b * 2 + 2)
                    for par in range(2):
                        q = b * (N // IT) + th * 2 + par
                        pool.wait_ge(s_sc, q * JP + JP)
                        nc.gpsimd.tensor_copy(q_now[:, par, :], q_sb[:, bass.ds(th * (2 * IT) + par * IT, IT)]
                                              ).then_inc(s_qn, 1)


FR, FL = W // 2 + 1, W // 4 + 1
Z1, Z2 = 2 * FR, 2 * FL
HC = C // 2


def fourier_conv(nc, x0, w1T, bn1, fuT, bnf, lfuT, bnl, w2T, dft, dftl, idft, idftl, ident, rms1, x1, xn):
    HT = TILES // 2
    with ExitStack() as ctx:
        m = Pool_(nc, ctx, "fc")
        w1_sb, w2_sb = m.sb("w1", [P, KC, HC]), m.sb("w2", [HC, C])
        fu_sb, lfu_sb = m.sb("fu", [HC, 2, C]), m.sb("lfu", [HC, 2, C])
        NB = HC + 2 * C
        bn_sb = m.sb("bn", [P, 4, NB])
        scale, shift = m.sb("scale", [P, NB]), m.sb("shift", [P, NB])
        bn1_col, shift_col = m.sb("bncol", [HC, 4]), m.sb("shiftcol", [HC, 4])
        dft_sb, dftl_sb = m.sb("dft", [P, 2 * Z1]), m.sb("dftl", [P, 2, 2 * Z2])
        idft_sb, idftl_sb = m.sb("idft", [Z1, 2, P]), m.sb("idftl", [Z2, 2, P])
        ident_sb, ones_row, rms_sb = m.sb("ident", [P, P]), m.sb("ones", [1, P]), m.sb("rms", [P, KC])
        xin = m.sb("xin", [P, 2, 2, C])
        xt_sb = m.sb("xt", [P, KC, 2, P])
        y_sb, yt_sb = m.sb("y", [P, 2, HC]), m.sb("yt", [HC, 2, P])
        f_sb, fl_sb = m.sb("f", [HC, 2, 2 * Z1]), m.sb("fl", [P, 2 * Z2])
        z_sb, zl_sb = m.sb("z", [Z1, 2, C]), m.sb("zl", [Z2, C])
        s_sb = m.sb("s", [HC, 2, P])
        x1_sb = m.sb("x1", [P, 2, 2, C])
        sq = m.sb("sq", [P, 2, C])
        ss, ms, rt, rstd = (m.sb(k, [P, 2]) for k in ("ss", "ms", "rt", "rstd"))
        xs_sb = m.sb("xs", [P, 2, C])
        xn_sb = m.sb("xn", [P, 2, 4, KC, 2, P])
        pT, pY, pYT, pF, pZ, pZL, pO, pX = (m.ps(k, [P, 512]) for k in ("T", "Y", "YT", "F", "Z", "ZL", "O", "X"))

        s_w, s_fold, s_fsc = m.sem("weights"), m.sem("bn_step"), m.sem("bn_sqrt")
        s_ready, s_passed = m.sem("weights_scaled"), m.sem("pool_passed")
        s_xnfree = m.sem("xn_free")
        s_in, s_x1st, s_xnst = ([m.sem(f"{k}{i}") for i in range(2)] for k in ("xin", "x1_stored", "xn_stored"))
        names = ["xt_ps", "xt", "y_ps", "y", "yt_ps", "yt", "f_ps", "f", "fl", "z_ps", "z", "zl_ps", "zl", "o_ps", "s",
                 "x1_ps", "x1", "ss", "ms", "rt", "rstd", "xs", "xnt_ps", "xn0", "xn1", "xn23"]
        S = {k: m.sem(k) for k in names}
        block = ctx.enter_context(nc.Block())
        NW = 14

        x0v = x0.rearrange("b (k t p) c -> p b t k c", p=P, k=2)
        x1v = x1.rearrange("b (k t p) c -> p b t k c", p=P, k=2)
        def tiles_of(v, b, a, e):
            return v[:, bass.ds(b, 1), bass.ds(a * 4 + e, 1), :, :].rearrange("p a o k c -> p (a o k) c")

        def order_of(o, b, a, e, t):
            chunk = a + t * (CHUNKS // 2) if o < 2 else a * -1 + (CHUNKS // 2 - 1 + t * (CHUNKS // 2))
            at = e * P if o < 2 else (3 - e) * P
            return xn[bass.ds(b + o * B, 1), bass.ds(chunk, 1), :, :, at:at + P].rearrange("s h p k n -> p (s h k) n")

        @block.sync
        def _(sp):
            sp.dma_start(w1_sb[:, :, :], w1T.rearrange("(k p) o -> p k o", p=P)).then_inc(s_w, 16)
            for dst, src in ((w2_sb, w2T), (fu_sb, fuT), (lfu_sb, lfuT), (bn1_col, bn1[0]), (dft_sb, dft),
                             (dftl_sb, dftl), (idft_sb, idft), (idftl_sb, idftl), (ident_sb, ident), (rms_sb, rms1)):
                sl = tuple(slice(None) for _ in src.shape)
                sp.dma_start(dst[sl], src).then_inc(s_w, 16)
            at = 0
            for src in (bn1[1], bnf, bnl):
                n = src.shape[1]
                sp.dma_start(bn_sb[:, :, at:at + n], src[None, :, :].broadcast_to([P, 4, n])).then_inc(s_w, 16)
                at += n
            for i in range(2):
                sp.sem_inc(s_x1st[i], 16)
                sp.sem_inc(s_xnfree, 1)
            sp.sem_inc(S["xt"], 2)
            with sp.Fori(0, B) as b:
                with sp.Fori(0, HT // 4) as a:
                    for e in range(4):
                        par = e % 2
                        u = b * HT + a * 4 + e
                        v = b * (HT // 2) + a * 2 + e // 2
                        sp.wait_ge(S["xt"], u + 1)
                        sp.dma_start(xin[:, par, :, :], tiles_of(x0v, b, a, e)).then_inc(s_in[par], 16)
            for i in range(2):
                sp.wait_ge(s_x1st[i], 16 + 16 * B * HT // 2)
                sp.wait_ge(s_xnst[i], 128 * B * HT // 2)

        @block.gpsimd
        def _(pool):
            with pool.Fori(0, B) as b:
                with pool.Fori(0, HT // 4) as a:
                    for e in range(4):
                        par = e % 2
                        u = b * HT + a * 4 + e
                        v = b * (HT // 2) + a * 2 + e // 2
                        pool.wait_ge(S["xn0"], u * 2 + 4)
                        pool.wait_ge(S["xn1"], u + 1)
                        pool.sem_inc(s_passed, 1)
                        for o in range(2):
                            nc.gpsimd.tensor_copy(xn_sb[:, par, 2 + o, :, :, :],
                                                  xn_sb[:, par, 1 - o, :, ::-1, ::-1]).then_inc(S["xn23"], 1)
                        for o in range(2):
                            for t in range(2):
                                pool.dma_start(order_of(o, b, a, e, t), xn_sb[:, par, o, :, t, :]).then_inc(s_xnst[par], 16)
                        pool.wait_ge(S["xn23"], u * 2 + 2)
                        for o in range(2, 4):
                            for t in range(2):
                                pool.dma_start(order_of(o, b, a, e, t), xn_sb[:, par, o, :, t, :]).then_inc(s_xnst[par], 16)
                        pool.wait_ge(s_xnst[par], v * 128 + 128)
                        pool.sem_inc(s_xnfree, 1)

        @block.scalar
        def _(act):
            act.wait_ge(s_fold, 2)
            nc.scalar.activation(scale[:, :], bn_sb[:, 3, :], ACT.Sqrt).then_inc(s_fsc, 1)
            nc.scalar.activation(shift_col[:, 0:1], bn1_col[:, 3:4], ACT.Sqrt).then_inc(s_fsc, 1)

            with act.Fori(0, B) as b:
                with act.Fori(0, HT // 4) as a:
                    for e in range(4):
                        par = e % 2
                        u = b * HT + a * 4 + e
                        v = b * (HT // 2) + a * 2 + e // 2
                        act.wait_ge(S["xt_ps"], u + 1)
                        nc.scalar.copy(xt_sb[:, :, :, :], pT[:, :].rearrange("p (k t n) -> p k t n", k=KC, t=2)
                                       ).then_inc(S["xt"], 1)
                        act.wait_ge(S["yt_ps"], u + 1)
                        act.wait_ge(S["y_ps"], u + 1)
                        nc.scalar.activation(yt_sb[:, :, :], pYT[:, 0:256].rearrange("p (t n) -> p t n", t=2), ACT.Relu,
                                             bias=shift_col[:, 3:4]).then_inc(S["yt"], 1)
                        act.wait_ge(S["f_ps"], u + 1)
                        nc.scalar.copy(f_sb[:, :, :], pF[:, 0:4 * Z1].rearrange("p (t n) -> p t n", t=2)).then_inc(S["f"], 1)
                        act.wait_ge(S["z_ps"], u + 1)
                        nc.scalar.activation(z_sb[:, :, :], pZ[0:Z1, :].rearrange("p (t n) -> p t n", t=2), ACT.Relu
                                             ).then_inc(S["z"], 1)
                        act.wait_ge(S["x1_ps"], u + 1)
                        act.wait_ge(s_x1st[par], v * 16 + 16)
                        nc.scalar.copy(x1_sb[:, par, :, :], pX[:, :].rearrange("p (t n) -> p t n", t=2)).then_inc(S["x1"], 1)
                        for t in range(2):
                            nc.scalar.activation(sq[:, t, :], pX[:, t * C:(t + 1) * C], ACT.Square,
                                                 accum_out=ss[:, t:t + 1]).then_inc(S["ss"], 1)
                        act.wait_ge(S["ms"], u + 1)
                        nc.scalar.activation(rt[:, :], ms[:, :], ACT.Sqrt).then_inc(S["rt"], 1)
                        act.wait_ge(S["xnt_ps"], u + 1)
                        act.wait_ge(s_xnfree, u + 1)
                        pv = pT[:, :].rearrange("p (k t n) -> p k t n", k=KC, t=2)
                        for kc in range(KC):
                            nc.scalar.activation(xn_sb[:, par, 0, kc, :, :], pv[:, kc, :, :], ACT.Copy,
                                                 scale=rms_sb[:, kc:kc + 1]).then_inc(S["xn0"], 1)
                        act.wait_ge(S["x1"], u + 1)
                        act.dma_start(tiles_of(x1v, b, a, e), x1_sb[:, par, :, :]).then_inc(s_x1st[par], 16)

        @block.vector
        def _(dve):
            done = [0]

            def step(ins):
                done[0] += 1
                ins.then_inc(s_fold, 1)
                dve.wait_ge(s_fold, done[0])

            nc.vector.memset(ones_row[:, :], 1.0).then_inc(s_ready, 1)
            dve.wait_ge(s_w, 16 * NW)
            nc.vector.tensor_scalar(bn1_col[:, 3:4], bn1_col[:, 3:4], 1e-3, None, ALU.add).then_inc(s_fold, 1)
            done[0] += 1
            step(nc.vector.tensor_scalar(bn_sb[:, 3, :], bn_sb[:, 3, :], 1e-3, None, ALU.add))
            dve.wait_ge(s_fsc, 2)
            step(nc.vector.reciprocal(scale[:, :], scale[:, :]))
            step(nc.vector.tensor_tensor(scale[:, :], scale[:, :], bn_sb[:, 0, :], ALU.mult))
            step(nc.vector.tensor_tensor(shift[:, :], scale[:, :], bn_sb[:, 2, :], ALU.mult))
            step(nc.vector.tensor_tensor(shift[:, :], bn_sb[:, 1, :], shift[:, :], ALU.subtract))
            step(nc.vector.reciprocal(shift_col[:, 1:2], shift_col[:, 0:1]))
            step(nc.vector.tensor_tensor(shift_col[:, 2:3], shift_col[:, 1:2], bn1_col[:, 0:1], ALU.mult))
            step(nc.vector.tensor_tensor(shift_col[:, 0:1], shift_col[:, 2:3], bn1_col[:, 2:3], ALU.mult))
            step(nc.vector.tensor_tensor(shift_col[:, 3:4], bn1_col[:, 1:2], shift_col[:, 0:1], ALU.subtract))
            for w, at, n in ((w1_sb, 0, HC), (fu_sb, HC, C), (lfu_sb, HC + C, C)):
                for k in range(2):
                    nc.vector.tensor_tensor(w[:, k, :], w[:, k, :], scale[:, at:at + n], ALU.mult).then_inc(s_ready, 1)
            with dve.Fori(0, B) as b:
                with dve.Fori(0, HT // 4) as a:
                    for e in range(4):
                        par = e % 2
                        u = b * HT + a * 4 + e
                        v = b * (HT // 2) + a * 2 + e // 2
                        dve.wait_ge(S["y_ps"], u + 1)
                        nc.vector.tensor_scalar(y_sb[:, :, :], pY[:, 0:256].rearrange("p (t n) -> p t n", t=2), 0.0, None,
                                                ALU.max).then_inc(S["y"], 1)
                        dve.wait_ge(S["f_ps"], u + 1)
                        nc.vector.tensor_copy(fl_sb[:, :], pZL[:, C:C + 2 * Z2]).then_inc(S["fl"], 1)
                        dve.wait_ge(S["zl_ps"], u + 1)
                        nc.vector.tensor_scalar(zl_sb[:, :], pZL[0:Z2, 0:C], 0.0, None, ALU.max).then_inc(S["zl"], 1)
                        dve.wait_ge(S["o_ps"], u + 1)
                        dve.wait_ge(S["yt"], u + 1)
                        nc.vector.tensor_tensor(s_sb[:, :, :], yt_sb[:, :, :], pO[:, 0:256].rearrange("p (t n) -> p t n", t=2),
                                                ALU.add).then_inc(S["s"], 1)
                        dve.wait_ge(S["ss"], u * 2 + 2)
                        nc.vector.tensor_scalar(ms[:, :], ss[:, :], 1.0 / C, 1e-5, ALU.mult, ALU.add).then_inc(S["ms"], 1)
                        dve.wait_ge(S["rt"], u + 1)
                        nc.vector.reciprocal(rstd[:, :], rt[:, :]).then_inc(S["rstd"], 1)
                        dve.wait_ge(S["rstd"], u + 1)
                        dve.wait_ge(S["x1"], u + 1)
                        for t in range(2):
                            nc.vector.tensor_scalar(xs_sb[:, t, :], x1_sb[:, par, t, :], rstd[:, t:t + 1], None, ALU.mult
                                                    ).then_inc(S["xs"], 1)
                        dve.wait_ge(S["xn0"], u * 2 + 4)
                        nc.vector.tensor_copy(xn_sb[:, par, 1, :, :, :].rearrange("p k t (h n) -> p (k t h) n", n=W),
                                              xn_sb[:, par, 0, :, :, :].rearrange("p k t (h n) -> p (k t h) n", n=W)[:, :, ::-1]
                                              ).then_inc(S["xn1"], 1)

        @block.tensor
        def _(pe):
            pe.wait_ge(s_w, 16 * NW)
            pe.wait_ge(s_ready, 7)
            pe.sem_inc(S["xn0"], 2)
            with pe.Fori(0, B) as b:
                with pe.Fori(0, HT // 4) as a:
                    for e in range(4):
                        par = e % 2
                        u = b * HT + a * 4 + e
                        v = b * (HT // 2) + a * 2 + e // 2
                        pe.wait_ge(s_in[par], v * 16 + 16)
                        pe.wait_ge(S["xn0"], u * 2 + 2)
                        for kc in range(KC):
                            for t in range(2):
                                at = (2 * kc + t) * P
                                mm = nc.tensor.transpose(pT[:, at:at + P], xin[:, par, t, kc * P:(kc + 1) * P], ident_sb[:, :])
                        mm.then_inc(S["xt_ps"], 1)
                        pe.wait_ge(S["xt"], u + 3)
                        for t in range(2):
                            o = pY[:, t * HC:(t + 1) * HC]
                            for kc in range(KC):
                                nc.tensor.matmul(o, xt_sb[:, kc, t, :], w1_sb[:, kc, :], start=(kc == 0), stop=False)
                            mm = nc.tensor.matmul(o, ones_row[:, :], shift[0:1, 0:HC], start=False, stop=True)
                        mm.then_inc(S["y_ps"], 1)
                        for kc in range(KC):
                            mm = nc.tensor.matmul(pYT[:, 0:256].rearrange("p (t n) -> p t n", t=2), w1_sb[:, kc, :], xt_sb[:, kc, :, :],
                                                  start=(kc == 0), stop=(kc == KC - 1))
                        mm.then_inc(S["yt_ps"], 1)
                        pe.wait_ge(S["y"], u + 1)
                        for t in range(2):
                            nc.tensor.matmul(pF[:, t * 2 * Z1:(t + 1) * 2 * Z1], y_sb[:, t, :], dft_sb[:, :], start=True, stop=True)
                        for wq in range(2):
                            for hq in range(2):
                                r = 64 * wq + 32 * hq
                                mm = nc.tensor.matmul(pZL[r:r + HC // 4, C:C + 2 * Z2], y_sb[:, hq, 0:HC // 4],
                                                      dftl_sb[:, wq, :], start=True, stop=True)
                        mm.then_inc(S["f_ps"], 1)
                        pe.wait_ge(S["f"], u + 1)
                        for t in range(2):
                            o = pZ[0:Z1, t * C:(t + 1) * C]
                            for ri in range(2):
                                nc.tensor.matmul(o, f_sb[:, t, ri * Z1:(ri + 1) * Z1], fu_sb[:, ri, :], start=(ri == 0), stop=False)
                            mm = nc.tensor.matmul(o, ones_row[:, 0:Z1], shift[0:1, HC:HC + C], start=False, stop=True)
                        mm.then_inc(S["z_ps"], 1)
                        pe.wait_ge(S["fl"], u + 1)
                        for ri in range(2):
                            nc.tensor.matmul(pZL[0:Z2, 0:C], fl_sb[:, ri * Z2:(ri + 1) * Z2], lfu_sb[:, ri, :], start=(ri == 0), stop=False)
                        nc.tensor.matmul(pZL[0:Z2, 0:C], ones_row[:, 0:Z2], shift[0:1, HC + C:HC + 2 * C], start=False, stop=True
                                         ).then_inc(S["zl_ps"], 1)
                        pe.wait_ge(S["z"], u + 1)
                        pe.wait_ge(S["zl"], u + 1)
                        for t in range(2):
                            o = pO[:, t * P:(t + 1) * P]
                            for ri in range(2):
                                nc.tensor.matmul(o, z_sb[:, t, ri * HC:(ri + 1) * HC], idft_sb[:, ri, :], start=(ri == 0), stop=False)
                            for ri in range(2):
                                mm = nc.tensor.matmul(o, zl_sb[:, ri * HC:(ri + 1) * HC], idftl_sb[:, ri, :], start=False, stop=(ri == 1))
                        mm.then_inc(S["o_ps"], 1)
                        pe.wait_ge(S["s"], u + 1)
                        for t in range(2):
                            mm = nc.tensor.matmul(pX[:, t * C:(t + 1) * C], s_sb[:, t, :], w2_sb[:, :], start=True, stop=True)
                        mm.then_inc(S["x1_ps"], 1)
                        pe.wait_ge(S["xs"], u * 2 + 2)
                        for kc in range(KC):
                            for t in range(2):
                                at = (2 * kc + t) * P
                                mm = nc.tensor.transpose(pT[:, at:at + P], xs_sb[:, t, kc * P:(kc + 1) * P], ident_sb[:, :])
                        mm.then_inc(S["xnt_ps"], 1)


def mamba(nc, xn, w_inT, conv_w, conv_b, w_xT, split, w_dtT, b_dt, a_log, d_skip, w_outT, ident, pick, keep, out):
    NC = SEQS * CHUNKS
    STEPS = 2 * NS
    BCR = 96
    GA, GO = 17, 2
    G = GA + GO
    FA, FO = GA + 1, GO
    F = FA + FO
    OUT_AT = 3
    HS_AT, GATE_AT, CONV_AT = 5, 9, 13
    SILU_AT, XP_AT, DT_AT, SP_AT, DU_AT = 17, 18, 20, 24, 26

    def group(c, g):
        return c * G + (g - GO + GA) if isinstance(c, int) and c == 0 else c * G + (g + 2 * GA - G)

    def freed(c, g):
        g = g + (1 if g > GO + 12 else 0)
        return (g - FO + FA) if isinstance(c, int) and c == 0 else c * F + (g + 2 * FA - F)

    with ExitStack() as ctx:
        m = Pool_(nc, ctx, "mm")
        w_in = m.sb("w_in", [P, KC, 2 * I])
        taps, cw = m.sb("taps", [P, IB * TAPS, P]), m.sb("cw", [P, IB * TAPS])
        w_x, w_dt, w_out = m.sb("w_x", [P, IB, BCR + RK]), m.sb("w_dt", [P, I]), m.sb("w_out", [P, IB, C])
        cb_sb, bdt_sb, d_sb, ab_sb = m.sb("cb", [P, IB]), m.sb("bdt", [P, IB]), m.sb("d", [P, IB]), m.sb("ab", [P, 2])
        alog, a_sb = m.sb("alog", [P, IB * NS]), m.sb("a", [P, IB * NS])
        ident_sb, keep_sb = m.sb("ident", [P, P]), m.sb("keep", [P, NC + 1])
        keep_now = m.sb("keep_now", [P, 2])
        pick_sb = m.sb("pick", [BCR, 2 * NS, P], BF16)
        xn_sb = m.sb("xn", [P, 2, KC, T])
        hs = m.sb("hs", [P, 2, IB, TAPS - 1 + T])
        u, gate = m.sb("u", [P, 2, IB, T]), m.sb("gate", [P, 2, IB, T])
        hi, mid, parts = m.sb("hi", [BCR, T], BF16), m.sb("mid", [BCR, T], BF16), m.sb("parts", [BCR, 2, T], BF16)
        rest, dtr = m.sb("rest", [BCR, T]), m.sb("dtr", [P, T])
        sp_e = m.sb("sp_e", [P, IB, T])
        dt, du = m.sb("dt", [P, 2, IB, T]), m.sb("du", [P, 2, IB, T])
        c_sb, bu, h, hc = m.sb("c", [P, 4, T]), m.sb("bu", [P, 4, 2, T]), m.sb("h", [P, 4, 2, T]), m.sb("hc", [P, 2, 2, T])
        carry = m.sb("carry", [P, 2, STEPS, 2])
        yg, out_sb = m.sb("yg", [P, IB, T]), m.sb("out", [P, 2, 4, C])
        p_b, p_c, p_a = m.ps("b", [P, 2, T]), m.ps("c", [P, T]), m.ps("a", [P, 2, T])
        p_y, p_w = m.ps("y", [P, 2, T]), m.ps("w", [P, T])

        s_w, s_prep, s_a, s_taps = m.sem("weights"), m.sem("a_exp"), m.sem("a"), m.sem("taps")
        s_zero = m.sem("zeroed")
        s_xn, s_st = ([m.sem(f"{k}{i}") for i in range(2)] for k in ("xn", "stored"))
        s_wk, s_wkf = m.sem("work_group"), m.sem("work_emptied")
        s_silu, s_parts, s_hi, s_softplus = m.sem("silu"), m.sem("parts"), m.sem("hi"), m.sem("softplus")
        s_tail, s_keep, s_sp1 = m.sem("tail"), m.sem("keep"), m.sem("softplus_exp")
        s_dt, s_du = m.sem("dt"), m.sem("du")
        s_bb, s_cb, s_cc, s_da = m.sem("b_spread"), m.sem("c_spread"), m.sem("c_copied"), m.sem("da")
        s_bu, s_scan, s_carry, s_hc, s_ys = m.sem("bu"), m.sem("scanned"), m.sem("carried"), m.sem("hc"), m.sem("y_added")
        s_yev, s_yg = m.sem("y_read"), m.sem("yg")
        block = ctx.enter_context(nc.Block())

        xnf = xn.rearrange("s h p k t -> p (s h) k t")
        outf = out.rearrange("s (h g p) c -> p (s h) g c", p=P, g=4)
        LOADS = ((w_in, w_inT.rearrange("(k p) o -> p k o", p=P)), (cw, conv_w), (w_x, w_xT.rearrange("(k p) o -> p k o", p=P)),
                 (w_out, w_outT.rearrange("(k p) o -> p k o", p=P)), (cb_sb, conv_b), (bdt_sb, b_dt), (d_sb, d_skip),
                 (ab_sb, split), (alog, a_log), (ident_sb, ident), (keep_sb, keep))

        NLOADS = len(LOADS) + 3

        def every_chunk(eng, body):
            body(0, 0, 0, True, False)
            with eng.Fori(0, (NC - 2) // 2) as i:
                body(i * 2 + 1, 1, i, False, False)
                body(i * 2 + 2, 0, i + 1, False, False)
            body(NC - 1, 1, NC // 2 - 1, False, True)

        def at_least(eng, sem, v):
            if not isinstance(v, int) or v > 0:
                eng.wait_ge(sem, v)

        @block.sync
        def _(sp):
            for dst, src in LOADS:
                sl = tuple(slice(None) for _ in src.shape)
                sp.dma_start(dst[sl], src).then_inc(s_w, 16)
            sp.dma_start(w_dt[BCR:BCR + RK, :], w_dtT).then_inc(s_w, 16)
            for i in range(2):
                sp.dma_start(du[0:BCR, i, :, :].rearrange("p a n -> p (a n)"), pick[:, i * NS:(i + 1) * NS, :].rearrange("p a n -> p (a n)")
                             ).then_inc(s_w, 16)
            for i in range(2):
                sp.sem_inc(s_st[i], 16)

            def load(c, par):
                src = xnf[:, bass.ds(c, 1), :, :].rearrange("p s k t -> p (s k) t")
                sp.dma_start(xn_sb[:, par, :, :], src).then_inc(s_xn[par], 16)

            def store(c, par):
                sp.wait_ge(s_wkf, freed(NC - 1, GO) + GO if isinstance(c, int) and c == NC - 1 else freed(c + 1, GO))
                dst = outf[:, bass.ds(c, 1), :, :].rearrange("p s g c -> p (s g) c")
                sp.dma_start(dst, out_sb[:, par, :, :]).then_inc(s_st[par], 16)

            load(0, 0)
            load(1, 1)
            sp.wait_ge(s_wk, 8)
            load(2, 0)
            sp.wait_ge(s_wk, group(0, GO) + 8)
            load(3, 1)
            with sp.Fori(0, (NC - 4) // 2) as i:
                for j in range(2):
                    c = i * 2 + (1 + j)
                    store(i * 2 + j, j)
                    sp.wait_ge(s_wk, group(c, GO) + 8)
                    load(i * 2 + (4 + j), j)
            for c in range(NC - 4, NC):
                store(c, c % 2)
            for i in range(2):
                sp.wait_ge(s_st[i], 16 + 16 * NC // 2)

        @block.tensor
        def _(pe):
            pe.wait_ge(s_w, 16 * NLOADS)
            pe.wait_ge(s_taps, IB * TAPS + 2)

            def wait_freed(c, g):
                if c is None:
                    if g > GO:
                        pe.wait_ge(s_wkf, g - GO + (1 if g > GO + 12 else 0))
                else:
                    pe.wait_ge(s_wkf, freed(c, g))

            def close(mm):
                mm.then_inc(s_wk, 1)

            def before_scan(c, pn, half, g):
                wait_freed(c, g + GO)
                if g < 8:
                    if g == 0:
                        pe.wait_ge(s_xn[pn], half * 16 + 16)
                    for kc in range(KC):
                        mm = nc.tensor.matmul(p_w[:, :], w_in[:, kc, g * P:(g + 1) * P], xn_sb[:, pn, kc, :],
                                              start=(kc == 0), stop=(kc == KC - 1))
                elif g < 12:
                    cb = g - 8
                    for k in range(TAPS):
                        mm = nc.tensor.matmul(p_w[:, :], taps[:, cb * TAPS + k, :], hs[:, pn, cb, k:k + T],
                                              start=(k == 0), stop=(k == TAPS - 1))
                elif g == 12:
                    pe.wait_ge(s_silu, 1 if c is None else c + 2)
                    for cb in range(IB):
                        mm = nc.tensor.matmul(p_w[0:BCR + RK, :], w_x[:, cb, :], u[:, pn, cb, :], start=(cb == 0), stop=(cb == IB - 1))
                else:
                    cb = g - 13
                    mm = nc.tensor.matmul(p_w[:, :], w_dt[BCR:BCR + RK, cb * P:(cb + 1) * P], dtr[BCR:BCR + RK, :],
                                          start=True, stop=True)
                close(mm)

            def output(c, last_c, g):
                wait_freed(c, g)
                pe.wait_ge(s_yg, last_c * IB + IB)
                for t in range(2):
                    tok = (2 * g + t) * P
                    for cb in range(IB):
                        mm = nc.tensor.matmul(p_w[:, t * C:(t + 1) * C], yg[:, cb, tok:tok + P], w_out[:, cb, :],
                                              start=(cb == 0), stop=(cb == IB - 1))
                close(mm)

            def spread(c, p, k):
                K = c * STEPS + k
                n = k % NS
                if k == 0:
                    pe.wait_ge(s_parts, c + 1)
                pe.wait_ge(s_bu, K + 1)
                nc.tensor.matmul(p_b[:, k % 2, :], pick_sb[:, n, :], parts[:, p, :], start=True, stop=True).then_inc(s_bb, 1)
                pe.wait_ge(s_cc, K + 1)
                nc.tensor.matmul(p_c[:, :], pick_sb[:, NS + n, :], parts[:, p, :], start=True, stop=True).then_inc(s_cb, 1)

            def add_y(c, k):
                K = c * STEPS + k
                if k % NS == 0:
                    pe.wait_ge(s_yev, c * 4 + (2 * (k // NS) + 2))
                pe.wait_ge(s_hc, K + 3)
                for j in range(2):
                    mm = nc.tensor.matmul(p_y[:, j, :], ident_sb[:, :], hc[:, k % 2, j, :],
                                          start=(k % NS == 0), stop=(k % NS == NS - 1))
                mm.then_inc(s_ys, 1)

            for g in range(GA):
                before_scan(None, 0, 0, g)
            spread(0, 0, 0)

            def body(c, p, half, first, last):
                nhalf = half + 1 if p == 1 else half
                for k in range(STEPS):
                    if k + 1 < STEPS:
                        spread(c, p, k + 1)
                    elif not last:
                        spread(c + 1, 1 - p, 0)
                    if OUT_AT <= k < OUT_AT + 2 and not first:
                        output(c, c + -1, k - OUT_AT)
                    if not last:
                        for at, g0, n in ((HS_AT, 0, 12), (XP_AT, 12, 1), (DT_AT, 13, 4)):
                            if at <= k < at + n:
                                before_scan(c, 1 - p, nhalf, g0 + k - at)
                    if k >= 2:
                        add_y(c, k - 2)
                    elif not first:
                        add_y(c + -1, STEPS + k - 2)

            every_chunk(pe, body)
            for k in range(2):
                add_y(NC - 1, STEPS + k - 2)
            for g in range(2):
                pe.wait_ge(s_wkf, freed(NC - 1, GO) + g)
                pe.wait_ge(s_yg, NC * IB)
                for t in range(2):
                    tok = (2 * g + t) * P
                    for cb in range(IB):
                        mm = nc.tensor.matmul(p_w[:, t * C:(t + 1) * C], yg[:, cb, tok:tok + P], w_out[:, cb, :],
                                              start=(cb == 0), stop=(cb == IB - 1))
                close(mm)

        @block.scalar
        def _(act):
            act.wait_ge(s_w, 16 * NLOADS)
            act.sem_inc(s_cc, 1)
            nc.scalar.activation(alog[:, :], alog[:, :], ACT.Exp).then_inc(s_prep, 1)
            act.wait_ge(s_prep, 1)
            nc.scalar.mul(a_sb[:, :], alog[:, :], -1.0).then_inc(s_a, 1)
            act.wait_ge(s_a, 1)

            def before_scan(c, pn, g):
                act.wait_ge(s_wk, g + 1 if c is None else group(c, g + GO) + 1)
                if g < 4:
                    nc.scalar.copy(hs[:, pn, g, TAPS - 1:], p_w[:, :]).then_inc(s_wkf, 1)
                elif g < 8:
                    nc.scalar.copy(gate[:, pn, g - 4, :], p_w[:, :]).then_inc(s_wkf, 1)
                elif g < 12:
                    nc.scalar.activation(u[:, pn, g - 8, :], p_w[:, :], ACT.Identity, bias=cb_sb[:, g - 8:g - 7]).then_inc(s_wkf, 1)
                elif g == 12:
                    nc.scalar.copy(dtr[BCR:BCR + RK, :], p_w[BCR:BCR + RK, :]).then_inc(s_wkf, 1)
                else:
                    cb = g - 13
                    nc.scalar.activation(dt[:, pn, cb, :], p_w[:, :], ACT.Relu, bias=bdt_sb[:, cb:cb + 1])
                    nc.scalar.activation(sp_e[:, cb, :], p_w[:, :], ACT.Abs, bias=bdt_sb[:, cb:cb + 1]).then_inc(s_wkf, 1)

            def tail(c, pn):
                nc.scalar.activation(hs[:, pn, :, 0:TAPS - 1], hs[:, 1 - pn, :, T:T + TAPS - 1], ACT.Copy,
                                     scale=keep_now[:, pn:pn + 1]).then_inc(s_tail, 1)

            def silu(c, pn):
                act.wait_ge(s_wkf, 12 if c is None else freed(c, GO + 12))
                nc.scalar.activation(gate[:, pn, :, :], gate[:, pn, :, :], ACT.Silu)
                nc.scalar.activation(u[:, pn, :, :], u[:, pn, :, :], ACT.Silu).then_inc(s_silu, 1)

            def softplus(c):
                act.wait_ge(s_wkf, 18 if c is None else freed(c, GO + 16) + 1)
                nc.scalar.activation(sp_e[:, :, :], sp_e[:, :, :], ACT.Exp, scale=-1.0).then_inc(s_sp1, 1)
                act.wait_ge(s_sp1, 1 if c is None else c + 2)
                nc.scalar.activation(sp_e[:, :, :], sp_e[:, :, :], ACT.Ln, bias=1.0).then_inc(s_softplus, 1)

            def copy_c(c, k):
                K = c * STEPS + k
                act.wait_ge(s_cb, K + 1)
                at_least(act, s_hc, K + -1)
                nc.scalar.copy(c_sb[:, k % 4, :], p_c[:, :]).then_inc(s_cc, 1)

            def decay(c, p, k):
                for j in range(2):
                    cb = 2 * (k // NS) + j
                    act.wait_ge(s_scan, (c * STEPS + k) * 2 + (j + 1))
                    nc.scalar.activation(p_a[:, j, :], dt[:, p, cb, :], ACT.Exp,
                                         scale=a_sb[:, cb * NS + k % NS:cb * NS + k % NS + 1]).then_inc(s_da, 1)

            def carry_on(c, p, k):
                act.wait_ge(s_scan, (c * STEPS + k) * 2 + 4)
                nc.scalar.activation(carry[:, 1 - p, k, :], h[:, k % 4, :, T - 1], ACT.Copy,
                                     scale=keep_now[:, 1 - p:2 - p]).then_inc(s_carry, 1)

            def output(c, last_c, lp, lhalf, g):
                act.wait_ge(s_wk, (group(c, 0) if c is not None else group(NC - 1, GO)) + g + 1)
                act.wait_ge(s_st[lp], lhalf * 16 + 16)
                nc.scalar.copy(out_sb[:, lp, 2 * g:2 * g + 2, :], p_w[:, :].rearrange("p (t n) -> p t n", t=2)
                               ).then_inc(s_wkf, 1)

            act.wait_ge(s_zero, 2)
            for g in range(GA):
                before_scan(None, 0, g)
                if g == 11:
                    silu(None, 0)
            softplus(None)
            copy_c(0, 0)

            def body(c, p, half, first, last):
                lc = c + -1
                lhalf = half if p == 1 else (half - 1 if isinstance(half, int) else half + -1)
                nc.scalar.copy(keep_now[:, 1 - p:2 - p], keep_sb[:, bass.ds(c + 1, 1)]).then_inc(s_keep, 1)
                act.wait_ge(s_keep, c + 1)
                act.wait_ge(s_dt, c * IB + IB)
                for k in range(STEPS):
                    if k + 1 < STEPS:
                        copy_c(c, k + 1)
                    elif not last:
                        copy_c(c + 1, 0)
                    decay(c, p, k)
                    if k >= 1:
                        carry_on(c, p, k - 1)
                    if OUT_AT <= k < OUT_AT + 2 and not first:
                        output(c, lc, 1 - p, lhalf, k - OUT_AT)
                    if not last:
                        if k == HS_AT - 1:
                            tail(c, 1 - p)
                        for at, g0, n in ((HS_AT, 0, 12), (XP_AT, 12, 1), (DT_AT, 13, 4)):
                            if at <= k < at + n:
                                before_scan(c, 1 - p, g0 + k - at)
                        if k == SILU_AT:
                            silu(c, 1 - p)
                        if k == SP_AT:
                            softplus(c)
                carry_on(c, p, STEPS - 1)

            every_chunk(act, body)
            for g in range(2):
                output(None, NC - 1, 1, NC // 2 - 1, g)

        @block.vector
        def _(dve):
            dve.wait_ge(s_w, 16 * NLOADS)
            for i in range(IB * TAPS):
                nc.vector.tensor_scalar(taps[:, i, :], ident_sb[:, :], cw[:, i:i + 1], None, ALU.mult).then_inc(s_taps, 1)
            for i in range(2):
                nc.vector.tensor_copy(pick_sb[:, i * NS:(i + 1) * NS, :].rearrange("p a n -> p (a n)"),
                                      du[0:BCR, i, :, :].rearrange("p a n -> p (a n)")).then_inc(s_taps, 1)
            nc.vector.memset(hs[:, 0, :, 0:TAPS - 1], 0.0).then_inc(s_zero, 1)
            nc.vector.memset(carry[:, 0, :, :], 0.0).then_inc(s_zero, 1)
            dve.wait_ge(s_zero, 2)
            dve.sem_inc(s_bu, 2)
            dve.sem_inc(s_scan, 2)
            dve.sem_inc(s_yev, 2)
            dve.sem_inc(s_carry, STEPS)

            def split_bc(c, pn):
                dve.wait_ge(s_wk, 13 if c is None else group(c, GO + 12) + 1)
                nc.vector.tensor_copy(hi[:, :], p_w[0:BCR, :]).then_inc(s_hi, 1)
                n = 0 if c is None else c * 2 + 2
                dve.wait_ge(s_hi, n + 1)
                nc.vector.scalar_tensor_tensor(rest[:, :], hi[:, :], ab_sb[0:BCR, 0:1], p_w[0:BCR, :], ALU.mult, ALU.add
                                               ).then_inc(s_wkf, 1)
                dve.wait_ge(s_wkf, 14 if c is None else freed(c, GO + 13))
                nc.vector.tensor_copy(mid[:, :], rest[:, :]).then_inc(s_hi, 1)
                dve.wait_ge(s_hi, n + 2)
                nc.vector.scalar_tensor_tensor(parts[:, pn, :], mid[:, :], ab_sb[0:BCR, 1:2], rest[:, :], ALU.mult, ALU.add
                                               ).then_inc(s_parts, 1)

            def times_b(c, p, k):
                K = c * STEPS + k
                if k == 0:
                    dve.wait_ge(s_du, c * IB + IB)
                q = k // NS
                dve.wait_ge(s_bb, K + 1)
                at_least(dve, s_scan, K * 2 + -4)
                nc.vector.tensor_tensor(bu[:, k % 4, :, :], du[:, p, 2 * q:2 * q + 2, :],
                                        p_b[:, k % 2:k % 2 + 1, :].broadcast_to([P, 2, T]), ALU.mult).then_inc(s_bu, 1)

            def scan(c, p, k):
                K = c * STEPS + k
                dve.wait_ge(s_bu, K + 3)
                dve.wait_ge(s_carry, K + (STEPS - 3))
                at_least(dve, s_hc, K + -1)
                for j in range(2):
                    dve.wait_ge(s_da, K * 2 + (j + 1))
                    nc.vector.tensor_tensor_scan(h[:, k % 4, j, :], p_a[:, j, :], bu[:, k % 4, j, :], carry[:, p, k, j:j + 1],
                                                 ALU.mult, ALU.add).then_inc(s_scan, 1)

            def read_y(c, p, q):
                dve.wait_ge(s_ys, c * STEPS + (NS * (q + 1) + 2))
                if q == 0 and not (isinstance(c, int) and c == 0):
                    dve.wait_ge(s_wk, group(c, GO))
                for j in range(2):
                    cb = 2 * q + j
                    nc.vector.scalar_tensor_tensor(yg[:, cb, :], u[:, p, cb, :], d_sb[:, cb:cb + 1], p_y[:, j, :],
                                                   ALU.mult, ALU.add).then_inc(s_yev, 1)

            split_bc(None, 0)
            times_b(0, 0, 0)

            def body(c, p, half, first, last):
                for k in range(STEPS):
                    if k + 1 < STEPS:
                        times_b(c, p, k + 1)
                    elif not last:
                        times_b(c + 1, 1 - p, 0)
                    scan(c, p, k)
                    if k == XP_AT and not last:
                        split_bc(c, 1 - p)
                    if k == 1 and not first:
                        read_y(c + -1, 1 - p, 1)
                    if k == NS + 1:
                        read_y(c, p, 0)

            every_chunk(dve, body)
            read_y(NC - 1, 1, 1)

        @block.gpsimd
        def _(pool):
            pool.sem_inc(s_hc, 2)
            pool.sem_inc(s_ys, 2)

            def make_dt(c, pn, cb):
                n = 0 if c is None else c + 1
                pool.wait_ge(s_softplus, n + 1)
                nc.gpsimd.tensor_tensor(dt[:, pn, cb, :], dt[:, pn, cb, :], sp_e[:, cb, :], ALU.add).then_inc(s_dt, 1)
                pool.wait_ge(s_dt, n * IB + (cb + 1))
                nc.gpsimd.tensor_tensor(du[:, pn, cb, :], dt[:, pn, cb, :], u[:, pn, cb, :], ALU.mult).then_inc(s_du, 1)

            def times_c(c, k):
                K = c * STEPS + k
                pool.wait_ge(s_scan, K * 2 + 4)
                pool.wait_ge(s_cc, K + 2)
                pool.wait_ge(s_ys, K + 1)
                nc.gpsimd.tensor_tensor(hc[:, k % 2, :, :], h[:, k % 4, :, :],
                                        c_sb[:, k % 4:k % 4 + 1, :].broadcast_to([P, 2, T]), ALU.mult).then_inc(s_hc, 1)

            def gate_y(c, p, q):
                pool.wait_ge(s_yev, c * 4 + (2 * q + 4))
                for j in range(2):
                    cb = 2 * q + j
                    nc.gpsimd.tensor_tensor(yg[:, cb, :], yg[:, cb, :], gate[:, p, cb, :], ALU.mult).then_inc(s_yg, 1)

            for cb in range(IB):
                make_dt(None, 0, cb)

            def body(c, p, half, first, last):
                for k in range(STEPS):
                    times_c(c, k)
                    if k == 1 and not first:
                        gate_y(c + -1, 1 - p, 1)
                    if k == NS + 1:
                        gate_y(c, p, 0)
                    if DU_AT <= k < DU_AT + IB and not last:
                        make_dt(c, 1 - p, k - DU_AT)

            every_chunk(pool, body)
            gate_y(NC - 1, 1, 1)


def combine_and_whiten(nc, mix, x1, flips, wf, ln_w, ln_b, ident, blocks, gamma, beta, out):
    NT = B * TILES
    ORD = 4
    ITERS = 26
    ROWS = float(B * N)
    with ExitStack() as outer:
        mo = Pool_(nc, outer, "cw")
        x2 = mo.sb("x2", [P, NT, C])
        ident_sb, ones = mo.sb("ident", [P, P]), mo.sb("ones", [P, P])
        mean_sb = mo.sb("mean", [P, C])
        p_sum = mo.ps("sum", [P, 512])
        with ExitStack() as ctx:
            m = Pool_(nc, ctx, "co")
            flip_sb, wf_sb, wf4 = m.sb("flips", [P, ORD - 1, P]), m.sb("wf", [P, C]), m.sb("wf4", [P, C])
            lw_sb, lb_sb = m.sb("lw", [P, C]), m.sb("lb", [P, C])
            xo = m.sb("xo", [P, 4, ORD + 1, C])
            h0, acc, y = m.sb("h0", [P, 2, C]), m.sb("acc", [P, 4, C]), m.sb("y", [P, 4, C])
            sq, ss, ms, rt, rs = (m.sb(k, [P, 4, 4] if k != "sq" else [P, 4, C]) for k in ("sq", "ss", "ms", "rt", "rs"))
            stats, mv = m.sb("stats", [P, 4, 6]), m.sb("mv", [P, 4, 2])
            ve, rt2, rs2, cen = m.sb("ve", [P, 4]), m.sb("rt2", [P, 4]), m.sb("rs2", [P, 4]), m.sb("cen", [P, 2, C])
            p_h = m.ps("h", [P, 2, 4, C])

            s_w, s_prep, s_passed = m.sem("weights"), m.sem("prepared"), m.sem("dve_passed")
            s_in = [m.sem(f"loaded{i}") for i in range(4)]
            s_g, s_h0, s_ss, s_ms, s_rt, s_rs = (m.sem(k) for k in ("h_summed", "h0", "squares", "ms", "root", "recip"))
            s_acc, s_y, s_bn, s_mv, s_ve = (m.sem(k) for k in ("acc", "y", "stats", "mean_var", "var_eps"))
            s_rt2, s_rs2, s_cen, s_x2, s_sum = (m.sem(k) for k in ("root2", "recip2", "centred", "x2", "summed"))
            block = ctx.enter_context(nc.Block())

            mv_dram = mix.rearrange("(o b) (t p) c -> p o (b t) c", p=P, b=B)
            x1_dram = x1.rearrange("b (t p) c -> p (b t) c", p=P)
            LOADS = ((flip_sb, flips), (wf_sb, wf), (lw_sb, ln_w), (lb_sb, ln_b), (ident_sb, ident))

            def every_tile(body):
                def run(eng):
                    body(0, 0, 0)
                    body(1, 1, 0)
                    with eng.Fori(0, (NT - 4) // 4) as i:
                        for j in range(4):
                            body(i * 4 + (2 + j), (2 + j) % 4, i + (2 + j) // 4)
                    body(NT - 2, 2, NT // 4 - 1)
                    body(NT - 1, 3, NT // 4 - 1)
                return run

            def inside(n, lo, hi):
                return not isinstance(n, int) or (n - lo >= 0 and n + hi < NT)

            @block.sync
            def _(sp):
                for dst, src in LOADS:
                    sl = tuple(slice(None) for _ in src.shape)
                    sp.dma_start(dst[sl], src).then_inc(s_w, 16)
                sp.sem_inc(s_g, 4)
                sp.sem_inc(s_h0, 4)
                with sp.Fori(0, B) as b:
                    with sp.Fori(0, TILES // 4) as i:
                        for j in range(4):
                            n = b * TILES + i * 4 + j
                            back = b * TILES + i * -4 + (TILES - 1 - j)
                            sp.wait_ge(s_g, n + 1)
                            sp.wait_ge(s_h0, n + 1)
                            for o, t in ((0, n), (2, back)):
                                sp.dma_start(xo[:, j, o:o + 2, :], mv_dram[:, o:o + 2, bass.ds(t, 1), :].rearrange("p o t c -> p o (t c)")
                                             ).then_inc(s_in[j], 16)
                            sp.dma_start(xo[:, j, 4, :], x1_dram[:, bass.ds(n, 1), :].rearrange("p t c -> p (t c)")
                                         ).then_inc(s_in[j], 16)

            @block.tensor
            def _(pe):
                pe.wait_ge(s_w, 16 * len(LOADS))
                pe.wait_ge(s_prep, 2)

                def gather(n, r, quarter):
                    pe.wait_ge(s_in[r], quarter * 48 + 48)
                    pe.wait_ge(s_acc, n * 4 + 4)
                    for o in range(1, ORD):
                        dst = p_h[:, r % 2, o - 1, :]
                        nc.tensor.matmul(dst, flip_sb[:, o - 1, :], xo[:, r, o, :], start=True, stop=False)
                        mm = nc.tensor.matmul(dst, ident_sb[:, :], xo[:, r, 4, :], start=False, stop=True)
                    mm.then_inc(s_g, 1)

                def column_sums(n, first, last):
                    pe.wait_ge(s_x2, n + 1)
                    nc.tensor.matmul(p_sum[:, 0:C], ones[:, :], x2[:, bass.ds(n, 1), :].rearrange("p t c -> p (t c)"),
                                     start=first, stop=last, skip_group_check=True).then_inc(s_sum, 1)

                gather(0, 0, 0)

                def body(n, r, quarter):
                    if inside(n, 0, 1):
                        gather(n + 1, (r + 1) % 4, quarter + (r + 1) // 4)
                    if inside(n, 3, 0):
                        column_sums(n + -3, isinstance(n, int) and n == 3, False)

                for n in range(4):
                    body(n, n % 4, 0)
                with pe.Fori(0, (NT - 8) // 4) as i:
                    for j in range(4):
                        body(i * 4 + (4 + j), j, i + 1)
                for n in range(NT - 4, NT):
                    body(n, n % 4, NT // 4 - 1)
                for n in range(NT - 3, NT):
                    column_sums(n, False, n == NT - 1)

            @block.vector
            def _(dve):
                nc.vector.memset(ones[:, :], 1.0).then_inc(s_prep, 1)
                dve.wait_ge(s_w, 16 * len(LOADS))
                nc.vector.tensor_scalar(wf4[:, :], wf_sb[:, :], 1.0 / ORD, None, ALU.mult).then_inc(s_prep, 1)
                dve.sem_inc(s_acc, 8)

                def scale_sum(n, r):
                    dve.wait_ge(s_rt, n + 1)
                    nc.vector.reciprocal(rs[:, r, :], rt[:, r, :]).then_inc(s_rs, 1)
                    dve.wait_ge(s_rs, n + 1)
                    dve.wait_ge(s_h0, n + 5)
                    dve.wait_ge(s_g, n + 5)
                    nc.vector.tensor_scalar(acc[:, r, :], h0[:, r % 2, :], rs[:, r, 0:1], None, ALU.mult).then_inc(s_acc, 1)
                    for o in range(1, ORD):
                        dve.wait_ge(s_acc, n * 4 + (8 + o))
                        nc.vector.scalar_tensor_tensor(acc[:, r, :], p_h[:, r % 2, o - 1, :], rs[:, r, o:o + 1], acc[:, r, :],
                                                       ALU.mult, ALU.add).then_inc(s_acc, 1)

                def moments(n, r):
                    dve.wait_ge(s_y, n + 1)
                    nc.vector.bn_stats(stats[:, r, :], y[:, r, :]).then_inc(s_bn, 1)
                    dve.wait_ge(s_bn, n + 1)
                    dve.sem_inc(s_passed, 1)
                    nc.vector.bn_aggr(mv[:, r, :], stats[:, r, :]).then_inc(s_mv, 1)
                    dve.wait_ge(s_mv, n + 1)
                    nc.vector.tensor_scalar(ve[:, r:r + 1], mv[:, r, 1:2], 1e-5, None, ALU.add).then_inc(s_ve, 1)

                def layer_norm(n, r):
                    dve.wait_ge(s_rt2, n + 1)
                    nc.vector.reciprocal(rs2[:, r:r + 1], rt2[:, r:r + 1]).then_inc(s_rs2, 1)
                    nc.vector.scalar_tensor_tensor(cen[:, r % 2, :], y[:, r, :], mv[:, r, 0:1], lw_sb[:, :], ALU.subtract, ALU.mult
                                                   ).then_inc(s_cen, 1)
                    dve.wait_ge(s_rs2, n + 1)
                    dve.wait_ge(s_cen, n + 1)
                    nc.vector.scalar_tensor_tensor(x2[:, bass.ds(n, 1), :].rearrange("p t c -> p (t c)"), cen[:, r % 2, :],
                                                   rs2[:, r:r + 1], lb_sb[:, :], ALU.mult, ALU.add).then_inc(s_x2, 1)

                def mean_square(n, r):
                    dve.wait_ge(s_ss, n * 4 + 4)
                    nc.vector.tensor_scalar(ms[:, r, :], ss[:, r, :], 1.0 / C, 1e-5, ALU.mult, ALU.add).then_inc(s_ms, 1)

                mean_square(0, 0)

                def body(n, r, quarter):
                    scale_sum(n, r)
                    if inside(n, 1, 0):
                        moments(n + -1, (r - 1) % 4)
                    if inside(n, 2, 0):
                        layer_norm(n + -2, (r - 2) % 4)
                    if inside(n, 0, 1):
                        mean_square(n + 1, (r + 1) % 4)

                every_tile(body)(dve)
                moments(NT - 1, 3)
                layer_norm(NT - 2, 2)
                layer_norm(NT - 1, 3)
                dve.wait_ge(s_sum, NT)
                nc.vector.tensor_scalar(mean_sb[:, :], p_sum[:, 0:C], 1.0 / ROWS, None, ALU.mult).then_inc(s_sum, 1)

            @block.scalar
            def _(act):
                def squares(n, r):
                    act.wait_ge(s_h0, n + 5)
                    act.wait_ge(s_g, n + 5)
                    for o in range(ORD):
                        src = h0[:, r % 2, :] if o == 0 else p_h[:, r % 2, o - 1, :]
                        nc.scalar.activation(sq[:, o, :], src, ACT.Square, accum_out=ss[:, r, o:o + 1]).then_inc(s_ss, 1)

                def root(n, r):
                    act.wait_ge(s_ms, n + 1)
                    nc.scalar.activation(rt[:, r, :], ms[:, r, :], ACT.Sqrt).then_inc(s_rt, 1)

                def root2(n, r):
                    act.wait_ge(s_ve, n + 1)
                    nc.scalar.activation(rt2[:, r:r + 1], ve[:, r:r + 1], ACT.Sqrt).then_inc(s_rt2, 1)

                squares(0, 0)
                root(0, 0)

                def body(n, r, quarter):
                    if inside(n, 0, 1):
                        squares(n + 1, (r + 1) % 4)
                    if inside(n, 1, 0):
                        root2(n + -1, (r - 1) % 4)
                    if inside(n, 0, 1):
                        root(n + 1, (r + 1) % 4)

                every_tile(body)(act)
                root2(NT - 1, 3)

            @block.gpsimd
            def _(pool):
                pool.wait_ge(s_prep, 2)

                def add_residual(n, r, quarter):
                    pool.wait_ge(s_in[r], quarter * 48 + 48)
                    pool.wait_ge(s_acc, n * 4 + 4)
                    nc.gpsimd.tensor_tensor(h0[:, r % 2, :], xo[:, r, 0, :], xo[:, r, 4, :], ALU.add).then_inc(s_h0, 1)

                add_residual(0, 0, 0)
                add_residual(1, 1, 0)

                def body(n, r, quarter):
                    pool.wait_ge(s_acc, n * 4 + 12)
                    nc.gpsimd.tensor_tensor(y[:, r, :], acc[:, r, :], wf4[:, :], ALU.mult).then_inc(s_y, 1)
                    if inside(n, 0, 2):
                        add_residual(n + 2, (r + 2) % 4, quarter + (r + 2) // 4)

                every_tile(body)(pool)

        with ExitStack() as ctx:
            m = Pool_(nc, ctx, "wh")
            mask_sb, g_sb, b_sb = m.sb("mask", [P, P]), m.sb("gamma", [P, C]), m.sb("beta", [P, C])
            cov, diag, junk = m.sb("cov", [P, KC, P]), m.sb("diag", [P, KC]), m.sb("junk", [P, P])
            tr, itr, rtr = m.sb("trace", [P, KC]), m.sb("itrace", [P, KC]), m.sb("rtrace", [P, KC])
            i15 = m.sb("i15", [P, P])
            Y, Z, Wm = m.sb("Y", [P, 2, KC, 2, P]), m.sb("Z", [P, 2, KC, 2, P]), m.sb("W", [P, KC, 2, P])
            proj = m.sb("proj", [P, KC, P])
            cT = m.sb("cT", [P, 2, 2, KC, P])
            o_sb = m.sb("o", [P, 4, 2, C])
            p_cov = [m.ps(f"cov{i}", [P, 512]) for i in range(2)]
            p_t, p_o = m.ps("t", [P, 2, 512]), m.ps("o", [P, 2, 512])

            s_w, s_c, s_cov, s_prep = m.sem("weights"), m.sem("centred"), m.sem("covariance"), m.sem("step")
            s_tr, s_rt = m.sem("trace"), m.sem("root")
            s_zy, s_wm, s_yz, s_new = ([m.sem(f"{k}{i}") for i in range(KC)] for k in ("zy", "w", "yz", "new"))
            s_t, s_ct, s_o, s_ob = m.sem("turned"), m.sem("turned_copied"), m.sem("whitened"), m.sem("out_ready")
            s_proj = m.sem("proj")
            s_st = [m.sem(f"stored{i}") for i in range(4)]
            block = ctx.enter_context(nc.Block())
            LOADS = ((mask_sb, blocks), (g_sb, gamma), (b_sb, beta))
            CH = 8
            out_dram = out.rearrange("b (t p) c -> p (b t) c", p=P)

            @block.sync
            def _(sp):
                for dst, src in LOADS:
                    sp.dma_start(dst[:, :], src).then_inc(s_w, 16)
                for n in range(NT // 2):
                    sp.wait_ge(s_ob, n + 1)
                    sp.dma_start(out_dram[:, 2 * n:2 * n + 2, :], o_sb[:, n % 4, :, :]).then_inc(s_st[n % 4], 16)
                for i in range(4):
                    sp.wait_ge(s_st[i], 16 * NT // 8)

            @block.tensor
            def _(pe):
                for t in range(NT):
                    pe.wait_ge(s_c, t // CH + 1)
                    for kc in range(KC):
                        blk = x2[:, t, kc * P:(kc + 1) * P]
                        mm = nc.tensor.matmul(p_cov[kc][:, 0:P], blk, blk, start=(t == 0), stop=(t == NT - 1))
                mm.then_inc(s_cov, 1)
                pe.wait_ge(s_prep, 8)
                nc.tensor.matmul(p_t[:, 0, 0:KC], mask_sb[:, :], diag[:, :], start=True, stop=True).then_inc(s_tr, 1)
                for it in range(ITERS):
                    a = it % 2
                    for kc in range(KC):
                        pe.wait_ge(s_new[kc], 2 * it + 2)
                        nc.tensor.matmul(p_cov[kc][:, 0:P], Z[:, a, kc, 1, :], Y[:, a, kc, 0, :], start=True, stop=True)
                        nc.tensor.matmul(p_cov[kc][:, P:2 * P], Y[:, a, kc, 0, :], Z[:, a, kc, 1, :], start=True, stop=True).then_inc(s_zy[kc], 1)
                    for kc in range(KC):
                        pe.wait_ge(s_wm[kc], it + 1)
                        nc.tensor.matmul(p_t[:, kc, 0:P], Y[:, a, kc, 1, :], Wm[:, kc, 0, :], start=True, stop=True)
                        nc.tensor.matmul(p_t[:, kc, P:2 * P], Wm[:, kc, 0, :], Y[:, a, kc, 1, :], start=True, stop=True).then_inc(s_yz[kc], 1)
                        nc.tensor.matmul(p_o[:, kc, 0:P], Wm[:, kc, 1, :], Z[:, a, kc, 0, :], start=True, stop=True)
                        nc.tensor.matmul(p_o[:, kc, P:2 * P], Z[:, a, kc, 0, :], Wm[:, kc, 1, :], start=True, stop=True).then_inc(s_yz[kc], 1)
                pe.wait_ge(s_proj, KC)

                def turn(n):
                    if n >= 2:
                        pe.wait_ge(s_ct, n - 1)
                    for t in range(2):
                        for kc in range(KC):
                            at = (2 * t + kc) * P
                            mm = nc.tensor.transpose(p_t[:, n % 2, at:at + P], x2[:, 2 * n + t, kc * P:(kc + 1) * P], ident_sb[:, :])
                    mm.then_inc(s_t, 1)

                turn(0)
                for n in range(NT // 2):
                    if n + 1 < NT // 2:
                        turn(n + 1)
                    pe.wait_ge(s_ct, n + 1)
                    if n >= 2:
                        pe.wait_ge(s_ob, n - 1)
                    for t in range(2):
                        for kc in range(KC):
                            at = (2 * t + kc) * P
                            mm = nc.tensor.matmul(p_o[:, n % 2, at:at + P], cT[:, n % 2, t, kc, :], proj[:, kc, :], start=True, stop=True)
                    mm.then_inc(s_o, 1)

            @block.scalar
            def _(act):
                act.wait_ge(s_prep, 10)
                nc.scalar.activation(rtr[:, :], tr[:, :], ACT.Sqrt).then_inc(s_rt, 1)
                for it in range(ITERS):
                    for kc in range(KC):
                        act.wait_ge(s_yz[kc], 2 * it + 2)
                        nc.scalar.copy(Z[:, (it + 1) % 2, kc, :, :], p_o[:, kc, 0:2 * P].rearrange("p (a n) -> p a n", a=2)).then_inc(s_new[kc], 1)
                for n in range(NT // 2):
                    act.wait_ge(s_t, n + 1)
                    if n >= 2:
                        act.wait_ge(s_o, n - 1)
                    nc.scalar.copy(cT[:, n % 2, :, :, :], p_t[:, n % 2, :].rearrange("p (t k n) -> p t k n", t=2, k=KC)
                                   ).then_inc(s_ct, 1)

            @block.vector
            def _(dve):
                mean_b = mean_sb[:, None, :].broadcast_to([P, CH, C])
                for i in range(NT // CH):
                    nc.vector.tensor_tensor(x2[:, i * CH:(i + 1) * CH, :], x2[:, i * CH:(i + 1) * CH, :], mean_b, ALU.subtract
                                            ).then_inc(s_c, 1)
                done = [0]

                def step(ins):
                    done[0] += 1
                    ins.then_inc(s_prep, 1)
                    dve.wait_ge(s_prep, done[0])

                dve.wait_ge(s_w, 16 * len(LOADS))
                dve.wait_ge(s_cov, 1)
                for kc in range(KC):
                    step(nc.vector.scalar_tensor_tensor(cov[:, kc, :], p_cov[kc][:, 0:P], 1.0 / ROWS, mask_sb[:, :], ALU.mult, ALU.mult))
                    step(nc.vector.scalar_tensor_tensor(cov[:, kc, :], ident_sb[:, :], 1e-5, cov[:, kc, :], ALU.mult, ALU.add))
                for kc in range(KC):
                    step(nc.vector.tensor_tensor(Wm[:, kc, 0, :], cov[:, kc, :], ident_sb[:, :], ALU.mult))
                    step(nc.vector.tensor_reduce(diag[:, kc:kc + 1], Wm[:, kc, 0, :], AX.X, ALU.add))
                step(nc.vector.tensor_scalar(i15[:, :], ident_sb[:, :], 1.5, None, ALU.mult))
                dve.wait_ge(s_tr, 1)
                step(nc.vector.tensor_copy(tr[:, :], p_t[:, 0, 0:KC]))
                step(nc.vector.reciprocal(itr[:, :], tr[:, :]))
                for kc in range(KC):
                    two = [P, 2, P]
                    nc.vector.tensor_scalar(Y[:, 0, kc, :, :], cov[:, kc:kc + 1, :].broadcast_to(two), itr[:, kc:kc + 1], None,
                                            ALU.mult).then_inc(s_new[kc], 1)
                    nc.vector.tensor_copy(Z[:, 0, kc, :, :], ident_sb[:, None, :].broadcast_to(two)).then_inc(s_new[kc], 1)
                for it in range(ITERS):
                    for kc in range(KC):
                        dve.wait_ge(s_zy[kc], it + 1)
                        nc.vector.scalar_tensor_tensor(Wm[:, kc, :, :], p_cov[kc][:, 0:2 * P].rearrange("p (a n) -> p a n", a=2), -0.5,
                                                       i15[:, None, :].broadcast_to(two), ALU.mult, ALU.add
                                                       ).then_inc(s_wm[kc], 1)
                    for kc in range(KC):
                        dve.wait_ge(s_yz[kc], 2 * it + 2)
                        nc.vector.tensor_copy(Y[:, (it + 1) % 2, kc, :, :], p_t[:, kc, 0:2 * P].rearrange("p (a n) -> p a n", a=2)).then_inc(s_new[kc], 1)
                dve.wait_ge(s_rt, 1)
                step(nc.vector.reciprocal(rtr[:, :], rtr[:, :]))
                for kc in range(KC):
                    dve.wait_ge(s_new[kc], 2 * ITERS + 2)
                    nc.vector.scalar_tensor_tensor(proj[:, kc, :], Z[:, ITERS % 2, kc, 0, :], rtr[:, kc:kc + 1],
                                                   g_sb[:, kc * P:(kc + 1) * P], ALU.mult, ALU.mult).then_inc(s_proj, 1)
                for n in range(NT // 2):
                    dve.wait_ge(s_o, n + 1)
                    if n >= 4:
                        dve.wait_ge(s_st[n % 4], 16 * (n // 4))
                    nc.vector.tensor_tensor(o_sb[:, n % 4, :, :], p_o[:, n % 2, :].rearrange("p (t c) -> p t c", t=2),
                                            b_sb[:, None, :].broadcast_to([P, 2, C]), ALU.add).then_inc(s_ob, 1)


def network(nc, a, out):
    def scratch(name, shape):
        return nc.dram_tensor(name, shape, F32, kind="Internal").ap()

    x0, x1 = scratch("x0", (B, N, C)), scratch("x1", (B, N, C))
    xn = scratch("xn", (SEQS, CHUNKS, P, KC, T))
    mix = scratch("mix", (SEQS, N, C))
    attention(nc, a["xT"], a["x"], a["wqT"], a["wkT"], a["bq"], a["bk"], a["wvT"], a["bv"], a["gamma"], a["ident"], x0)
    fourier_conv(nc, x0, a["w1T"], (a["bn1c"], a["bn1"]), a["fuT"], a["bnf"], a["lfuT"], a["bnl"], a["w2T"], a["dft"],
                 a["dftl"], a["idft"], a["idftl"], a["ident"], a["rms1"], x1, xn)
    mamba(nc, xn, a["w_inT"], a["conv_w"], a["conv_b"], a["w_xT"], a["split"], a["w_dtT"], a["b_dt"], a["a_log"],
          a["d_skip"], a["w_outT"], a["ident"], a["pick"], a["keep"], mix)
    combine_and_whiten(nc, mix, x1, a["flips"], a["wf"], a["ln_w"], a["ln_b"], a["ident"], a["blocks"], a["gamma3"],
                       a["beta3"], out)


def fourier_matrices(np):
    def pair(n):
        w, k = np.arange(n)[:, None], np.arange(n // 2 + 1)[None]
        ang = 2 * np.pi * w * k / n
        weight = np.full((1, n // 2 + 1), 2.0)
        weight[0, 0] = weight[0, -1] = 1
        im = (-weight * np.sin(ang) / np.sqrt(n)).T
        im[0] = im[-1] = 0
        return np.cos(ang) / np.sqrt(n), -np.sin(ang) / np.sqrt(n), (weight * np.cos(ang) / np.sqrt(n)).T, im

    fr, fi, ir, ii = pair(W)
    dft, idft = np.zeros((P, 2, 2, FR)), np.zeros((2, FR, 2, P))
    for r in range(2):
        at = slice(r * W, (r + 1) * W)
        dft[at, 0, r], dft[at, 1, r], idft[r, :, 0, at], idft[r, :, 1, at] = fr, fi, ir, ii
    fr, fi, ir, ii = pair(W // 2)
    dftl, idftl = np.zeros((P, 2, 2, 2, FL)), np.zeros((2, FL, 2, P))
    for r in range(2):
        for half in range(2):
            at = slice(r * W + half * W // 2, r * W + (half + 1) * W // 2)
            dftl[at, half, 0, r], dftl[at, half, 1, r], idftl[r, :, 0, at], idftl[r, :, 1, at] = fr, fi, ir, ii
    f32 = np.float32
    return (dft.reshape(P, 4 * FR).astype(f32), idft.reshape(2 * FR, 2, P).astype(f32),
            dftl.reshape(P, 2, 4 * FL).astype(f32), idftl.reshape(2 * FL, 2, P).astype(f32))


def layouts(np, i):
    d = {}
    x = i["x"].reshape(B, N, C)
    d["x"], d["xT"] = x, x.transpose(0, 2, 1)

    def twice(w):
        gap = np.zeros((w.shape[0], ROW2 - CQ), np.float32)
        return np.concatenate([w, gap, w, gap[:, :1]], 1)

    def twice_col(v, last):
        gap = np.full((ROW2 - CQ,), last, np.float32)
        return np.concatenate([v, gap, v, gap[:1]])[:, None]

    d["wqT"], d["wkT"] = twice(i["L0_conv_Wq"].T), twice(i["L0_conv_Wk"].T)
    d["bq"], d["bk"] = twice_col(i["L0_conv_bq"], 0), twice_col(i["L0_conv_bk"], 1)
    d["wvT"], d["bv"] = i["L0_conv_Wv"].T, i["L0_conv_bv"][None]
    d["gamma"] = np.broadcast_to(i["L0_conv_gamma"], (P, 1))
    d["ident"] = np.eye(P, dtype=np.float32)

    def parts(v):
        return np.concatenate([v[..., 0::2], v[..., 1::2]], -1)

    def bn(*names):
        return np.stack([i["L1_conv_" + n] for n in names])

    d["w1T"], d["w2T"] = i["L1_conv_w1"].T, i["L1_conv_w2"].T
    d["bn1"] = bn("g1", "b1", "m1", "v1")
    d["bn1c"] = d["bn1"].T
    d["bnf"] = parts(bn("fu_g", "fu_b", "fu_m", "fu_v"))
    d["bnl"] = parts(bn("lfu_g", "lfu_b", "lfu_m", "lfu_v"))
    d["fuT"] = parts(i["L1_conv_fu_w"].T.reshape(HC, 2, C))
    d["lfuT"] = parts(i["L1_conv_lfu_w"].T.reshape(HC, 2, C))
    d["dft"], d["idft"], d["dftl"], d["idftl"] = fourier_matrices(np)

    m = {k[len("L2_conv_"):]: v for k, v in i.items() if k.startswith("L2_conv_")}
    d["rms1"] = m["rms_w1"].reshape(KC, P).T

    def by_block(v):
        return v.reshape(IB, P, -1).transpose(1, 0, 2).reshape(P, -1)

    d["w_inT"], d["w_dtT"], d["w_outT"] = m["W_in"].T, m["W_dt"].T, m["W_out"].T
    d["conv_w"], d["conv_b"] = by_block(m["conv_w"]), by_block(m["conv_b"])
    wx = m["W_x"].T
    d["w_xT"] = np.concatenate([wx[:, RK:]] * 3 + [wx[:, :RK]], 1)
    d["b_dt"], d["a_log"], d["d_skip"] = by_block(m["b_dt"]), by_block(m["A_log"]), by_block(m["Dp"])
    copy = np.arange(P)[:, None] // (2 * NS)
    d["split"] = np.concatenate([np.where(copy >= 1, -1, 0), np.where(copy >= 2, -1, 0)], 1).astype(np.float32)
    d["pick"] = np.repeat(np.tile(np.eye(2 * NS, dtype=np.float32), (3, 1))[:, :, None], P, 2)
    d["keep"] = np.repeat((np.arange(SEQS * CHUNKS + 1)[None] % CHUNKS != 0).astype(np.float32), P, 0)

    def on_all(v):
        return np.broadcast_to(v.reshape(1, C), (P, C))

    d["wf"], d["ln_w"], d["ln_b"] = on_all(m["rms_wf"]), on_all(m["ln_w"]), on_all(m["ln_b"])
    d["gamma3"], d["beta3"] = on_all(i["L3_conv_gamma"]), on_all(i["L3_conv_beta"])
    t = np.arange(P)
    r, w = t // W, t % W
    sources = (r * W + W - 1 - w, (1 - r) * W + w, P - 1 - t)
    d["flips"] = np.stack([np.eye(P, dtype=np.float32)[:, s] for s in sources], 1)
    d["blocks"] = np.kron(np.eye(P // M), np.ones((M, M))).astype(np.float32)
    return {k: np.ascontiguousarray(v) for k, v in d.items()}


def kernel(**inputs):
    import numpy as np
    import concourse.bacc as bacc
    from concourse import mybir as mb
    from concourse.bass_utils import run_bass_kernel_spmd

    nc = bacc.Bacc("TRN2", target_bir_lowering=False, num_devices=1)
    arrays = {f"in_{k}": v for k, v in layouts(np, {k: np.asarray(v) for k, v in inputs.items()}).items()}
    a = {k[3:]: nc.dram_tensor(k, v.shape, mb.dt.from_np(v.dtype), kind="ExternalInput").ap() for k, v in arrays.items()}
    out = nc.dram_tensor("out_0", (B, N, C), F32, kind="ExternalOutput").ap()
    network(nc, a, out)
    r = run_bass_kernel_spmd(nc, [arrays], core_ids=[0])
    return r.results[0]["out_0"].reshape(B, H, W, C)
```

```python
from contextlib import ExitStack

import concourse.bass as bass
from concourse import mybir

F32 = mybir.dt.float32
BF16 = mybir.dt.bfloat16
ALU = mybir.AluOpType
ACT = mybir.ActivationFunctionType
AX = mybir.AxisListType

P = 128
B, H, W, C = 2, 64, 64, 256
N = H * W
KC = C // P
TILES = N // P
CQ = C // 8

I = 2 * C
IB = I // P
NS = 16
RK = 16
TAPS = 4
T = 512
CHUNKS = N // T
SEQS = 4 * B

M = 16


class Pool_:

    def __init__(self, nc, ctx, tag):
        self.nc, self.ctx, self.tag = nc, ctx, tag

    def sb(self, name, shape, dt=F32):
        return self.ctx.enter_context(self.nc.sbuf_tensor(f"{self.tag}_{name}", shape, dt))

    def ps(self, name, shape, dt=F32):
        return self.ctx.enter_context(self.nc.psum_tensor(f"{self.tag}_p_{name}", shape, dt))

    def sem(self, name):
        return self.ctx.enter_context(self.nc.semaphore(f"{self.tag}_s_{name}"))


def attention(nc, xT, x, wqT, wkT, bq, bk, wvT, bv, gamma, ident, halves, x0):
    LOW = 2 * CQ
    LM = LOW + 3
    IT = 512
    JP = TILES // 2
    with ExitStack() as ctx:
        m = Pool_(nc, ctx, "at")
        xT_sb = m.sb("xT", [P, KC, N])
        wq_sb, wk_sb = m.sb("wq", [P, KC, P]), m.sb("wk", [P, KC, P])
        wv_sb = m.sb("wv", [P, KC, C])
        bq_sb, bk_sb, halves_sb = m.sb("bq", [P, 1]), m.sb("bk", [P, 1]), m.sb("halves", [P, 4])
        bv_sb, gbv = m.sb("bv", [P, C]), m.sb("gbv", [P, C])
        gamma_sb, ident_sb, ident16 = m.sb("gamma", [P, 1]), m.sb("ident", [P, P]), m.sb("ident16", [P, P], BF16)
        qa, ka, qb, kb = m.sb("qa", [P, N], BF16), m.sb("ka", [P, N], BF16), m.sb("qb", [LM, N], BF16), m.sb("kb", [LM, N], BF16)
        whole, hi = m.sb("whole", [P, 2, IT]), m.sb("hi", [P, 2, IT], BF16)
        rest, mid = m.sb("rest", [LOW, 2, IT]), m.sb("mid", [LOW, 2, IT], BF16)
        q_now = m.sb("qnow", [P, 2, 2, IT], BF16)
        v_sb = m.sb("v", [P, TILES, C + 1])
        part_max = m.sb("pmax", [P, TILES, 4])
        negmax, neg_rest = m.sb("negmax", [P, TILES]), m.sb("negrest", [P, 2, TILES])
        neg3 = m.sb("neg3", [P, 3, TILES], BF16)
        probs = m.sb("probs", [P, 2, 2, IT])
        x_now, xb = m.sb("xnow", [P, 2, 4, C]), m.sb("xb", [P, 2, 4, C])
        recip = m.sb("recip", [P, 4])
        rg = m.sb("rg", [P, 4])
        out_sb = m.sb("out", [P, 2, 4, C])
        ps = m.ps("all", [P, 8, 512])

        s_w, s_xT = m.sem("weights"), m.sem("xT_loaded")
        s_const = m.sem("consts_set")
        s_proj, s_whole, s_hi = m.sem("projected"), m.sem("projection_copied"), m.sem("hi")
        s_first, s_rest, s_mid, s_second = m.sem("first_rows"), m.sem("rest"), m.sem("mid"), m.sem("second_rows")
        s_v, s_vc = m.sem("values"), m.sem("values_copied")
        s_mx, s_mx_free = m.sem("scores_for_max"), m.sem("max_taken")
        s_neg, s_negT, s_negrow = m.sem("negmax"), m.sem("negmax_row"), m.sem("negmax_row_in_q")
        s_pm, s_xb = m.sem("max_split_step"), m.sem("x_with_bias")
        s_passed = m.sem("pool_passed")
        s_qn, s_qn_free = m.sem("q_now"), m.sem("q_now_free")
        s_sc, s_pr, s_pv = m.sem("scores"), m.sem("probs"), m.sem("pair_summed")
        s_x = [m.sem("x_now0"), m.sem("x_now1")]
        s_rc, s_rg, s_o = m.sem("recip"), m.sem("recip_gamma"), m.sem("out_ready")
        s_st = [m.sem("stored0"), m.sem("stored1")]
        s_acc_free = m.sem("acc_free")
        block = ctx.enter_context(nc.Block())
        PROJ = 2 * (N // 512)
        VS = TILES // 2
        GR = 4
        MAXS = GR * TILES

        xv = x.rearrange("b (t g p) c -> b t p g c", p=P, g=4)
        ov = x0.rearrange("b (t g p) c -> b t p g c", p=P, g=4)

        @block.sync
        def _(sp):
            for dst, src in ((wq_sb, wqT), (wk_sb, wkT), (wv_sb, wvT)):
                sp.dma_start(dst[:, :, :], src.rearrange("(k p) o -> p k o", p=P)).then_inc(s_w, 16)
            for dst, src in ((bq_sb, bq), (bk_sb, bk), (bv_sb, bv), (gamma_sb, gamma), (ident_sb, ident),
                             (halves_sb, halves)):
                sp.dma_start(dst[:, :], src).then_inc(s_w, 16)
            sp.sem_inc(s_st[0], 16)
            sp.sem_inc(s_st[1], 16)
            for b in range(B):
                if b:
                    sp.wait_ge(s_proj, PROJ * b)
                    sp.wait_ge(s_v, VS * b)
                sp.dma_start(xT_sb[:, :, :], xT[b].rearrange("(k p) n -> p k n", p=P)).then_inc(s_xT, 16)
                for t in range(N // IT):
                    n = b * (N // IT) + t
                    if n >= 2:
                        sp.wait_ge(s_xb, n - 1)
                    sp.dma_start(x_now[:, n % 2, :, :], xv[b, t]).then_inc(s_x[n % 2], 16)
                    if n >= 1:
                        sp.wait_ge(s_o, 4 * n)
                        sp.dma_start(ov[(n - 1) // 8, (n - 1) % 8], out_sb[:, (n - 1) % 2, :, :]).then_inc(s_st[(n - 1) % 2], 16)
            n = B * (N // IT)
            sp.wait_ge(s_o, 4 * n)
            sp.dma_start(ov[B - 1, 7], out_sb[:, (n - 1) % 2, :, :]).then_inc(s_st[(n - 1) % 2], 16)
            for par in range(2):
                sp.wait_ge(s_st[par], 8 * n + 16)

        @block.tensor
        def _(pe):
            pe.sem_inc(s_sc, 2 * JP)
            pe.wait_ge(s_w, 16 * 9)
            pe.wait_ge(s_const, 3)
            with pe.Fori(0, B) as b:
                pe.wait_ge(s_xT, b * 16 + 16)
                pe.wait_ge(s_acc_free, b * 8 + 2)
                for step in range(PROJ):
                    w, t = (wq_sb, wk_sb)[step // 8], step % 8
                    if step >= 6:
                        pe.wait_ge(s_whole, b * PROJ + (step - 5))
                    for kc in range(KC):
                        mm = nc.tensor.matmul(ps[:, step % 6, :], w[:, kc, :], xT_sb[:, kc, t * 512:(t + 1) * 512],
                                              start=(kc == 0), stop=(kc == KC - 1))
                    mm.then_inc(s_proj, 1)

                def values(t):
                    if t >= 2:
                        pe.wait_ge(s_vc, b * VS + (t - 1))
                    for g in range(2):
                        o = ps[:, 6 + t % 2, g * C:(g + 1) * C]
                        tok = (2 * t + g) * P
                        for kc in range(KC):
                            mm = nc.tensor.matmul(o, xT_sb[:, kc, tok:tok + P], wv_sb[:, kc, :], start=(kc == 0), stop=(kc == KC - 1))
                    mm.then_inc(s_v, 1)

                values(0)
                values(1)
                pe.wait_ge(s_whole, b * PROJ + PROJ)
                pe.wait_ge(s_first, b * PROJ + PROJ)
                pe.wait_ge(s_second, b * PROJ + PROJ)
                for it in range(TILES):
                    if it % 2 == 0 and it >= 4:
                        values(it // 2)
                    for g in range(GR):
                        n, tok = GR * it + g, it * P
                        if n >= 3:
                            pe.wait_ge(s_mx_free, b * MAXS + (n - 2))
                        for q_rows, k_rows, rows, first in ((qa, ka, P, True), (qb, kb, LOW, False)):
                            for j in range(2):
                                jj = (2 * g + j) * 512
                                mm = nc.tensor.matmul(ps[:, 2 * (n % 3) + j, :], q_rows[0:rows, tok:tok + P],
                                                      k_rows[0:rows, jj:jj + 512], start=first, stop=not first)
                        mm.then_inc(s_mx, 1)
                pe.wait_ge(s_neg, b + 1)
                pe.wait_ge(s_vc, b * VS + VS)
                for it in range(TILES):
                    mm = nc.tensor.matmul(ps[LOW:LM, it // 4, (it % 4) * P:(it % 4 + 1) * P],
                                          neg3[:, :, it], ident16[:, :], start=True, stop=True)
                mm.then_inc(s_negT, 1)
                with pe.Fori(0, N // IT // 2) as th:
                    pe.wait_ge(s_negrow, b * 2 + 2)
                    for par in range(2):
                        q = b * (N // IT) + th * 2 + par

                        def scores(j):
                            pe.wait_ge(s_pr, q * JP + (j + 1))
                            for r in range(2):
                                tok, bank = (2 * j + r) * P, 2 * (j % 2) + r
                                nc.tensor.matmul(ps[:, bank, :], ka[:, tok:tok + P], q_now[:, par, 0, :], start=True, stop=False)
                                mm = nc.tensor.matmul(ps[:, bank, :], kb[:, tok:tok + P], q_now[0:LM, par, 1, :], start=False, stop=True)
                            mm.then_inc(s_sc, 1)

                        pe.wait_ge(s_qn, q * 2 + 2)
                        scores(0)
                        for j in range(JP):
                            if j + 1 < JP:
                                scores(j + 1)
                            if j == 0:
                                pe.wait_ge(s_acc_free, q + 2)
                            pe.wait_ge(s_pr, q * JP + (j + 3))
                            for r in range(2):
                                jb = 2 * j + r
                                for g in range(4):
                                    mm = nc.tensor.matmul(ps[:, 4 + g, 0:C + 1], probs[:, j % 2, r, g * P:(g + 1) * P],
                                                          v_sb[:, jb, :], start=(jb == 0), stop=(jb == TILES - 1))
                            mm.then_inc(s_pv, 1)

        @block.vector
        def _(dve):
            dve.sem_inc(s_acc_free, 2)
            nc.vector.memset(kb[LOW:LM, :], 1.0).then_inc(s_const, 1)
            nc.vector.memset(v_sb[:, :, C:C + 1], 1.0).then_inc(s_const, 1)
            dve.wait_ge(s_w, 16 * 9)
            nc.vector.tensor_copy(ident16[:, :], ident_sb[:, :]).then_inc(s_const, 1)
            nc.vector.tensor_scalar(gbv[:, :], bv_sb[:, :], gamma_sb[:, 0:1], None, ALU.mult).then_inc(s_const, 1)
            with dve.Fori(0, B) as b:
                dve.wait_ge(s_pv, b * (8 * JP) + 2)

                def second_rows(t):
                    dve.wait_ge(s_mid, b * PROJ + (t + 1))
                    dst, col, at = (qb, kb)[t // 8], 2 + t // 8, (t % 8) * 512
                    nc.vector.scalar_tensor_tensor(dst[0:LOW, at:at + 512], mid[:, t % 2, :], halves_sb[0:LOW, col:col + 1],
                                                   rest[:, t % 2, :], ALU.mult, ALU.add).then_inc(s_second, 1)

                for t in range(PROJ):
                    dve.wait_ge(s_hi, b * PROJ + (t + 1))
                    dst, col, at = (qa, ka)[t // 8], t // 8, (t % 8) * 512
                    nc.vector.scalar_tensor_tensor(dst[:, at:at + 512], hi[:, t % 2, :], halves_sb[:, col:col + 1],
                                                   whole[:, t % 2, :], ALU.mult, ALU.add).then_inc(s_first, 1)
                    if t >= 2:
                        dve.wait_ge(s_second, b * PROJ + (t - 1))
                    nc.vector.scalar_tensor_tensor(rest[:, t % 2, :], hi[0:LOW, t % 2, :], halves_sb[0:LOW, col + 2:col + 3],
                                                   whole[0:LOW, t % 2, :], ALU.mult, ALU.add).then_inc(s_rest, 1)
                    if t >= 1:
                        second_rows(t - 1)
                second_rows(PROJ - 1)
                for n in range(MAXS):
                    dve.wait_ge(s_mx, b * MAXS + (n + 1))
                    bank = 2 * (n % 3)
                    nc.vector.tensor_reduce(part_max[:, n // GR, n % GR:n % GR + 1], ps[:, bank:bank + 2, :],
                                            AX.XY, ALU.max).then_inc(s_mx_free, 1)
                dve.wait_ge(s_mx_free, b * MAXS + MAXS)
                steps = [0]

                def step(ins):
                    steps[0] += 1
                    ins.then_inc(s_pm, 1)
                    dve.wait_ge(s_pm, b * 6 + steps[0])

                step(nc.vector.tensor_reduce(neg_rest[:, 0, :], part_max[:, :, :], AX.X, ALU.max))
                step(nc.vector.tensor_scalar(negmax[:, :], neg_rest[:, 0, :], -1.0, None, ALU.mult))
                step(nc.vector.tensor_copy(neg3[:, 0, :], negmax[:, :]))
                step(nc.vector.tensor_tensor(neg_rest[:, 0, :], negmax[:, :], neg3[:, 0, :], ALU.subtract))
                step(nc.vector.tensor_copy(neg3[:, 1, :], neg_rest[:, 0, :]))
                step(nc.vector.tensor_tensor(neg3[:, 2, :], neg_rest[:, 0, :], neg3[:, 1, :], ALU.subtract))
                dve.sem_inc(s_neg, 1)
                dve.wait_ge(s_negT, b + 1)
                nc.vector.tensor_copy(qb[LOW:LM, N // 2:].rearrange("p (a n) -> p a n", a=4), ps[LOW:LM, 4:8, :]).then_inc(s_negrow, 1)
                with dve.Fori(0, N // IT // 2) as th:
                    for par in range(2):
                        q = b * (N // IT) + th * 2 + par
                        dve.wait_ge(s_pv, q * JP + (JP + 2))
                        dve.wait_ge(s_xb, q + 1)
                        dve.wait_ge(s_st[par], b * 64 + th * 16 + 16)
                        nc.vector.reciprocal(recip[:, :], ps[:, 4:8, C]).then_inc(s_rc, 1)
                        dve.wait_ge(s_rc, q + 1)
                        nc.vector.tensor_scalar(rg[:, :], recip[:, :], gamma_sb[:, 0:1], None, ALU.mult).then_inc(s_rg, 1)
                        dve.wait_ge(s_rg, q + 1)
                        for g in range(4):
                            nc.vector.scalar_tensor_tensor(out_sb[:, par, g, :], ps[:, 4 + g, 0:C], rg[:, g:g + 1],
                                                           xb[:, par, g, :], ALU.mult, ALU.add).then_inc(s_o, 1)
                        dve.wait_ge(s_o, q * 4 + 4)
                        dve.sem_inc(s_acc_free, 1)

        @block.scalar
        def _(act):
            act.wait_ge(s_w, 16 * 9)
            act.sem_inc(s_pr, 2)
            with act.Fori(0, B) as b:
                act.wait_ge(s_pv, b * (8 * JP) + 2)

                def middle(t):
                    act.wait_ge(s_rest, b * PROJ + (t + 1))
                    if t >= 2:
                        act.wait_ge(s_second, b * PROJ + (t - 1))
                    nc.scalar.copy(mid[:, t % 2, :], rest[:, t % 2, :]).then_inc(s_mid, 1)

                for t in range(PROJ):
                    act.wait_ge(s_proj, b * PROJ + (t + 1))
                    if t >= 2:
                        act.wait_ge(s_rest, b * PROJ + (t - 1))
                    bias = (bq_sb, bk_sb)[t // 8]
                    nc.scalar.activation(whole[:, t % 2, :], ps[:, t % 6, :], ACT.Identity, bias=bias[:, 0:1]).then_inc(s_whole, 1)
                    act.wait_ge(s_whole, b * PROJ + (t + 1))
                    nc.scalar.copy(hi[:, t % 2, :], whole[:, t % 2, :]).then_inc(s_hi, 1)
                    if t >= 1:
                        middle(t - 1)
                middle(PROJ - 1)
                for t in range(VS):
                    act.wait_ge(s_v, b * VS + (t + 1))
                    nc.scalar.copy(v_sb[:, 2 * t:2 * t + 2, 0:C], ps[:, 6 + t % 2, :].rearrange("p (g c) -> p g c", g=2)
                                   ).then_inc(s_vc, 1)
                act.wait_ge(s_negT, b + 1)
                nc.scalar.copy(qb[LOW:LM, 0:N // 2].rearrange("p (a n) -> p a n", a=4), ps[LOW:LM, 0:4, :]).then_inc(s_negrow, 1)
                with act.Fori(0, N // IT) as t:
                    for j in range(JP):
                        n = b * (8 * JP) + t * JP + j
                        act.wait_ge(s_sc, n + (1 + 2 * JP))
                        act.wait_ge(s_pv, n + 1)
                        nc.scalar.activation(probs[:, j % 2, :, :], ps[:, 2 * (j % 2):2 * (j % 2) + 2, :], ACT.Exp
                                             ).then_inc(s_pr, 1)

        @block.gpsimd
        def _(pool):
            pool.sem_inc(s_pv, 2)
            with pool.Fori(0, B) as b:
                with pool.Fori(0, N // IT // 2) as th:
                    pool.wait_ge(s_negrow, b * 2 + 2)
                    for par in range(2):
                        q = b * (N // IT) + th * 2 + par
                        pool.wait_ge(s_sc, q * JP + JP)
                        nc.gpsimd.tensor_copy(q_now[:, par, 0, :], qa[:, bass.ds(th * (2 * IT) + par * IT, IT)]).then_inc(s_qn, 1)
                        nc.gpsimd.tensor_copy(q_now[0:LM, par, 1, :], qb[:, bass.ds(th * (2 * IT) + par * IT, IT)]).then_inc(s_qn, 1)
                        pool.wait_ge(s_const, 4)
                        pool.wait_ge(s_x[par], b * 64 + th * 16 + 16)
                        pool.wait_ge(s_acc_free, q + 1)
                        pool.sem_inc(s_passed, 1)
                        nc.gpsimd.tensor_tensor(xb[:, par, :, :], x_now[:, par, :, :],
                                                gbv[:, None, :].broadcast_to([P, 4, C]), ALU.add).then_inc(s_xb, 1)


FR, FL = W // 2 + 1, W // 4 + 1
Z1, Z2 = 2 * FR, 2 * FL
HC = C // 2


def fourier_conv(nc, x0, w1T, bn1, fuT, bnf, lfuT, bnl, w2T, dft, dftl, idft, idftl, ident, rms1, x1, xn):
    HT = TILES // 2
    with ExitStack() as ctx:
        m = Pool_(nc, ctx, "fc")
        w1_sb, w2_sb = m.sb("w1", [P, KC, HC]), m.sb("w2", [HC, C])
        fu_sb, lfu_sb = m.sb("fu", [HC, 2, C]), m.sb("lfu", [HC, 2, C])
        NB = HC + 2 * C
        bn_sb = m.sb("bn", [P, 4, NB])
        scale, shift = m.sb("scale", [P, NB]), m.sb("shift", [P, NB])
        bn1_col, shift_col = m.sb("bncol", [HC, 4]), m.sb("shiftcol", [HC, 4])
        dft_sb, dftl_sb = m.sb("dft", [P, 2 * Z1]), m.sb("dftl", [P, 2, 2 * Z2])
        idft_sb, idftl_sb = m.sb("idft", [Z1, 2, P]), m.sb("idftl", [Z2, 2, P])
        ident_sb, ones_row, rms_sb = m.sb("ident", [P, P]), m.sb("ones", [1, P]), m.sb("rms", [P, KC])
        xin = m.sb("xin", [P, 2, 2, C])
        xt_sb = m.sb("xt", [P, KC, 2, P])
        y_sb, yt_sb = m.sb("y", [P, 2, HC]), m.sb("yt", [HC, 2, P])
        f_sb, fl_sb = m.sb("f", [HC, 2, 2 * Z1]), m.sb("fl", [P, 2 * Z2])
        z_sb, zl_sb = m.sb("z", [Z1, 2, C]), m.sb("zl", [Z2, C])
        s_sb = m.sb("s", [HC, 2, P])
        x1_sb = m.sb("x1", [P, 2, 2, C])
        sq = m.sb("sq", [P, 2, C])
        ss, ms, rt, rstd = (m.sb(k, [P, 2]) for k in ("ss", "ms", "rt", "rstd"))
        xs_sb = m.sb("xs", [P, 2, C])
        xn_sb = m.sb("xn", [P, 2, 4, KC, 2, P])
        pT, pY, pYT, pF, pZ, pZL, pO, pX = (m.ps(k, [P, 512]) for k in ("T", "Y", "YT", "F", "Z", "ZL", "O", "X"))

        s_w, s_fold, s_fsc = m.sem("weights"), m.sem("bn_step"), m.sem("bn_sqrt")
        s_ready, s_passed = m.sem("weights_scaled"), m.sem("pool_passed")
        s_xnfree = m.sem("xn_free")
        s_in, s_x1st, s_xnst = ([m.sem(f"{k}{i}") for i in range(2)] for k in ("xin", "x1_stored", "xn_stored"))
        names = ["xt_ps", "xt", "y_ps", "y", "yt_ps", "yt", "f_ps", "f", "fl", "z_ps", "z", "zl_ps", "zl", "o_ps", "s",
                 "x1_ps", "x1", "ss", "ms", "rt", "rstd", "xs", "xnt_ps", "xn0", "xn1", "xn23"]
        S = {k: m.sem(k) for k in names}
        block = ctx.enter_context(nc.Block())
        NW = 14

        x0v = x0.rearrange("b (k t p) c -> p b t k c", p=P, k=2)
        x1v = x1.rearrange("b (k t p) c -> p b t k c", p=P, k=2)
        def tiles_of(v, b, a, e):
            return v[:, bass.ds(b, 1), bass.ds(a * 4 + e, 1), :, :].rearrange("p a o k c -> p (a o k) c")

        def order_of(o, b, a, e, t):
            chunk = a + t * (CHUNKS // 2) if o < 2 else a * -1 + (CHUNKS // 2 - 1 + t * (CHUNKS // 2))
            at = e * P if o < 2 else (3 - e) * P
            return xn[bass.ds(b + o * B, 1), bass.ds(chunk, 1), :, :, at:at + P].rearrange("s h p k n -> p (s h k) n")

        @block.sync
        def _(sp):
            sp.dma_start(w1_sb[:, :, :], w1T.rearrange("(k p) o -> p k o", p=P)).then_inc(s_w, 16)
            for dst, src in ((w2_sb, w2T), (fu_sb, fuT), (lfu_sb, lfuT), (bn1_col, bn1[0]), (dft_sb, dft),
                             (dftl_sb, dftl), (idft_sb, idft), (idftl_sb, idftl), (ident_sb, ident), (rms_sb, rms1)):
                sl = tuple(slice(None) for _ in src.shape)
                sp.dma_start(dst[sl], src).then_inc(s_w, 16)
            at = 0
            for src in (bn1[1], bnf, bnl):
                n = src.shape[1]
                sp.dma_start(bn_sb[:, :, at:at + n], src[None, :, :].broadcast_to([P, 4, n])).then_inc(s_w, 16)
                at += n
            for i in range(2):
                sp.sem_inc(s_x1st[i], 16)
                sp.sem_inc(s_xnfree, 1)
            sp.sem_inc(S["xt"], 2)
            with sp.Fori(0, B) as b:
                with sp.Fori(0, HT // 4) as a:
                    for e in range(4):
                        par = e % 2
                        u = b * HT + a * 4 + e
                        v = b * (HT // 2) + a * 2 + e // 2
                        sp.wait_ge(S["xt"], u + 1)
                        sp.dma_start(xin[:, par, :, :], tiles_of(x0v, b, a, e)).then_inc(s_in[par], 16)
            for i in range(2):
                sp.wait_ge(s_x1st[i], 16 + 16 * B * HT // 2)
                sp.wait_ge(s_xnst[i], 128 * B * HT // 2)

        @block.gpsimd
        def _(pool):
            with pool.Fori(0, B) as b:
                with pool.Fori(0, HT // 4) as a:
                    for e in range(4):
                        par = e % 2
                        u = b * HT + a * 4 + e
                        v = b * (HT // 2) + a * 2 + e // 2
                        pool.wait_ge(S["xn0"], u * 2 + 4)
                        pool.wait_ge(S["xn1"], u + 1)
                        pool.sem_inc(s_passed, 1)
                        for o in range(2):
                            nc.gpsimd.tensor_copy(xn_sb[:, par, 2 + o, :, :, :],
                                                  xn_sb[:, par, 1 - o, :, ::-1, ::-1]).then_inc(S["xn23"], 1)
                        for o in range(2):
                            for t in range(2):
                                pool.dma_start(order_of(o, b, a, e, t), xn_sb[:, par, o, :, t, :]).then_inc(s_xnst[par], 16)
                        pool.wait_ge(S["xn23"], u * 2 + 2)
                        for o in range(2, 4):
                            for t in range(2):
                                pool.dma_start(order_of(o, b, a, e, t), xn_sb[:, par, o, :, t, :]).then_inc(s_xnst[par], 16)
                        pool.wait_ge(s_xnst[par], v * 128 + 128)
                        pool.sem_inc(s_xnfree, 1)

        @block.scalar
        def _(act):
            act.wait_ge(s_fold, 2)
            nc.scalar.activation(scale[:, :], bn_sb[:, 3, :], ACT.Sqrt).then_inc(s_fsc, 1)
            nc.scalar.activation(shift_col[:, 0:1], bn1_col[:, 3:4], ACT.Sqrt).then_inc(s_fsc, 1)

            with act.Fori(0, B) as b:
                with act.Fori(0, HT // 4) as a:
                    for e in range(4):
                        par = e % 2
                        u = b * HT + a * 4 + e
                        v = b * (HT // 2) + a * 2 + e // 2
                        act.wait_ge(S["xt_ps"], u + 1)
                        nc.scalar.copy(xt_sb[:, :, :, :], pT[:, :].rearrange("p (k t n) -> p k t n", k=KC, t=2)
                                       ).then_inc(S["xt"], 1)
                        act.wait_ge(S["yt_ps"], u + 1)
                        act.wait_ge(S["y_ps"], u + 1)
                        nc.scalar.activation(yt_sb[:, :, :], pYT[:, 0:256].rearrange("p (t n) -> p t n", t=2), ACT.Relu,
                                             bias=shift_col[:, 3:4]).then_inc(S["yt"], 1)
                        act.wait_ge(S["f_ps"], u + 1)
                        nc.scalar.copy(f_sb[:, :, :], pF[:, 0:4 * Z1].rearrange("p (t n) -> p t n", t=2)).then_inc(S["f"], 1)
                        act.wait_ge(S["z_ps"], u + 1)
                        nc.scalar.activation(z_sb[:, :, :], pZ[0:Z1, :].rearrange("p (t n) -> p t n", t=2), ACT.Relu
                                             ).then_inc(S["z"], 1)
                        act.wait_ge(S["x1_ps"], u + 1)
                        act.wait_ge(s_x1st[par], v * 16 + 16)
                        nc.scalar.copy(x1_sb[:, par, :, :], pX[:, :].rearrange("p (t n) -> p t n", t=2)).then_inc(S["x1"], 1)
                        for t in range(2):
                            nc.scalar.activation(sq[:, t, :], pX[:, t * C:(t + 1) * C], ACT.Square,
                                                 accum_out=ss[:, t:t + 1]).then_inc(S["ss"], 1)
                        act.wait_ge(S["ms"], u + 1)
                        nc.scalar.activation(rt[:, :], ms[:, :], ACT.Sqrt).then_inc(S["rt"], 1)
                        act.wait_ge(S["xnt_ps"], u + 1)
                        act.wait_ge(s_xnfree, u + 1)
                        pv = pT[:, :].rearrange("p (k t n) -> p k t n", k=KC, t=2)
                        for kc in range(KC):
                            nc.scalar.activation(xn_sb[:, par, 0, kc, :, :], pv[:, kc, :, :], ACT.Copy,
                                                 scale=rms_sb[:, kc:kc + 1]).then_inc(S["xn0"], 1)
                        act.wait_ge(S["x1"], u + 1)
                        act.dma_start(tiles_of(x1v, b, a, e), x1_sb[:, par, :, :]).then_inc(s_x1st[par], 16)

        @block.vector
        def _(dve):
            done = [0]

            def step(ins):
                done[0] += 1
                ins.then_inc(s_fold, 1)
                dve.wait_ge(s_fold, done[0])

            nc.vector.memset(ones_row[:, :], 1.0).then_inc(s_ready, 1)
            dve.wait_ge(s_w, 16 * NW)
            nc.vector.tensor_scalar(bn1_col[:, 3:4], bn1_col[:, 3:4], 1e-3, None, ALU.add).then_inc(s_fold, 1)
            done[0] += 1
            step(nc.vector.tensor_scalar(bn_sb[:, 3, :], bn_sb[:, 3, :], 1e-3, None, ALU.add))
            dve.wait_ge(s_fsc, 2)
            step(nc.vector.reciprocal(scale[:, :], scale[:, :]))
            step(nc.vector.tensor_tensor(scale[:, :], scale[:, :], bn_sb[:, 0, :], ALU.mult))
            step(nc.vector.tensor_tensor(shift[:, :], scale[:, :], bn_sb[:, 2, :], ALU.mult))
            step(nc.vector.tensor_tensor(shift[:, :], bn_sb[:, 1, :], shift[:, :], ALU.subtract))
            step(nc.vector.reciprocal(shift_col[:, 1:2], shift_col[:, 0:1]))
            step(nc.vector.tensor_tensor(shift_col[:, 2:3], shift_col[:, 1:2], bn1_col[:, 0:1], ALU.mult))
            step(nc.vector.tensor_tensor(shift_col[:, 0:1], shift_col[:, 2:3], bn1_col[:, 2:3], ALU.mult))
            step(nc.vector.tensor_tensor(shift_col[:, 3:4], bn1_col[:, 1:2], shift_col[:, 0:1], ALU.subtract))
            for w, at, n in ((w1_sb, 0, HC), (fu_sb, HC, C), (lfu_sb, HC + C, C)):
                for k in range(2):
                    nc.vector.tensor_tensor(w[:, k, :], w[:, k, :], scale[:, at:at + n], ALU.mult).then_inc(s_ready, 1)
            with dve.Fori(0, B) as b:
                with dve.Fori(0, HT // 4) as a:
                    for e in range(4):
                        par = e % 2
                        u = b * HT + a * 4 + e
                        v = b * (HT // 2) + a * 2 + e // 2
                        dve.wait_ge(S["y_ps"], u + 1)
                        nc.vector.tensor_scalar(y_sb[:, :, :], pY[:, 0:256].rearrange("p (t n) -> p t n", t=2), 0.0, None,
                                                ALU.max).then_inc(S["y"], 1)
                        dve.wait_ge(S["f_ps"], u + 1)
                        nc.vector.tensor_copy(fl_sb[:, :], pZL[:, C:C + 2 * Z2]).then_inc(S["fl"], 1)
                        dve.wait_ge(S["zl_ps"], u + 1)
                        nc.vector.tensor_scalar(zl_sb[:, :], pZL[0:Z2, 0:C], 0.0, None, ALU.max).then_inc(S["zl"], 1)
                        dve.wait_ge(S["o_ps"], u + 1)
                        dve.wait_ge(S["yt"], u + 1)
                        nc.vector.tensor_tensor(s_sb[:, :, :], yt_sb[:, :, :], pO[:, 0:256].rearrange("p (t n) -> p t n", t=2),
                                                ALU.add).then_inc(S["s"], 1)
                        dve.wait_ge(S["ss"], u * 2 + 2)
                        nc.vector.tensor_scalar(ms[:, :], ss[:, :], 1.0 / C, 1e-5, ALU.mult, ALU.add).then_inc(S["ms"], 1)
                        dve.wait_ge(S["rt"], u + 1)
                        nc.vector.reciprocal(rstd[:, :], rt[:, :]).then_inc(S["rstd"], 1)
                        dve.wait_ge(S["rstd"], u + 1)
                        dve.wait_ge(S["x1"], u + 1)
                        for t in range(2):
                            nc.vector.tensor_scalar(xs_sb[:, t, :], x1_sb[:, par, t, :], rstd[:, t:t + 1], None, ALU.mult
                                                    ).then_inc(S["xs"], 1)
                        dve.wait_ge(S["xn0"], u * 2 + 4)
                        nc.vector.tensor_copy(xn_sb[:, par, 1, :, :, :].rearrange("p k t (h n) -> p (k t h) n", n=W),
                                              xn_sb[:, par, 0, :, :, :].rearrange("p k t (h n) -> p (k t h) n", n=W)[:, :, ::-1]
                                              ).then_inc(S["xn1"], 1)

        @block.tensor
        def _(pe):
            pe.wait_ge(s_w, 16 * NW)
            pe.wait_ge(s_ready, 7)
            pe.sem_inc(S["xn0"], 2)
            with pe.Fori(0, B) as b:
                with pe.Fori(0, HT // 4) as a:
                    for e in range(4):
                        par = e % 2
                        u = b * HT + a * 4 + e
                        v = b * (HT // 2) + a * 2 + e // 2
                        pe.wait_ge(s_in[par], v * 16 + 16)
                        pe.wait_ge(S["xn0"], u * 2 + 2)
                        for kc in range(KC):
                            for t in range(2):
                                at = (2 * kc + t) * P
                                mm = nc.tensor.transpose(pT[:, at:at + P], xin[:, par, t, kc * P:(kc + 1) * P], ident_sb[:, :])
                        mm.then_inc(S["xt_ps"], 1)
                        pe.wait_ge(S["xt"], u + 3)
                        for t in range(2):
                            o = pY[:, t * HC:(t + 1) * HC]
                            for kc in range(KC):
                                nc.tensor.matmul(o, xt_sb[:, kc, t, :], w1_sb[:, kc, :], start=(kc == 0), stop=False)
                            mm = nc.tensor.matmul(o, ones_row[:, :], shift[0:1, 0:HC], start=False, stop=True)
                        mm.then_inc(S["y_ps"], 1)
                        for kc in range(KC):
                            mm = nc.tensor.matmul(pYT[:, 0:256].rearrange("p (t n) -> p t n", t=2), w1_sb[:, kc, :], xt_sb[:, kc, :, :],
                                                  start=(kc == 0), stop=(kc == KC - 1))
                        mm.then_inc(S["yt_ps"], 1)
                        pe.wait_ge(S["y"], u + 1)
                        for t in range(2):
                            nc.tensor.matmul(pF[:, t * 2 * Z1:(t + 1) * 2 * Z1], y_sb[:, t, :], dft_sb[:, :], start=True, stop=True)
                        for wq in range(2):
                            for hq in range(2):
                                r = 64 * wq + 32 * hq
                                mm = nc.tensor.matmul(pZL[r:r + HC // 4, C:C + 2 * Z2], y_sb[:, hq, 0:HC // 4],
                                                      dftl_sb[:, wq, :], start=True, stop=True)
                        mm.then_inc(S["f_ps"], 1)
                        pe.wait_ge(S["f"], u + 1)
                        for t in range(2):
                            o = pZ[0:Z1, t * C:(t + 1) * C]
                            for ri in range(2):
                                nc.tensor.matmul(o, f_sb[:, t, ri * Z1:(ri + 1) * Z1], fu_sb[:, ri, :], start=(ri == 0), stop=False)
                            mm = nc.tensor.matmul(o, ones_row[:, 0:Z1], shift[0:1, HC:HC + C], start=False, stop=True)
                        mm.then_inc(S["z_ps"], 1)
                        pe.wait_ge(S["fl"], u + 1)
                        for ri in range(2):
                            nc.tensor.matmul(pZL[0:Z2, 0:C], fl_sb[:, ri * Z2:(ri + 1) * Z2], lfu_sb[:, ri, :], start=(ri == 0), stop=False)
                        nc.tensor.matmul(pZL[0:Z2, 0:C], ones_row[:, 0:Z2], shift[0:1, HC + C:HC + 2 * C], start=False, stop=True
                                         ).then_inc(S["zl_ps"], 1)
                        pe.wait_ge(S["z"], u + 1)
                        pe.wait_ge(S["zl"], u + 1)
                        for t in range(2):
                            o = pO[:, t * P:(t + 1) * P]
                            for ri in range(2):
                                nc.tensor.matmul(o, z_sb[:, t, ri * HC:(ri + 1) * HC], idft_sb[:, ri, :], start=(ri == 0), stop=False)
                            for ri in range(2):
                                mm = nc.tensor.matmul(o, zl_sb[:, ri * HC:(ri + 1) * HC], idftl_sb[:, ri, :], start=False, stop=(ri == 1))
                        mm.then_inc(S["o_ps"], 1)
                        pe.wait_ge(S["s"], u + 1)
                        for t in range(2):
                            mm = nc.tensor.matmul(pX[:, t * C:(t + 1) * C], s_sb[:, t, :], w2_sb[:, :], start=True, stop=True)
                        mm.then_inc(S["x1_ps"], 1)
                        pe.wait_ge(S["xs"], u * 2 + 2)
                        for kc in range(KC):
                            for t in range(2):
                                at = (2 * kc + t) * P
                                mm = nc.tensor.transpose(pT[:, at:at + P], xs_sb[:, t, kc * P:(kc + 1) * P], ident_sb[:, :])
                        mm.then_inc(S["xnt_ps"], 1)


def mamba(nc, xn, w_inT, conv_w, conv_b, w_xT, split, w_dtT, b_dt, a_log, d_skip, w_outT, ident, pick, keep, out):
    NC = SEQS * CHUNKS
    STEPS = 2 * NS
    BCR = 96
    HS0, CONV0, OUT0, XP, GATE_A, DT0, GATE_B = 0, 4, 8, 10, 11, 12, 16
    G, GO = 19, 2
    FIRST = G - GO
    PIECES = {g: at for g, at in ([(HS0 + i, (i, 1)) for i in range(4)] + [(CONV0 + i, (4 + 2 * i, 2)) for i in range(4)]
                                  + [(OUT0 + i, (12 + 2 * i, 2)) for i in range(2)] + [(XP, (16, 2)), (GATE_A, (18, 1))]
                                  + [(DT0 + i, (19 + i, 1)) for i in range(4)] + [(GATE_B + i, (23 + 2 * i, 2)) for i in range(3)])}
    SILU_GATE_AT, SILU_AT, LN_AT, READ_AT = 8, 13, 24, 2
    DU_LATE_AT, DU_AT = 4, 25
    AHEAD, CARRY_LAG = 2, 2

    def count(c, g):
        if isinstance(c, int) and c == 0:
            return FIRST + (g if g <= OUT0 else g - GO)
        return c * G + (g + 2 * FIRST - G)

    def issue_order(first, last):
        return [(at + i, g, i, n) for g, (at, n) in PIECES.items() for i in range(n)
                if not (first and OUT0 <= g < OUT0 + GO) and not (last and not OUT0 <= g < OUT0 + GO)]

    with ExitStack() as ctx:
        m = Pool_(nc, ctx, "mm")
        w_in = m.sb("w_in", [P, KC, 2 * I])
        taps, cw = m.sb("taps", [P, IB * TAPS, P]), m.sb("cw", [P, IB * TAPS])
        w_x, w_dt, w_out = m.sb("w_x", [P, IB, BCR + RK]), m.sb("w_dt", [P, I]), m.sb("w_out", [P, IB, C])
        cb_sb, bdt_sb, d_sb, ab_sb = m.sb("cb", [P, IB]), m.sb("bdt", [P, IB]), m.sb("d", [P, IB]), m.sb("ab", [P, 2])
        alog, a_sb = m.sb("alog", [P, IB * NS]), m.sb("a", [P, IB * NS])
        ident_sb, keep_sb = m.sb("ident", [P, P]), m.sb("keep", [P, NC + 1])
        keep_now = m.sb("keep_now", [P, 2])
        pick_sb = m.sb("pick", [BCR, 2 * NS, P], BF16)
        xn_sb = m.sb("xn", [P, 2, KC, T])
        hs = m.sb("hs", [P, IB, TAPS - 1 + T])
        u, gate = m.sb("u", [P, 2, IB, T]), m.sb("gate", [P, 2, IB, T])
        hi, mid, parts = m.sb("hi", [BCR, T], BF16), m.sb("mid", [BCR, T], BF16), m.sb("parts", [BCR, 2, T], BF16)
        rest = m.sb("rest", [BCR + RK, T])
        sp_e = m.sb("sp_e", [P, IB, T])
        dt, du = m.sb("dt", [P, 2, IB, T]), m.sb("du", [P, 2, IB, T])
        da = m.sb("da", [P, 4, 2, T])
        c_sb, bu, h, hc = m.sb("c", [P, 4, T]), m.sb("bu", [P, 4, 2, T]), m.sb("h", [P, 4, 2, T]), m.sb("hc", [P, 2, 2, T])
        carry = m.sb("carry", [P, 2, STEPS, 2])
        yg, out_sb = m.sb("yg", [P, IB, T]), m.sb("out", [P, 2, 2, C])
        p_b, p_c = m.ps("b", [P, 2, T]), m.ps("c", [P, 2, T])
        p_y, p_w = m.ps("y", [P, 2, T]), m.ps("w", [P, 2, T])

        s_w, s_prep, s_a, s_taps = m.sem("weights"), m.sem("a_exp"), m.sem("a"), m.sem("taps")
        s_zero = m.sem("zeroed")
        s_xn, s_st = ([m.sem(f"{k}{i}") for i in range(2)] for k in ("xn", "stored"))
        s_wk, s_wkf = m.sem("work_group"), m.sem("work_emptied")
        s_xpf, s_silu_gate = m.sem("bc_read"), m.sem("silu_gate")
        s_silu, s_parts, s_hi, s_softplus = m.sem("silu"), m.sem("parts"), m.sem("hi"), m.sem("softplus")
        s_tail, s_keep, s_sp1 = m.sem("tail"), m.sem("keep"), m.sem("softplus_exp")
        s_dt, s_du = m.sem("dt"), m.sem("du")
        s_bb, s_cb, s_cc, s_da = m.sem("b_spread"), m.sem("c_spread"), m.sem("c_copied"), m.sem("da")
        s_bu, s_scan, s_carry, s_hc, s_ys = m.sem("bu"), m.sem("scanned"), m.sem("carried"), m.sem("hc"), m.sem("y_added")
        s_yev, s_yg = m.sem("y_read"), m.sem("yg")
        block = ctx.enter_context(nc.Block())

        xnf = xn.rearrange("s h p k t -> p (s h) k t")
        outf = out.rearrange("s (h g p) c -> p (s h) g c", p=P, g=4)
        LOADS = ((w_in, w_inT.rearrange("(k p) o -> p k o", p=P)), (cw, conv_w), (w_x, w_xT.rearrange("(k p) o -> p k o", p=P)),
                 (w_out, w_outT.rearrange("(k p) o -> p k o", p=P)), (cb_sb, conv_b), (bdt_sb, b_dt), (d_sb, d_skip),
                 (ab_sb, split), (alog, a_log), (ident_sb, ident), (keep_sb, keep))

        NLOADS = len(LOADS) + 3

        def every_chunk(eng, body):
            body(0, 0, 0, True, False)
            with eng.Fori(0, (NC - 2) // 2) as i:
                body(i * 2 + 1, 1, i, False, False)
                body(i * 2 + 2, 0, i + 1, False, False)
            body(NC - 1, 1, NC // 2 - 1, False, True)

        def at_least(eng, sem, v):
            if not isinstance(v, int) or v > 0:
                eng.wait_ge(sem, v)

        @block.sync
        def _(sp):
            for dst, src in LOADS:
                sl = tuple(slice(None) for _ in src.shape)
                sp.dma_start(dst[sl], src).then_inc(s_w, 16)
            sp.dma_start(w_dt[BCR:BCR + RK, :], w_dtT).then_inc(s_w, 16)
            for i in range(2):
                sp.dma_start(du[0:BCR, i, :, :].rearrange("p a n -> p (a n)"), pick[:, i * NS:(i + 1) * NS, :].rearrange("p a n -> p (a n)")
                             ).then_inc(s_w, 16)
            for i in range(2):
                sp.sem_inc(s_st[i], 16)

            def load(c, par):
                src = xnf[:, bass.ds(c, 1), :, :].rearrange("p s k t -> p (s k) t")
                sp.dma_start(xn_sb[:, par, :, :], src).then_inc(s_xn[par], 16)

            def store(c):
                for g in range(2):
                    sp.wait_ge(s_wkf, count(NC - 1, 0) + (GO + g + 1) if isinstance(c, int) and c == NC - 1 else
                               count(NC - 1, 0) + (g + 1) if isinstance(c, int) and c == NC - 2 else count(c + 1, OUT0 + g + 1))
                    dst = outf[:, bass.ds(c, 1), 2 * g:2 * g + 2, :].rearrange("p s g c -> p (s g) c")
                    sp.dma_start(dst, out_sb[:, g, :, :]).then_inc(s_st[g], 16)

            load(0, 0)
            load(1, 1)
            sp.wait_ge(s_wk, FIRST)
            load(2, 0)
            sp.wait_ge(s_wk, count(0, G))
            load(3, 1)
            with sp.Fori(0, (NC - 4) // 2) as i:
                for j in range(2):
                    c = i * 2 + (1 + j)
                    store(i * 2 + j)
                    sp.wait_ge(s_wk, count(c, G))
                    load(i * 2 + (4 + j), j)
            for c in range(NC - 4, NC):
                store(c)
            for g in range(2):
                sp.wait_ge(s_st[g], 16 + 16 * NC)

        @block.tensor
        def _(pe):
            pe.wait_ge(s_w, 16 * NLOADS)
            pe.wait_ge(s_taps, IB * TAPS + 2)

            def wait_bank(c, g):
                if c is None:
                    n = g if g < OUT0 else g - GO
                    if n >= 2:
                        pe.wait_ge(s_wkf, n - 1)
                    if g >= XP + 2:
                        pe.wait_ge(s_xpf, 1)
                elif isinstance(c, int) and c == NC - 1:
                    pe.wait_ge(s_wkf, count(c, 0))
                else:
                    first = isinstance(c, int) and c == 0
                    n = count(c, 0) if g < 2 else count(c, OUT0) if first and g in (XP, XP + 1) else count(c, g - 2) + 1
                    pe.wait_ge(s_wkf, n)
                    if g >= XP + 2:
                        pe.wait_ge(s_xpf, c + 2)

            def products(c, pn, half, g):
                w = p_w[:, g % 2, :]
                if g < CONV0 or g == GATE_A or g >= GATE_B:
                    o = g if g < CONV0 else IB if g == GATE_A else IB + 1 + (g - GATE_B)
                    if g == 0:
                        pe.wait_ge(s_xn[pn], half * 16 + 16)
                    return [(w, w_in[:, kc, o * P:(o + 1) * P], xn_sb[:, pn, kc, :], kc == 0, kc == KC - 1) for kc in range(KC)]
                if g < OUT0:
                    cb = g - CONV0
                    if c is None:
                        pe.wait_ge(s_wkf, cb + 1)
                    else:
                        pe.wait_ge(s_wkf, count(c, cb) + 1)
                    return [(w, taps[:, cb * TAPS + k, :], hs[:, cb, k:k + T], k == 0, k == TAPS - 1) for k in range(TAPS)]
                if g < XP:
                    pe.wait_ge(s_yg, c * IB)
                    return [(w[:, t * C:(t + 1) * C], yg[:, cb, (2 * (g - OUT0) + t) * P:(2 * (g - OUT0) + t + 1) * P],
                             w_out[:, cb, :], cb == 0, cb == IB - 1) for t in range(2) for cb in range(IB)]
                if g == XP:
                    pe.wait_ge(s_silu, 1 if c is None else c + 2)
                    return [(w[0:BCR + RK, :], w_x[:, cb, :], u[:, pn, cb, :], cb == 0, cb == IB - 1) for cb in range(IB)]
                if g == DT0:
                    pe.wait_ge(s_wkf, XP - GO + 1 if c is None else count(c, XP) + 1)
                cb = g - DT0
                return [(w, w_dt[BCR:BCR + RK, cb * P:(cb + 1) * P], rest[BCR:BCR + RK, :], True, True)]

            def piece(c, pn, half, g, i, n):
                if i == 0:
                    wait_bank(c, g)
                todo = products(c, pn, half, g)
                per = len(todo) // n
                for o, a, b, start, stop in todo[i * per:(i + 1) * per]:
                    mm = nc.tensor.matmul(o, a, b, start=start, stop=stop)
                if i == n - 1:
                    mm.then_inc(s_wk, 1)

            def spread(c, p, k):
                K = c * STEPS + k
                n = k % NS
                if k == 0:
                    pe.wait_ge(s_parts, c + 1)
                pe.wait_ge(s_bu, K + 1)
                nc.tensor.matmul(p_b[:, k % 2, :], pick_sb[:, n, :], parts[:, p, :], start=True, stop=True).then_inc(s_bb, 1)
                pe.wait_ge(s_cc, K + 1)
                nc.tensor.matmul(p_c[:, k % 2, :], pick_sb[:, NS + n, :], parts[:, p, :], start=True, stop=True).then_inc(s_cb, 1)

            def add_y(c, k):
                K = c * STEPS + k
                if k % NS == 0:
                    pe.wait_ge(s_yev, c * 4 + (2 * (k // NS) + 2))
                pe.wait_ge(s_hc, K + 3)
                for j in range(2):
                    mm = nc.tensor.matmul(p_y[:, j, :], ident_sb[:, :], hc[:, k % 2, j, :],
                                          start=(k % NS == 0), stop=(k % NS == NS - 1))
                mm.then_inc(s_ys, 1)

            for g in PIECES:
                if not OUT0 <= g < XP:
                    piece(None, 0, 0, g, 0, 1)
            spread(0, 0, 0)

            def body(c, p, half, first, last):
                nhalf = half + 1 if p == 1 else half
                for k in range(STEPS):
                    if k + 1 < STEPS:
                        spread(c, p, k + 1)
                    elif not last:
                        spread(c + 1, 1 - p, 0)
                    for at, g, i, n in issue_order(first, last):
                        if at == k:
                            piece(c, 1 - p, nhalf, g, i, n)
                    if k >= 2:
                        add_y(c, k - 2)
                    elif not first:
                        add_y(c + -1, STEPS + k - 2)

            every_chunk(pe, body)
            for k in range(2):
                add_y(NC - 1, STEPS + k - 2)
            for g in range(GO):
                pe.wait_ge(s_wkf, count(NC - 1, 0) + GO)
                pe.wait_ge(s_yg, NC * IB)
                for o, a, b, start, stop in products(NC, 0, 0, OUT0 + g):
                    mm = nc.tensor.matmul(o, a, b, start=start, stop=stop)
                mm.then_inc(s_wk, 1)

        @block.scalar
        def _(act):
            act.wait_ge(s_w, 16 * NLOADS)
            act.sem_inc(s_cc, 2)
            nc.scalar.activation(alog[:, :], alog[:, :], ACT.Exp).then_inc(s_prep, 1)
            act.wait_ge(s_prep, 1)
            nc.scalar.mul(a_sb[:, :], alog[:, :], -1.0).then_inc(s_a, 1)
            act.wait_ge(s_a, 1)

            def empty(c, pn, g):
                act.wait_ge(s_wk, (g if g < OUT0 else g - GO) + 1 if c is None else count(c, g) + 1)
                w = p_w[:, g % 2, :]
                if g < CONV0:
                    nc.scalar.copy(hs[:, g, TAPS - 1:], w).then_inc(s_wkf, 1)
                elif g == GATE_A or g >= GATE_B:
                    cb = 0 if g == GATE_A else g - GATE_B + 1
                    nc.scalar.copy(gate[:, pn, cb, :], w).then_inc(s_wkf, 1)
                elif g < OUT0:
                    cb = g - CONV0
                    nc.scalar.activation(u[:, pn, cb, :], w, ACT.Identity, bias=cb_sb[:, cb:cb + 1]).then_inc(s_wkf, 1)
                elif g == XP:
                    nc.scalar.copy(rest[BCR:BCR + RK, :], p_w[BCR:BCR + RK, g % 2, :]).then_inc(s_wkf, 1)
                else:
                    cb = g - DT0
                    if cb == 0 and c is not None:
                        act.wait_ge(s_dt, c * IB + IB)
                    nc.scalar.activation(dt[:, pn, cb, :], w, ACT.Relu, bias=bdt_sb[:, cb:cb + 1])
                    nc.scalar.activation(sp_e[:, cb, :], w, ACT.Abs, bias=bdt_sb[:, cb:cb + 1]).then_inc(s_wkf, 1)

            def empty_output(c, g, n):
                act.wait_ge(s_wk, n + 1)
                act.wait_ge(s_st[g], c * 16 + 16)
                nc.scalar.copy(out_sb[:, g, :, :], p_w[:, g % 2, :].rearrange("p (t n) -> p t n", t=2)).then_inc(s_wkf, 1)

            def tail(c, pn):
                nc.scalar.activation(hs[:, :, 0:TAPS - 1], hs[:, :, T:T + TAPS - 1], ACT.Copy,
                                     scale=keep_now[:, pn:pn + 1]).then_inc(s_tail, 1)
                act.wait_ge(s_tail, c + 1)

            def silu_u(c, pn):
                act.wait_ge(s_wkf, OUT0 if c is None else count(c, OUT0))
                nc.scalar.activation(u[:, pn, :, :], u[:, pn, :, :], ACT.Silu).then_inc(s_silu, 1)

            def silu_gate(c, p):
                act.wait_ge(s_wkf, count(c, 0))
                nc.scalar.activation(gate[:, p, :, :], gate[:, p, :, :], ACT.Silu).then_inc(s_silu_gate, 1)

            def softplus_exp(c, cb):
                act.wait_ge(s_wkf, DT0 - GO + cb + 1 if c is None else count(c, DT0 + cb) + 1)
                nc.scalar.activation(sp_e[:, cb, :], sp_e[:, cb, :], ACT.Exp, scale=-1.0).then_inc(s_sp1, 1)

            def softplus_ln(c):
                act.wait_ge(s_sp1, IB if c is None else c * IB + 2 * IB)
                nc.scalar.activation(sp_e[:, :, :], sp_e[:, :, :], ACT.Ln, bias=1.0).then_inc(s_softplus, 1)

            def copy_c(c, k):
                K = c * STEPS + k
                act.wait_ge(s_cb, K + 1)
                at_least(act, s_hc, K + -1)
                nc.scalar.copy(c_sb[:, k % 4, :], p_c[:, k % 2, :]).then_inc(s_cc, 1)

            def decay(c, p, k):
                K = c * STEPS + k
                if k % NS == 0:
                    act.wait_ge(s_dt, c * IB + (2 if k == 0 else 4))
                at_least(act, s_scan, K * 2 + -4)
                for j in range(2):
                    cb = 2 * (k // NS) + j
                    nc.scalar.activation(da[:, k % 4, j, :], dt[:, p, cb, :], ACT.Exp,
                                         scale=a_sb[:, cb * NS + k % NS:cb * NS + k % NS + 1]).then_inc(s_da, 1)

            def carry_on(c, p, k):
                act.wait_ge(s_scan, (c * STEPS + k) * 2 + 4)
                nc.scalar.activation(carry[:, 1 - p, k, :], h[:, k % 4, :, T - 1], ACT.Copy,
                                     scale=keep_now[:, 1 - p:2 - p]).then_inc(s_carry, 1)

            act.wait_ge(s_zero, 2)
            for g in PIECES:
                if not OUT0 <= g < XP:
                    empty(None, 0, g)
                if g == OUT0 - 1:
                    silu_u(None, 0)
            for cb in range(IB):
                softplus_exp(None, cb)
            softplus_ln(None)
            copy_c(0, 0)
            for k in range(AHEAD):
                decay(0, 0, k)

            def body(c, p, half, first, last):
                nc.scalar.copy(keep_now[:, 1 - p:2 - p], keep_sb[:, bass.ds(c + 1, 1)]).then_inc(s_keep, 1)
                act.wait_ge(s_keep, c + 1)
                for k in range(STEPS):
                    if k + 1 < STEPS:
                        copy_c(c, k + 1)
                    elif not last:
                        copy_c(c + 1, 0)
                    if k + AHEAD < STEPS:
                        decay(c, p, k + AHEAD)
                    elif not last:
                        decay(c + 1, 1 - p, k + AHEAD - STEPS)
                    if k >= CARRY_LAG:
                        carry_on(c, p, k - CARRY_LAG)
                    elif not first:
                        carry_on(c + -1, 1 - p, STEPS + k - CARRY_LAG)
                    if k == 0 and not last:
                        tail(c, 1 - p)
                    for at, g, i, n in issue_order(first, last):
                        if at + 1 == k and i == n - 1:
                            if OUT0 <= g < XP:
                                empty_output(c + -1, g - OUT0, count(c, 0) + (g - OUT0) if last else count(c, g))
                            else:
                                empty(c, 1 - p, g)
                            if DT0 < g < GATE_B:
                                softplus_exp(c, g - DT0 - 1)
                    if k == SILU_GATE_AT:
                        silu_gate(c, p)
                    if not last:
                        if k == SILU_AT:
                            silu_u(c, 1 - p)
                        if k == LN_AT:
                            softplus_exp(c, IB - 1)
                            softplus_ln(c)

            every_chunk(act, body)
            for g in range(GO):
                empty_output(NC - 1, g, count(NC - 1, 0) + (GO + g))

        @block.vector
        def _(dve):
            dve.wait_ge(s_w, 16 * NLOADS)
            for i in range(IB * TAPS):
                nc.vector.tensor_scalar(taps[:, i, :], ident_sb[:, :], cw[:, i:i + 1], None, ALU.mult).then_inc(s_taps, 1)
            for i in range(2):
                nc.vector.tensor_copy(pick_sb[:, i * NS:(i + 1) * NS, :].rearrange("p a n -> p (a n)"),
                                      du[0:BCR, i, :, :].rearrange("p a n -> p (a n)")).then_inc(s_taps, 1)
            nc.vector.memset(hs[:, :, 0:TAPS - 1], 0.0).then_inc(s_zero, 1)
            nc.vector.memset(carry[:, 0, :, :], 0.0).then_inc(s_zero, 1)
            dve.wait_ge(s_zero, 2)
            dve.sem_inc(s_bu, 2)
            dve.sem_inc(s_scan, 2)
            dve.sem_inc(s_yev, 2)
            dve.sem_inc(s_carry, STEPS)

            def split_bc(c, pn):
                dve.wait_ge(s_wk, XP - GO + 1 if c is None else count(c, XP) + 1)
                w = p_w[0:BCR, XP % 2, :]
                nc.vector.tensor_copy(hi[:, :], w).then_inc(s_hi, 1)
                n = 0 if c is None else c * 2 + 2
                dve.wait_ge(s_hi, n + 1)
                nc.vector.scalar_tensor_tensor(rest[0:BCR, :], hi[:, :], ab_sb[0:BCR, 0:1], w, ALU.mult, ALU.add).then_inc(s_xpf, 1)
                dve.wait_ge(s_xpf, 1 if c is None else c + 2)
                nc.vector.tensor_copy(mid[:, :], rest[0:BCR, :]).then_inc(s_hi, 1)
                dve.wait_ge(s_hi, n + 2)
                nc.vector.scalar_tensor_tensor(parts[:, pn, :], mid[:, :], ab_sb[0:BCR, 1:2], rest[0:BCR, :], ALU.mult, ALU.add
                                               ).then_inc(s_parts, 1)

            def times_b(c, p, k):
                K = c * STEPS + k
                if k % NS == 0:
                    dve.wait_ge(s_du, c * IB + (2 if k == 0 else 4))
                q = k // NS
                dve.wait_ge(s_bb, K + 1)
                at_least(dve, s_scan, K * 2 + -4)
                nc.vector.tensor_tensor(bu[:, k % 4, :, :], du[:, p, 2 * q:2 * q + 2, :],
                                        p_b[:, k % 2:k % 2 + 1, :].broadcast_to([P, 2, T]), ALU.mult).then_inc(s_bu, 1)

            def scan(c, p, k):
                K = c * STEPS + k
                dve.wait_ge(s_bu, K + 3)
                dve.wait_ge(s_carry, K + (STEPS - 3))
                at_least(dve, s_hc, K + -1)
                for j in range(2):
                    dve.wait_ge(s_da, K * 2 + (j + 1))
                    nc.vector.tensor_tensor_scan(h[:, k % 4, j, :], da[:, k % 4, j, :], bu[:, k % 4, j, :], carry[:, p, k, j:j + 1],
                                                 ALU.mult, ALU.add).then_inc(s_scan, 1)

            def read_y(c, p, q):
                dve.wait_ge(s_ys, c * STEPS + (NS * (q + 1) + 2))
                if q == 0 and not (isinstance(c, int) and c == 0):
                    dve.wait_ge(s_wk, count(c, 0) + GO if isinstance(c, int) and c == NC - 1 else count(c, XP))
                for j in range(2):
                    cb = 2 * q + j
                    nc.vector.scalar_tensor_tensor(yg[:, cb, :], u[:, p, cb, :], d_sb[:, cb:cb + 1], p_y[:, j, :],
                                                   ALU.mult, ALU.add).then_inc(s_yev, 1)

            split_bc(None, 0)
            times_b(0, 0, 0)

            def body(c, p, half, first, last):
                for k in range(STEPS):
                    if k == READ_AT and not first:
                        read_y(c + -1, 1 - p, 1)
                    if k == NS + READ_AT:
                        read_y(c, p, 0)
                    if k + 1 < STEPS:
                        times_b(c, p, k + 1)
                    elif not last:
                        times_b(c + 1, 1 - p, 0)
                    scan(c, p, k)
                    if k == PIECES[XP][0] + PIECES[XP][1] and not last:
                        split_bc(c, 1 - p)

            every_chunk(dve, body)
            read_y(NC - 1, 1, 1)

        @block.gpsimd
        def _(pool):
            pool.sem_inc(s_hc, 2)
            pool.sem_inc(s_ys, 2)

            def dt_step(c, par, i):
                cb = i // 2
                if i % 2 == 0:
                    pool.wait_ge(s_softplus, c + 1)
                    nc.gpsimd.tensor_tensor(dt[:, par, cb, :], dt[:, par, cb, :], sp_e[:, cb, :], ALU.add).then_inc(s_dt, 1)
                else:
                    pool.wait_ge(s_dt, c * IB + (cb + 1))
                    nc.gpsimd.tensor_tensor(du[:, par, cb, :], dt[:, par, cb, :], u[:, par, cb, :], ALU.mult).then_inc(s_du, 1)

            def times_c(c, k):
                K = c * STEPS + k
                pool.wait_ge(s_scan, K * 2 + 4)
                pool.wait_ge(s_cc, K + 3)
                pool.wait_ge(s_ys, K + 1)
                nc.gpsimd.tensor_tensor(hc[:, k % 2, :, :], h[:, k % 4, :, :],
                                        c_sb[:, k % 4:k % 4 + 1, :].broadcast_to([P, 2, T]), ALU.mult).then_inc(s_hc, 1)

            def gate_y(c, p, q, j):
                pool.wait_ge(s_silu_gate, c + 1)
                pool.wait_ge(s_yev, c * 4 + (2 * q + 4))
                cb = 2 * q + j
                nc.gpsimd.tensor_tensor(yg[:, cb, :], yg[:, cb, :], gate[:, p, cb, :], ALU.mult).then_inc(s_yg, 1)

            for i in range(IB):
                dt_step(0, 0, i)

            def body(c, p, half, first, last):
                for k in range(STEPS):
                    times_c(c, k)
                    for j in range(2):
                        if k == READ_AT + j and not first:
                            gate_y(c + -1, 1 - p, 1, j)
                        if k == NS + READ_AT + j:
                            gate_y(c, p, 0, j)
                    if DU_LATE_AT <= k < DU_LATE_AT + IB:
                        dt_step(c, p, IB + k - DU_LATE_AT)
                    if DU_AT <= k < DU_AT + IB and not last:
                        dt_step(c + 1, 1 - p, k - DU_AT)

            every_chunk(pool, body)
            for j in range(2):
                gate_y(NC - 1, 1, 1, j)


def combine_and_whiten(nc, mix, x1, flips, wf, ln_w, ln_b, ident, blocks, gamma, beta, out):
    NT = B * TILES
    ORD = 4
    ITERS = 26
    ROWS = float(B * N)
    with ExitStack() as outer:
        mo = Pool_(nc, outer, "cw")
        x2 = mo.sb("x2", [P, NT, C])
        ident_sb, ones = mo.sb("ident", [P, P]), mo.sb("ones", [P, P])
        mean_sb = mo.sb("mean", [P, C])
        p_sum = mo.ps("sum", [P, 512])
        with ExitStack() as ctx:
            m = Pool_(nc, ctx, "co")
            flip_sb, wf_sb, wf4 = m.sb("flips", [P, ORD - 1, P]), m.sb("wf", [P, C]), m.sb("wf4", [P, C])
            lw_sb, lb_sb = m.sb("lw", [P, C]), m.sb("lb", [P, C])
            xo = m.sb("xo", [P, 4, ORD + 1, C])
            h0, acc, y = m.sb("h0", [P, 2, C]), m.sb("acc", [P, 4, C]), m.sb("y", [P, 4, C])
            sq, ss, ms, rt, rs = (m.sb(k, [P, 4, 4] if k != "sq" else [P, 4, C]) for k in ("sq", "ss", "ms", "rt", "rs"))
            stats, mv = m.sb("stats", [P, 4, 6]), m.sb("mv", [P, 4, 2])
            ve, rt2, rs2, cen = m.sb("ve", [P, 4]), m.sb("rt2", [P, 4]), m.sb("rs2", [P, 4]), m.sb("cen", [P, 2, C])
            p_h = m.ps("h", [P, 2, 4, C])

            s_w, s_prep, s_passed = m.sem("weights"), m.sem("prepared"), m.sem("dve_passed")
            s_in = [m.sem(f"loaded{i}") for i in range(4)]
            s_g, s_h0, s_ss, s_ms, s_rt, s_rs = (m.sem(k) for k in ("h_summed", "h0", "squares", "ms", "root", "recip"))
            s_acc, s_y, s_bn, s_mv, s_ve = (m.sem(k) for k in ("acc", "y", "stats", "mean_var", "var_eps"))
            s_rt2, s_rs2, s_cen, s_x2, s_sum = (m.sem(k) for k in ("root2", "recip2", "centred", "x2", "summed"))
            block = ctx.enter_context(nc.Block())

            mv_dram = mix.rearrange("(o b) (t p) c -> p o (b t) c", p=P, b=B)
            x1_dram = x1.rearrange("b (t p) c -> p (b t) c", p=P)
            LOADS = ((flip_sb, flips), (wf_sb, wf), (lw_sb, ln_w), (lb_sb, ln_b), (ident_sb, ident))

            def every_tile(body):
                def run(eng):
                    body(0, 0, 0)
                    body(1, 1, 0)
                    with eng.Fori(0, (NT - 4) // 4) as i:
                        for j in range(4):
                            body(i * 4 + (2 + j), (2 + j) % 4, i + (2 + j) // 4)
                    body(NT - 2, 2, NT // 4 - 1)
                    body(NT - 1, 3, NT // 4 - 1)
                return run

            def inside(n, lo, hi):
                return not isinstance(n, int) or (n - lo >= 0 and n + hi < NT)

            @block.sync
            def _(sp):
                for dst, src in LOADS:
                    sl = tuple(slice(None) for _ in src.shape)
                    sp.dma_start(dst[sl], src).then_inc(s_w, 16)
                sp.sem_inc(s_g, 4)
                sp.sem_inc(s_h0, 4)
                with sp.Fori(0, B) as b:
                    with sp.Fori(0, TILES // 4) as i:
                        for j in range(4):
                            n = b * TILES + i * 4 + j
                            back = b * TILES + i * -4 + (TILES - 1 - j)
                            sp.wait_ge(s_g, n + 1)
                            sp.wait_ge(s_h0, n + 1)
                            for o, t in ((0, n), (2, back)):
                                sp.dma_start(xo[:, j, o:o + 2, :], mv_dram[:, o:o + 2, bass.ds(t, 1), :].rearrange("p o t c -> p o (t c)")
                                             ).then_inc(s_in[j], 16)
                            sp.dma_start(xo[:, j, 4, :], x1_dram[:, bass.ds(n, 1), :].rearrange("p t c -> p (t c)")
                                         ).then_inc(s_in[j], 16)

            @block.tensor
            def _(pe):
                pe.wait_ge(s_w, 16 * len(LOADS))
                pe.wait_ge(s_prep, 2)

                def gather(n, r, quarter):
                    pe.wait_ge(s_in[r], quarter * 48 + 48)
                    pe.wait_ge(s_acc, n * 4 + 4)
                    for o in range(1, ORD):
                        dst = p_h[:, r % 2, o - 1, :]
                        nc.tensor.matmul(dst, flip_sb[:, o - 1, :], xo[:, r, o, :], start=True, stop=False)
                        mm = nc.tensor.matmul(dst, ident_sb[:, :], xo[:, r, 4, :], start=False, stop=True)
                    mm.then_inc(s_g, 1)

                def column_sums(n, first, last):
                    pe.wait_ge(s_x2, n + 1)
                    nc.tensor.matmul(p_sum[:, 0:C], ones[:, :], x2[:, bass.ds(n, 1), :].rearrange("p t c -> p (t c)"),
                                     start=first, stop=last, skip_group_check=True).then_inc(s_sum, 1)

                gather(0, 0, 0)

                def body(n, r, quarter):
                    if inside(n, 0, 1):
                        gather(n + 1, (r + 1) % 4, quarter + (r + 1) // 4)
                    if inside(n, 3, 0):
                        column_sums(n + -3, isinstance(n, int) and n == 3, False)

                for n in range(4):
                    body(n, n % 4, 0)
                with pe.Fori(0, (NT - 8) // 4) as i:
                    for j in range(4):
                        body(i * 4 + (4 + j), j, i + 1)
                for n in range(NT - 4, NT):
                    body(n, n % 4, NT // 4 - 1)
                for n in range(NT - 3, NT):
                    column_sums(n, False, n == NT - 1)

            @block.vector
            def _(dve):
                nc.vector.memset(ones[:, :], 1.0).then_inc(s_prep, 1)
                dve.wait_ge(s_w, 16 * len(LOADS))
                nc.vector.tensor_scalar(wf4[:, :], wf_sb[:, :], 1.0 / ORD, None, ALU.mult).then_inc(s_prep, 1)
                dve.sem_inc(s_acc, 8)

                def scale_sum(n, r):
                    dve.wait_ge(s_rt, n + 1)
                    nc.vector.reciprocal(rs[:, r, :], rt[:, r, :]).then_inc(s_rs, 1)
                    dve.wait_ge(s_rs, n + 1)
                    dve.wait_ge(s_h0, n + 5)
                    dve.wait_ge(s_g, n + 5)
                    nc.vector.tensor_scalar(acc[:, r, :], h0[:, r % 2, :], rs[:, r, 0:1], None, ALU.mult).then_inc(s_acc, 1)
                    for o in range(1, ORD):
                        dve.wait_ge(s_acc, n * 4 + (8 + o))
                        nc.vector.scalar_tensor_tensor(acc[:, r, :], p_h[:, r % 2, o - 1, :], rs[:, r, o:o + 1], acc[:, r, :],
                                                       ALU.mult, ALU.add).then_inc(s_acc, 1)

                def moments(n, r):
                    dve.wait_ge(s_y, n + 1)
                    nc.vector.bn_stats(stats[:, r, :], y[:, r, :]).then_inc(s_bn, 1)
                    dve.wait_ge(s_bn, n + 1)
                    dve.sem_inc(s_passed, 1)
                    nc.vector.bn_aggr(mv[:, r, :], stats[:, r, :]).then_inc(s_mv, 1)
                    dve.wait_ge(s_mv, n + 1)
                    nc.vector.tensor_scalar(ve[:, r:r + 1], mv[:, r, 1:2], 1e-5, None, ALU.add).then_inc(s_ve, 1)

                def layer_norm(n, r):
                    dve.wait_ge(s_rt2, n + 1)
                    nc.vector.reciprocal(rs2[:, r:r + 1], rt2[:, r:r + 1]).then_inc(s_rs2, 1)
                    nc.vector.scalar_tensor_tensor(cen[:, r % 2, :], y[:, r, :], mv[:, r, 0:1], lw_sb[:, :], ALU.subtract, ALU.mult
                                                   ).then_inc(s_cen, 1)
                    dve.wait_ge(s_rs2, n + 1)
                    dve.wait_ge(s_cen, n + 1)
                    nc.vector.scalar_tensor_tensor(x2[:, bass.ds(n, 1), :].rearrange("p t c -> p (t c)"), cen[:, r % 2, :],
                                                   rs2[:, r:r + 1], lb_sb[:, :], ALU.mult, ALU.add).then_inc(s_x2, 1)

                def mean_square(n, r):
                    dve.wait_ge(s_ss, n * 4 + 4)
                    nc.vector.tensor_scalar(ms[:, r, :], ss[:, r, :], 1.0 / C, 1e-5, ALU.mult, ALU.add).then_inc(s_ms, 1)

                mean_square(0, 0)

                def body(n, r, quarter):
                    scale_sum(n, r)
                    if inside(n, 1, 0):
                        moments(n + -1, (r - 1) % 4)
                    if inside(n, 2, 0):
                        layer_norm(n + -2, (r - 2) % 4)
                    if inside(n, 0, 1):
                        mean_square(n + 1, (r + 1) % 4)

                every_tile(body)(dve)
                moments(NT - 1, 3)
                layer_norm(NT - 2, 2)
                layer_norm(NT - 1, 3)
                dve.wait_ge(s_sum, NT)
                nc.vector.tensor_scalar(mean_sb[:, :], p_sum[:, 0:C], 1.0 / ROWS, None, ALU.mult).then_inc(s_sum, 1)

            @block.scalar
            def _(act):
                def squares(n, r):
                    act.wait_ge(s_h0, n + 5)
                    act.wait_ge(s_g, n + 5)
                    for o in range(ORD):
                        src = h0[:, r % 2, :] if o == 0 else p_h[:, r % 2, o - 1, :]
                        nc.scalar.activation(sq[:, o, :], src, ACT.Square, accum_out=ss[:, r, o:o + 1]).then_inc(s_ss, 1)

                def root(n, r):
                    act.wait_ge(s_ms, n + 1)
                    nc.scalar.activation(rt[:, r, :], ms[:, r, :], ACT.Sqrt).then_inc(s_rt, 1)

                def root2(n, r):
                    act.wait_ge(s_ve, n + 1)
                    nc.scalar.activation(rt2[:, r:r + 1], ve[:, r:r + 1], ACT.Sqrt).then_inc(s_rt2, 1)

                squares(0, 0)
                root(0, 0)

                def body(n, r, quarter):
                    if inside(n, 0, 1):
                        squares(n + 1, (r + 1) % 4)
                    if inside(n, 1, 0):
                        root2(n + -1, (r - 1) % 4)
                    if inside(n, 0, 1):
                        root(n + 1, (r + 1) % 4)

                every_tile(body)(act)
                root2(NT - 1, 3)

            @block.gpsimd
            def _(pool):
                pool.wait_ge(s_prep, 2)

                def add_residual(n, r, quarter):
                    pool.wait_ge(s_in[r], quarter * 48 + 48)
                    pool.wait_ge(s_acc, n * 4 + 4)
                    nc.gpsimd.tensor_tensor(h0[:, r % 2, :], xo[:, r, 0, :], xo[:, r, 4, :], ALU.add).then_inc(s_h0, 1)

                add_residual(0, 0, 0)
                add_residual(1, 1, 0)

                def body(n, r, quarter):
                    pool.wait_ge(s_acc, n * 4 + 12)
                    nc.gpsimd.tensor_tensor(y[:, r, :], acc[:, r, :], wf4[:, :], ALU.mult).then_inc(s_y, 1)
                    if inside(n, 0, 2):
                        add_residual(n + 2, (r + 2) % 4, quarter + (r + 2) // 4)

                every_tile(body)(pool)

        with ExitStack() as ctx:
            m = Pool_(nc, ctx, "wh")
            mask_sb, g_sb, b_sb = m.sb("mask", [P, P]), m.sb("gamma", [P, C]), m.sb("beta", [P, C])
            cov, diag, junk = m.sb("cov", [P, KC, P]), m.sb("diag", [P, KC]), m.sb("junk", [P, P])
            tr, itr, rtr = m.sb("trace", [P, KC]), m.sb("itrace", [P, KC]), m.sb("rtrace", [P, KC])
            i15 = m.sb("i15", [P, P])
            Y, Z, Wm = m.sb("Y", [P, 2, KC, 2, P]), m.sb("Z", [P, 2, KC, 2, P]), m.sb("W", [P, KC, 2, P])
            proj = m.sb("proj", [P, KC, P])
            cT = m.sb("cT", [P, 2, 2, KC, P])
            o_sb = m.sb("o", [P, 4, 2, C])
            p_cov = [m.ps(f"cov{i}", [P, 512]) for i in range(2)]
            p_t, p_o = m.ps("t", [P, 2, 512]), m.ps("o", [P, 2, 512])

            s_w, s_c, s_cov, s_prep = m.sem("weights"), m.sem("centred"), m.sem("covariance"), m.sem("step")
            s_tr, s_rt = m.sem("trace"), m.sem("root")
            s_zy, s_wm, s_yz, s_new = ([m.sem(f"{k}{i}") for i in range(KC)] for k in ("zy", "w", "yz", "new"))
            s_t, s_ct, s_o, s_ob = m.sem("turned"), m.sem("turned_copied"), m.sem("whitened"), m.sem("out_ready")
            s_proj = m.sem("proj")
            s_st = [m.sem(f"stored{i}") for i in range(4)]
            block = ctx.enter_context(nc.Block())
            LOADS = ((mask_sb, blocks), (g_sb, gamma), (b_sb, beta))
            CH = 8
            out_dram = out.rearrange("b (t p) c -> p (b t) c", p=P)

            @block.sync
            def _(sp):
                for dst, src in LOADS:
                    sp.dma_start(dst[:, :], src).then_inc(s_w, 16)
                for n in range(NT // 2):
                    sp.wait_ge(s_ob, n + 1)
                    sp.dma_start(out_dram[:, 2 * n:2 * n + 2, :], o_sb[:, n % 4, :, :]).then_inc(s_st[n % 4], 16)
                for i in range(4):
                    sp.wait_ge(s_st[i], 16 * NT // 8)

            @block.tensor
            def _(pe):
                for t in range(NT):
                    pe.wait_ge(s_c, t // CH + 1)
                    for kc in range(KC):
                        blk = x2[:, t, kc * P:(kc + 1) * P]
                        mm = nc.tensor.matmul(p_cov[kc][:, 0:P], blk, blk, start=(t == 0), stop=(t == NT - 1))
                mm.then_inc(s_cov, 1)
                pe.wait_ge(s_prep, 8)
                nc.tensor.matmul(p_t[:, 0, 0:KC], mask_sb[:, :], diag[:, :], start=True, stop=True).then_inc(s_tr, 1)
                for it in range(ITERS):
                    a = it % 2
                    for kc in range(KC):
                        pe.wait_ge(s_new[kc], 2 * it + 2)
                        nc.tensor.matmul(p_cov[kc][:, 0:P], Z[:, a, kc, 1, :], Y[:, a, kc, 0, :], start=True, stop=True)
                        nc.tensor.matmul(p_cov[kc][:, P:2 * P], Y[:, a, kc, 0, :], Z[:, a, kc, 1, :], start=True, stop=True).then_inc(s_zy[kc], 1)
                    for kc in range(KC):
                        pe.wait_ge(s_wm[kc], it + 1)
                        nc.tensor.matmul(p_t[:, kc, 0:P], Y[:, a, kc, 1, :], Wm[:, kc, 0, :], start=True, stop=True)
                        nc.tensor.matmul(p_t[:, kc, P:2 * P], Wm[:, kc, 0, :], Y[:, a, kc, 1, :], start=True, stop=True).then_inc(s_yz[kc], 1)
                        nc.tensor.matmul(p_o[:, kc, 0:P], Wm[:, kc, 1, :], Z[:, a, kc, 0, :], start=True, stop=True)
                        nc.tensor.matmul(p_o[:, kc, P:2 * P], Z[:, a, kc, 0, :], Wm[:, kc, 1, :], start=True, stop=True).then_inc(s_yz[kc], 1)
                pe.wait_ge(s_proj, KC)

                def turn(n):
                    if n >= 2:
                        pe.wait_ge(s_ct, n - 1)
                    for t in range(2):
                        for kc in range(KC):
                            at = (2 * t + kc) * P
                            mm = nc.tensor.transpose(p_t[:, n % 2, at:at + P], x2[:, 2 * n + t, kc * P:(kc + 1) * P], ident_sb[:, :])
                    mm.then_inc(s_t, 1)

                turn(0)
                for n in range(NT // 2):
                    if n + 1 < NT // 2:
                        turn(n + 1)
                    pe.wait_ge(s_ct, n + 1)
                    if n >= 2:
                        pe.wait_ge(s_ob, n - 1)
                    for t in range(2):
                        for kc in range(KC):
                            at = (2 * t + kc) * P
                            mm = nc.tensor.matmul(p_o[:, n % 2, at:at + P], cT[:, n % 2, t, kc, :], proj[:, kc, :], start=True, stop=True)
                    mm.then_inc(s_o, 1)

            @block.scalar
            def _(act):
                act.wait_ge(s_prep, 10)
                nc.scalar.activation(rtr[:, :], tr[:, :], ACT.Sqrt).then_inc(s_rt, 1)
                for it in range(ITERS):
                    for kc in range(KC):
                        act.wait_ge(s_yz[kc], 2 * it + 2)
                        nc.scalar.copy(Z[:, (it + 1) % 2, kc, :, :], p_o[:, kc, 0:2 * P].rearrange("p (a n) -> p a n", a=2)).then_inc(s_new[kc], 1)
                for n in range(NT // 2):
                    act.wait_ge(s_t, n + 1)
                    if n >= 2:
                        act.wait_ge(s_o, n - 1)
                    nc.scalar.copy(cT[:, n % 2, :, :, :], p_t[:, n % 2, :].rearrange("p (t k n) -> p t k n", t=2, k=KC)
                                   ).then_inc(s_ct, 1)

            @block.vector
            def _(dve):
                mean_b = mean_sb[:, None, :].broadcast_to([P, CH, C])
                for i in range(NT // CH):
                    nc.vector.tensor_tensor(x2[:, i * CH:(i + 1) * CH, :], x2[:, i * CH:(i + 1) * CH, :], mean_b, ALU.subtract
                                            ).then_inc(s_c, 1)
                done = [0]

                def step(ins):
                    done[0] += 1
                    ins.then_inc(s_prep, 1)
                    dve.wait_ge(s_prep, done[0])

                dve.wait_ge(s_w, 16 * len(LOADS))
                dve.wait_ge(s_cov, 1)
                for kc in range(KC):
                    step(nc.vector.scalar_tensor_tensor(cov[:, kc, :], p_cov[kc][:, 0:P], 1.0 / ROWS, mask_sb[:, :], ALU.mult, ALU.mult))
                    step(nc.vector.scalar_tensor_tensor(cov[:, kc, :], ident_sb[:, :], 1e-5, cov[:, kc, :], ALU.mult, ALU.add))
                for kc in range(KC):
                    step(nc.vector.tensor_tensor(Wm[:, kc, 0, :], cov[:, kc, :], ident_sb[:, :], ALU.mult))
                    step(nc.vector.tensor_reduce(diag[:, kc:kc + 1], Wm[:, kc, 0, :], AX.X, ALU.add))
                step(nc.vector.tensor_scalar(i15[:, :], ident_sb[:, :], 1.5, None, ALU.mult))
                dve.wait_ge(s_tr, 1)
                step(nc.vector.tensor_copy(tr[:, :], p_t[:, 0, 0:KC]))
                step(nc.vector.reciprocal(itr[:, :], tr[:, :]))
                for kc in range(KC):
                    two = [P, 2, P]
                    nc.vector.tensor_scalar(Y[:, 0, kc, :, :], cov[:, kc:kc + 1, :].broadcast_to(two), itr[:, kc:kc + 1], None,
                                            ALU.mult).then_inc(s_new[kc], 1)
                    nc.vector.tensor_copy(Z[:, 0, kc, :, :], ident_sb[:, None, :].broadcast_to(two)).then_inc(s_new[kc], 1)
                for it in range(ITERS):
                    for kc in range(KC):
                        dve.wait_ge(s_zy[kc], it + 1)
                        nc.vector.scalar_tensor_tensor(Wm[:, kc, :, :], p_cov[kc][:, 0:2 * P].rearrange("p (a n) -> p a n", a=2), -0.5,
                                                       i15[:, None, :].broadcast_to(two), ALU.mult, ALU.add
                                                       ).then_inc(s_wm[kc], 1)
                    for kc in range(KC):
                        dve.wait_ge(s_yz[kc], 2 * it + 2)
                        nc.vector.tensor_copy(Y[:, (it + 1) % 2, kc, :, :], p_t[:, kc, 0:2 * P].rearrange("p (a n) -> p a n", a=2)).then_inc(s_new[kc], 1)
                dve.wait_ge(s_rt, 1)
                step(nc.vector.reciprocal(rtr[:, :], rtr[:, :]))
                for kc in range(KC):
                    dve.wait_ge(s_new[kc], 2 * ITERS + 2)
                    nc.vector.scalar_tensor_tensor(proj[:, kc, :], Z[:, ITERS % 2, kc, 0, :], rtr[:, kc:kc + 1],
                                                   g_sb[:, kc * P:(kc + 1) * P], ALU.mult, ALU.mult).then_inc(s_proj, 1)
                for n in range(NT // 2):
                    dve.wait_ge(s_o, n + 1)
                    if n >= 4:
                        dve.wait_ge(s_st[n % 4], 16 * (n // 4))
                    nc.vector.tensor_tensor(o_sb[:, n % 4, :, :], p_o[:, n % 2, :].rearrange("p (t c) -> p t c", t=2),
                                            b_sb[:, None, :].broadcast_to([P, 2, C]), ALU.add).then_inc(s_ob, 1)


def network(nc, a, out):
    def scratch(name, shape):
        return nc.dram_tensor(name, shape, F32, kind="Internal").ap()

    x0, x1 = scratch("x0", (B, N, C)), scratch("x1", (B, N, C))
    xn = scratch("xn", (SEQS, CHUNKS, P, KC, T))
    mix = scratch("mix", (SEQS, N, C))
    attention(nc, a["xT"], a["x"], a["wqT"], a["wkT"], a["bq"], a["bk"], a["wvT"], a["bv"], a["gamma"], a["ident"],
              a["halves"], x0)
    fourier_conv(nc, x0, a["w1T"], (a["bn1c"], a["bn1"]), a["fuT"], a["bnf"], a["lfuT"], a["bnl"], a["w2T"], a["dft"],
                 a["dftl"], a["idft"], a["idftl"], a["ident"], a["rms1"], x1, xn)
    mamba(nc, xn, a["w_inT"], a["conv_w"], a["conv_b"], a["w_xT"], a["split"], a["w_dtT"], a["b_dt"], a["a_log"],
          a["d_skip"], a["w_outT"], a["ident"], a["pick"], a["keep"], mix)
    combine_and_whiten(nc, mix, x1, a["flips"], a["wf"], a["ln_w"], a["ln_b"], a["ident"], a["blocks"], a["gamma3"],
                       a["beta3"], out)


def fourier_matrices(np):
    def pair(n):
        w, k = np.arange(n)[:, None], np.arange(n // 2 + 1)[None]
        ang = 2 * np.pi * w * k / n
        weight = np.full((1, n // 2 + 1), 2.0)
        weight[0, 0] = weight[0, -1] = 1
        im = (-weight * np.sin(ang) / np.sqrt(n)).T
        im[0] = im[-1] = 0
        return np.cos(ang) / np.sqrt(n), -np.sin(ang) / np.sqrt(n), (weight * np.cos(ang) / np.sqrt(n)).T, im

    fr, fi, ir, ii = pair(W)
    dft, idft = np.zeros((P, 2, 2, FR)), np.zeros((2, FR, 2, P))
    for r in range(2):
        at = slice(r * W, (r + 1) * W)
        dft[at, 0, r], dft[at, 1, r], idft[r, :, 0, at], idft[r, :, 1, at] = fr, fi, ir, ii
    fr, fi, ir, ii = pair(W // 2)
    dftl, idftl = np.zeros((P, 2, 2, 2, FL)), np.zeros((2, FL, 2, P))
    for r in range(2):
        for half in range(2):
            at = slice(r * W + half * W // 2, r * W + (half + 1) * W // 2)
            dftl[at, half, 0, r], dftl[at, half, 1, r], idftl[r, :, 0, at], idftl[r, :, 1, at] = fr, fi, ir, ii
    f32 = np.float32
    return (dft.reshape(P, 4 * FR).astype(f32), idft.reshape(2 * FR, 2, P).astype(f32),
            dftl.reshape(P, 2, 4 * FL).astype(f32), idftl.reshape(2 * FL, 2, P).astype(f32))


def layouts(np, i):
    d = {}
    x = i["x"].reshape(B, N, C)
    d["x"], d["xT"] = x, x.transpose(0, 2, 1)

    d["wqT"], d["wkT"] = np.tile(i["L0_conv_Wq"].T, (1, 4)), np.tile(i["L0_conv_Wk"].T, (1, 4))
    d["bq"], d["bk"] = np.tile(i["L0_conv_bq"], 4)[:, None], np.tile(i["L0_conv_bk"], 4)[:, None]
    halves = np.array([[0, 0, 0, -1], [0, -1, -1, 0], [-1, 0, 0, 0], [-1, -1, 0, 0]], np.float32)
    d["halves"] = np.repeat(halves, CQ, 0)
    d["wvT"], d["bv"] = i["L0_conv_Wv"].T, np.broadcast_to(i["L0_conv_bv"], (P, C))
    d["gamma"] = np.broadcast_to(i["L0_conv_gamma"], (P, 1))
    d["ident"] = np.eye(P, dtype=np.float32)

    def parts(v):
        return np.concatenate([v[..., 0::2], v[..., 1::2]], -1)

    def bn(*names):
        return np.stack([i["L1_conv_" + n] for n in names])

    d["w1T"], d["w2T"] = i["L1_conv_w1"].T, i["L1_conv_w2"].T
    d["bn1"] = bn("g1", "b1", "m1", "v1")
    d["bn1c"] = d["bn1"].T
    d["bnf"] = parts(bn("fu_g", "fu_b", "fu_m", "fu_v"))
    d["bnl"] = parts(bn("lfu_g", "lfu_b", "lfu_m", "lfu_v"))
    d["fuT"] = parts(i["L1_conv_fu_w"].T.reshape(HC, 2, C))
    d["lfuT"] = parts(i["L1_conv_lfu_w"].T.reshape(HC, 2, C))
    d["dft"], d["idft"], d["dftl"], d["idftl"] = fourier_matrices(np)

    m = {k[len("L2_conv_"):]: v for k, v in i.items() if k.startswith("L2_conv_")}
    d["rms1"] = m["rms_w1"].reshape(KC, P).T

    def by_block(v):
        return v.reshape(IB, P, -1).transpose(1, 0, 2).reshape(P, -1)

    d["w_inT"], d["w_dtT"], d["w_outT"] = m["W_in"].T, m["W_dt"].T, m["W_out"].T
    d["conv_w"], d["conv_b"] = by_block(m["conv_w"]), by_block(m["conv_b"])
    wx = m["W_x"].T
    d["w_xT"] = np.concatenate([wx[:, RK:]] * 3 + [wx[:, :RK]], 1)
    d["b_dt"], d["a_log"], d["d_skip"] = by_block(m["b_dt"]), by_block(m["A_log"]), by_block(m["Dp"])
    copy = np.arange(P)[:, None] // (2 * NS)
    d["split"] = np.concatenate([np.where(copy >= 1, -1, 0), np.where(copy >= 2, -1, 0)], 1).astype(np.float32)
    d["pick"] = np.repeat(np.tile(np.eye(2 * NS, dtype=np.float32), (3, 1))[:, :, None], P, 2)
    d["keep"] = np.repeat((np.arange(SEQS * CHUNKS + 1)[None] % CHUNKS != 0).astype(np.float32), P, 0)

    def on_all(v):
        return np.broadcast_to(v.reshape(1, C), (P, C))

    d["wf"], d["ln_w"], d["ln_b"] = on_all(m["rms_wf"]), on_all(m["ln_w"]), on_all(m["ln_b"])
    d["gamma3"], d["beta3"] = on_all(i["L3_conv_gamma"]), on_all(i["L3_conv_beta"])
    t = np.arange(P)
    r, w = t // W, t % W
    sources = (r * W + W - 1 - w, (1 - r) * W + w, P - 1 - t)
    d["flips"] = np.stack([np.eye(P, dtype=np.float32)[:, s] for s in sources], 1)
    d["blocks"] = np.kron(np.eye(P // M), np.ones((M, M))).astype(np.float32)
    return {k: np.ascontiguousarray(v) for k, v in d.items()}


def kernel(**inputs):
    import numpy as np
    import concourse.bacc as bacc
    from concourse import mybir as mb
    from concourse.bass_utils import run_bass_kernel_spmd

    nc = bacc.Bacc("TRN2", target_bir_lowering=False, num_devices=1)
    arrays = {f"in_{k}": v for k, v in layouts(np, {k: np.asarray(v) for k, v in inputs.items()}).items()}
    a = {k[3:]: nc.dram_tensor(k, v.shape, mb.dt.from_np(v.dtype), kind="ExternalInput").ap() for k, v in arrays.items()}
    out = nc.dram_tensor("out_0", (B, N, C), F32, kind="ExternalOutput").ap()
    network(nc, a, out)
    r = run_bass_kernel_spmd(nc, [arrays], core_ids=[0])
    return r.results[0]["out_0"].reshape(B, H, W, C)
```

```python
from contextlib import ExitStack

import concourse.bass as bass
from concourse import mybir

F32 = mybir.dt.float32
BF16 = mybir.dt.bfloat16
ALU = mybir.AluOpType
ACT = mybir.ActivationFunctionType
AX = mybir.AxisListType

P = 128
B, H, W, C = 2, 64, 64, 256
N = H * W
KC = C // P
TILES = N // P
CQ = C // 8

I = 2 * C
IB = I // P
NS = 16
RK = 16
TAPS = 4
T = 512
CHUNKS = N // T
SEQS = 4 * B

M = 16


class Pool_:

    def __init__(self, nc, ctx, tag):
        self.nc, self.ctx, self.tag = nc, ctx, tag

    def sb(self, name, shape, dt=F32):
        return self.ctx.enter_context(self.nc.sbuf_tensor(f"{self.tag}_{name}", shape, dt))

    def ps(self, name, shape, dt=F32):
        return self.ctx.enter_context(self.nc.psum_tensor(f"{self.tag}_p_{name}", shape, dt))

    def sem(self, name):
        return self.ctx.enter_context(self.nc.semaphore(f"{self.tag}_s_{name}"))


def attention(nc, xT, x, wqT, wkT, bq, bk, wvT, bv, gamma, ident, halves, x0):
    LOW = 2 * CQ
    LM = LOW + 3
    IT = 512
    JP = TILES // 2
    with ExitStack() as ctx:
        m = Pool_(nc, ctx, "at")
        xT_sb = m.sb("xT", [P, KC, N])
        wq_sb, wk_sb = m.sb("wq", [P, KC, P]), m.sb("wk", [P, KC, P])
        wv_sb = m.sb("wv", [P, KC, C])
        bq_sb, bk_sb, halves_sb = m.sb("bq", [P, 1]), m.sb("bk", [P, 1]), m.sb("halves", [P, 4])
        bv_sb, gbv = m.sb("bv", [P, C]), m.sb("gbv", [P, C])
        gamma_sb, ident_sb, ident16 = m.sb("gamma", [P, 1]), m.sb("ident", [P, P]), m.sb("ident16", [P, P], BF16)
        qa, ka, qb, kb = m.sb("qa", [P, N], BF16), m.sb("ka", [P, N], BF16), m.sb("qb", [LM, N], BF16), m.sb("kb", [LM, N], BF16)
        whole, hi = m.sb("whole", [P, 2, IT]), m.sb("hi", [P, 2, IT], BF16)
        rest, mid = m.sb("rest", [LOW, 2, IT]), m.sb("mid", [LOW, 2, IT], BF16)
        q_now = m.sb("qnow", [P, 2, 2, IT], BF16)
        v_sb = m.sb("v", [P, TILES, C + 1])
        part_max = m.sb("pmax", [P, TILES, 4])
        negmax, neg_rest = m.sb("negmax", [P, TILES]), m.sb("negrest", [P, 2, TILES])
        neg3 = m.sb("neg3", [P, 3, TILES], BF16)
        probs = m.sb("probs", [P, 2, 2, IT])
        x_now, xb = m.sb("xnow", [P, 2, 4, C]), m.sb("xb", [P, 2, 4, C])
        recip = m.sb("recip", [P, 4])
        rg = m.sb("rg", [P, 4])
        out_sb = m.sb("out", [P, 2, 4, C])
        ps = m.ps("all", [P, 8, 512])

        s_w, s_xT = m.sem("weights"), [m.sem(f"xT_half{i}_loaded") for i in range(2)]
        s_const = m.sem("consts_set")
        s_proj, s_whole, s_hi = m.sem("projected"), m.sem("projection_copied"), m.sem("hi")
        s_first, s_rest, s_mid, s_second = m.sem("first_rows"), m.sem("rest"), m.sem("mid"), m.sem("second_rows")
        s_v, s_vc = m.sem("values"), m.sem("values_copied")
        s_mx, s_mx_free = m.sem("scores_for_max"), m.sem("max_taken")
        s_neg, s_negT, s_negrow = m.sem("negmax"), m.sem("negmax_row"), m.sem("negmax_row_in_q")
        s_pm, s_xb = m.sem("max_split_step"), m.sem("x_with_bias")
        s_passed = m.sem("pool_passed")
        s_qn, s_qn_free = m.sem("q_now"), m.sem("q_now_free")
        s_sc, s_pr, s_pv = m.sem("scores"), m.sem("probs"), m.sem("pair_summed")
        s_x = [m.sem("x_now0"), m.sem("x_now1")]
        s_rc, s_rg, s_o = m.sem("recip"), m.sem("recip_gamma"), m.sem("out_ready")
        s_st = [m.sem("stored0"), m.sem("stored1")]
        s_acc_free = m.sem("acc_free")
        block = ctx.enter_context(nc.Block())
        PROJ = 2 * (N // 512)
        VS = TILES // 2
        GR = 4
        MAXS = GR * TILES

        xv = x.rearrange("b (t g p) c -> b t p g c", p=P, g=4)
        ov = x0.rearrange("b (t g p) c -> b t p g c", p=P, g=4)

        @block.sync
        def _(sp):
            for dst, src in ((wq_sb, wqT), (wk_sb, wkT), (wv_sb, wvT)):
                sp.dma_start(dst[:, :, :], src.rearrange("(k p) o -> p k o", p=P)).then_inc(s_w, 16)
            for dst, src in ((bq_sb, bq), (bk_sb, bk), (bv_sb, bv), (gamma_sb, gamma), (ident_sb, ident),
                             (halves_sb, halves)):
                sp.dma_start(dst[:, :], src).then_inc(s_w, 16)
            sp.sem_inc(s_st[0], 16)
            sp.sem_inc(s_st[1], 16)
            for b in range(B):
                if b:
                    sp.wait_ge(s_proj, PROJ * b)
                    sp.wait_ge(s_v, VS * b)
                for i in range(2):
                    half = slice(i * N // 2, (i + 1) * N // 2)
                    sp.dma_start(xT_sb[:, :, half], xT[b].rearrange("(k p) n -> p k n", p=P)[:, :, half]).then_inc(s_xT[i], 16)
                for t in range(N // IT):
                    n = b * (N // IT) + t
                    if n >= 2:
                        sp.wait_ge(s_xb, n - 1)
                    sp.dma_start(x_now[:, n % 2, :, :], xv[b, t]).then_inc(s_x[n % 2], 16)
                    if n >= 1:
                        sp.wait_ge(s_o, 4 * n)
                        sp.dma_start(ov[(n - 1) // 8, (n - 1) % 8], out_sb[:, (n - 1) % 2, :, :]).then_inc(s_st[(n - 1) % 2], 16)
            n = B * (N // IT)
            sp.wait_ge(s_o, 4 * n)
            sp.dma_start(ov[B - 1, 7], out_sb[:, (n - 1) % 2, :, :]).then_inc(s_st[(n - 1) % 2], 16)
            for par in range(2):
                sp.wait_ge(s_st[par], 8 * n + 16)

        @block.tensor
        def _(pe):
            pe.sem_inc(s_sc, 2 * JP)
            pe.wait_ge(s_w, 16 * 9)
            pe.wait_ge(s_const, 3)
            with pe.Fori(0, B) as b:
                pe.wait_ge(s_acc_free, b * 8 + 2)
                for step in range(PROJ):
                    w, t = (wq_sb, wk_sb)[step // 8], step % 8
                    if step in (0, 4):
                        pe.wait_ge(s_xT[step // 4], b * 16 + 16)
                    if step >= 6:
                        pe.wait_ge(s_whole, b * PROJ + (step - 5))
                    for kc in range(KC):
                        mm = nc.tensor.matmul(ps[:, step % 6, :], w[:, kc, :], xT_sb[:, kc, t * 512:(t + 1) * 512],
                                              start=(kc == 0), stop=(kc == KC - 1))
                    mm.then_inc(s_proj, 1)

                def values(t):
                    if t >= 2:
                        pe.wait_ge(s_vc, b * VS + (t - 1))
                    for g in range(2):
                        o = ps[:, 6 + t % 2, g * C:(g + 1) * C]
                        tok = (2 * t + g) * P
                        for kc in range(KC):
                            mm = nc.tensor.matmul(o, xT_sb[:, kc, tok:tok + P], wv_sb[:, kc, :], start=(kc == 0), stop=(kc == KC - 1))
                    mm.then_inc(s_v, 1)

                values(0)
                values(1)
                pe.wait_ge(s_whole, b * PROJ + PROJ)
                pe.wait_ge(s_first, b * PROJ + PROJ)
                pe.wait_ge(s_second, b * PROJ + PROJ)
                for it in range(TILES):
                    if it % 2 == 0 and it >= 4:
                        values(it // 2)
                    for g in range(GR):
                        n, tok = GR * it + g, it * P
                        if n >= 3:
                            pe.wait_ge(s_mx_free, b * MAXS + (n - 2))
                        for q_rows, k_rows, rows, first in ((qa, ka, P, True), (qb, kb, LOW, False)):
                            for j in range(2):
                                jj = (2 * g + j) * 512
                                mm = nc.tensor.matmul(ps[:, 2 * (n % 3) + j, :], q_rows[0:rows, tok:tok + P],
                                                      k_rows[0:rows, jj:jj + 512], start=first, stop=not first)
                        mm.then_inc(s_mx, 1)
                pe.wait_ge(s_neg, b + 1)
                pe.wait_ge(s_vc, b * VS + VS)
                for it in range(TILES):
                    mm = nc.tensor.matmul(ps[LOW:LM, it // 4, (it % 4) * P:(it % 4 + 1) * P],
                                          neg3[:, :, it], ident16[:, :], start=True, stop=True)
                mm.then_inc(s_negT, 1)
                with pe.Fori(0, N // IT // 2) as th:
                    pe.wait_ge(s_negrow, b * 2 + 2)
                    for par in range(2):
                        q = b * (N // IT) + th * 2 + par

                        def scores(j):
                            pe.wait_ge(s_pr, q * JP + (j + 1))
                            for r in range(2):
                                tok, bank = (2 * j + r) * P, 2 * (j % 2) + r
                                nc.tensor.matmul(ps[:, bank, :], ka[:, tok:tok + P], q_now[:, par, 0, :], start=True, stop=False)
                                mm = nc.tensor.matmul(ps[:, bank, :], kb[:, tok:tok + P], q_now[0:LM, par, 1, :], start=False, stop=True)
                            mm.then_inc(s_sc, 1)

                        pe.wait_ge(s_qn, q * 2 + 2)
                        scores(0)
                        for j in range(JP):
                            if j + 1 < JP:
                                scores(j + 1)
                            if j == 0:
                                pe.wait_ge(s_acc_free, q + 2)
                            pe.wait_ge(s_pr, q * JP + (j + 3))
                            for r in range(2):
                                jb = 2 * j + r
                                for g in range(4):
                                    mm = nc.tensor.matmul(ps[:, 4 + g, 0:C + 1], probs[:, j % 2, r, g * P:(g + 1) * P],
                                                          v_sb[:, jb, :], start=(jb == 0), stop=(jb == TILES - 1))
                            mm.then_inc(s_pv, 1)

        @block.vector
        def _(dve):
            dve.sem_inc(s_acc_free, 2)
            nc.vector.memset(kb[LOW:LM, :], 1.0).then_inc(s_const, 1)
            nc.vector.memset(v_sb[:, :, C:C + 1], 1.0).then_inc(s_const, 1)
            dve.wait_ge(s_w, 16 * 9)
            nc.vector.tensor_copy(ident16[:, :], ident_sb[:, :]).then_inc(s_const, 1)
            nc.vector.tensor_scalar(gbv[:, :], bv_sb[:, :], gamma_sb[:, 0:1], None, ALU.mult).then_inc(s_const, 1)
            with dve.Fori(0, B) as b:
                dve.wait_ge(s_pv, b * (8 * JP) + 2)

                def second_rows(t):
                    dve.wait_ge(s_mid, b * PROJ + (t + 1))
                    dst, col, at = (qb, kb)[t // 8], 2 + t // 8, (t % 8) * 512
                    nc.vector.scalar_tensor_tensor(dst[0:LOW, at:at + 512], mid[:, t % 2, :], halves_sb[0:LOW, col:col + 1],
                                                   rest[:, t % 2, :], ALU.mult, ALU.add).then_inc(s_second, 1)

                for t in range(PROJ):
                    dve.wait_ge(s_hi, b * PROJ + (t + 1))
                    dst, col, at = (qa, ka)[t // 8], t // 8, (t % 8) * 512
                    nc.vector.scalar_tensor_tensor(dst[:, at:at + 512], hi[:, t % 2, :], halves_sb[:, col:col + 1],
                                                   whole[:, t % 2, :], ALU.mult, ALU.add).then_inc(s_first, 1)
                    if t >= 2:
                        dve.wait_ge(s_second, b * PROJ + (t - 1))
                    nc.vector.scalar_tensor_tensor(rest[:, t % 2, :], hi[0:LOW, t % 2, :], halves_sb[0:LOW, col + 2:col + 3],
                                                   whole[0:LOW, t % 2, :], ALU.mult, ALU.add).then_inc(s_rest, 1)
                    if t >= 1:
                        second_rows(t - 1)
                second_rows(PROJ - 1)
                for n in range(MAXS):
                    dve.wait_ge(s_mx, b * MAXS + (n + 1))
                    bank = 2 * (n % 3)
                    nc.vector.tensor_reduce(part_max[:, n // GR, n % GR:n % GR + 1], ps[:, bank:bank + 2, :],
                                            AX.XY, ALU.max).then_inc(s_mx_free, 1)
                dve.wait_ge(s_mx_free, b * MAXS + MAXS)
                steps = [0]

                def step(ins):
                    steps[0] += 1
                    ins.then_inc(s_pm, 1)
                    dve.wait_ge(s_pm, b * 6 + steps[0])

                step(nc.vector.tensor_reduce(neg_rest[:, 0, :], part_max[:, :, :], AX.X, ALU.max))
                step(nc.vector.tensor_scalar(negmax[:, :], neg_rest[:, 0, :], -1.0, None, ALU.mult))
                step(nc.vector.tensor_copy(neg3[:, 0, :], negmax[:, :]))
                step(nc.vector.tensor_tensor(neg_rest[:, 0, :], negmax[:, :], neg3[:, 0, :], ALU.subtract))
                step(nc.vector.tensor_copy(neg3[:, 1, :], neg_rest[:, 0, :]))
                step(nc.vector.tensor_tensor(neg3[:, 2, :], neg_rest[:, 0, :], neg3[:, 1, :], ALU.subtract))
                dve.sem_inc(s_neg, 1)
                dve.wait_ge(s_negT, b + 1)
                nc.vector.tensor_copy(qb[LOW:LM, N // 2:].rearrange("p (a n) -> p a n", a=4), ps[LOW:LM, 4:8, :]).then_inc(s_negrow, 1)
                with dve.Fori(0, N // IT // 2) as th:
                    for par in range(2):
                        q = b * (N // IT) + th * 2 + par
                        dve.wait_ge(s_pv, q * JP + (JP + 2))
                        dve.wait_ge(s_xb, q + 1)
                        dve.wait_ge(s_st[par], b * 64 + th * 16 + 16)
                        nc.vector.reciprocal(recip[:, :], ps[:, 4:8, C]).then_inc(s_rc, 1)
                        dve.wait_ge(s_rc, q + 1)
                        nc.vector.tensor_scalar(rg[:, :], recip[:, :], gamma_sb[:, 0:1], None, ALU.mult).then_inc(s_rg, 1)
                        dve.wait_ge(s_rg, q + 1)
                        for g in range(4):
                            nc.vector.scalar_tensor_tensor(out_sb[:, par, g, :], ps[:, 4 + g, 0:C], rg[:, g:g + 1],
                                                           xb[:, par, g, :], ALU.mult, ALU.add).then_inc(s_o, 1)
                        dve.wait_ge(s_o, q * 4 + 4)
                        dve.sem_inc(s_acc_free, 1)

        @block.scalar
        def _(act):
            act.wait_ge(s_w, 16 * 9)
            act.sem_inc(s_pr, 2)
            with act.Fori(0, B) as b:
                act.wait_ge(s_pv, b * (8 * JP) + 2)

                def middle(t):
                    act.wait_ge(s_rest, b * PROJ + (t + 1))
                    if t >= 2:
                        act.wait_ge(s_second, b * PROJ + (t - 1))
                    nc.scalar.copy(mid[:, t % 2, :], rest[:, t % 2, :]).then_inc(s_mid, 1)

                for t in range(PROJ):
                    act.wait_ge(s_proj, b * PROJ + (t + 1))
                    if t >= 2:
                        act.wait_ge(s_rest, b * PROJ + (t - 1))
                    bias = (bq_sb, bk_sb)[t // 8]
                    nc.scalar.activation(whole[:, t % 2, :], ps[:, t % 6, :], ACT.Identity, bias=bias[:, 0:1]).then_inc(s_whole, 1)
                    act.wait_ge(s_whole, b * PROJ + (t + 1))
                    nc.scalar.copy(hi[:, t % 2, :], whole[:, t % 2, :]).then_inc(s_hi, 1)
                    if t >= 1:
                        middle(t - 1)
                middle(PROJ - 1)
                for t in range(VS):
                    act.wait_ge(s_v, b * VS + (t + 1))
                    nc.scalar.copy(v_sb[:, 2 * t:2 * t + 2, 0:C], ps[:, 6 + t % 2, :].rearrange("p (g c) -> p g c", g=2)
                                   ).then_inc(s_vc, 1)
                act.wait_ge(s_negT, b + 1)
                nc.scalar.copy(qb[LOW:LM, 0:N // 2].rearrange("p (a n) -> p a n", a=4), ps[LOW:LM, 0:4, :]).then_inc(s_negrow, 1)
                with act.Fori(0, N // IT) as t:
                    for j in range(JP):
                        n = b * (8 * JP) + t * JP + j
                        act.wait_ge(s_sc, n + (1 + 2 * JP))
                        act.wait_ge(s_pv, n + 1)
                        nc.scalar.activation(probs[:, j % 2, :, :], ps[:, 2 * (j % 2):2 * (j % 2) + 2, :], ACT.Exp
                                             ).then_inc(s_pr, 1)

        @block.gpsimd
        def _(pool):
            pool.sem_inc(s_pv, 2)
            with pool.Fori(0, B) as b:
                with pool.Fori(0, N // IT // 2) as th:
                    pool.wait_ge(s_negrow, b * 2 + 2)
                    for par in range(2):
                        q = b * (N // IT) + th * 2 + par
                        pool.wait_ge(s_sc, q * JP + JP)
                        nc.gpsimd.tensor_copy(q_now[:, par, 0, :], qa[:, bass.ds(th * (2 * IT) + par * IT, IT)]).then_inc(s_qn, 1)
                        nc.gpsimd.tensor_copy(q_now[0:LM, par, 1, :], qb[:, bass.ds(th * (2 * IT) + par * IT, IT)]).then_inc(s_qn, 1)
                        pool.wait_ge(s_const, 4)
                        pool.wait_ge(s_x[par], b * 64 + th * 16 + 16)
                        pool.wait_ge(s_acc_free, q + 1)
                        pool.sem_inc(s_passed, 1)
                        nc.gpsimd.tensor_tensor(xb[:, par, :, :], x_now[:, par, :, :],
                                                gbv[:, None, :].broadcast_to([P, 4, C]), ALU.add).then_inc(s_xb, 1)


FR, FL = W // 2 + 1, W // 4 + 1
Z1, Z2 = 2 * FR, 2 * FL
HC = C // 2


def fourier_conv(nc, x0, w1T, bn1, fuT, bnf, lfuT, bnl, w2T, dft, dftl, idft, idftl, ident, rms1, thirds, x1, xn):
    HT = TILES // 2
    with ExitStack() as ctx:
        m = Pool_(nc, ctx, "fc")
        w1_sb, w2_sb = m.sb("w1", [P, KC, HC]), m.sb("w2", [HC, C])
        fu_sb, lfu_sb = m.sb("fu", [HC, 2, C]), m.sb("lfu", [HC, 2, C])
        NB = HC + 2 * C
        bn_sb = m.sb("bn", [P, 4, NB])
        scale, shift = m.sb("scale", [P, NB]), m.sb("shift", [P, NB])
        bn1_col, shift_col = m.sb("bncol", [HC, 4]), m.sb("shiftcol", [HC, 4])
        dft_sb, dftl_sb = m.sb("dft", [P, 2 * Z1]), m.sb("dftl", [P, 2, 2 * Z2])
        idft_sb, idftl_sb = m.sb("idft", [Z1, 2, P]), m.sb("idftl", [Z2, 2, P])
        ident_sb, rms_sb = m.sb("ident", [P, P]), m.sb("rms", [P, KC])
        ones_rows, shift3, thirds_sb = m.sb("ones", [3, P], BF16), m.sb("shift3", [3, NB], BF16), m.sb("thirds", [3, 2])
        part16, shift_rest = m.sb("part16", [3, NB], BF16), m.sb("shift_rest", [3, NB])
        xin = m.sb("xin", [P, 4, 2, C])
        xt_sb = m.sb("xt", [P, KC, 2, P])
        y_sb, yt_sb = m.sb("y", [P, 2, HC]), m.sb("yt", [HC, 2, 2, P])
        f_sb, fl_sb = m.sb("f", [HC, 2, 2 * Z1]), m.sb("fl", [P, 2 * Z2])
        z_sb, zl_sb = m.sb("z", [Z1, 2, C]), m.sb("zl", [Z2, C])
        s_sb = m.sb("s", [HC, 2, P])
        x1_sb = m.sb("x1", [P, 2, 2, C])
        sq = m.sb("sq", [P, 2, C])
        ss, ms, rt, rstd = (m.sb(k, [P, 2]) for k in ("ss", "ms", "rt", "rstd"))
        xs_sb = m.sb("xs", [P, 2, C])
        xn_sb = m.sb("xn", [P, 2, 4, KC, 2, P])
        pT, pY, pYT, pF, pZ, pZL, pO, pX = (m.ps(k, [P, 512]) for k in ("T", "Y", "YT", "F", "Z", "ZL", "O", "X"))

        s_w, s_fold, s_fsc = m.sem("weights"), m.sem("bn_step"), m.sem("bn_sqrt")
        s_ready, s_passed = m.sem("weights_scaled"), m.sem("pool_passed")
        s_sp_passed = m.sem("sp_passed")
        s_in = [m.sem(f"xin{i}") for i in range(4)]
        s_x1st, s_xnst = ([m.sem(f"{k}{i}") for i in range(2)] for k in ("x1_stored", "xn_stored"))
        names = ["xt_ps", "xt", "y_ps", "y", "yt_ps", "yt", "f_ps", "f", "fl", "z_ps", "z", "zl_ps", "zl", "o_ps", "s",
                 "x1_ps", "x1", "ss", "ms", "rt", "rstd", "xs", "xnt_ps", "xn0", "xn1", "xn23"]
        S = {k: m.sem(k) for k in names}
        block = ctx.enter_context(nc.Block())
        NW = 15

        x0v = x0.rearrange("b (k t p) c -> p b t k c", p=P, k=2)
        x1v = x1.rearrange("b (k t p) c -> p b t k c", p=P, k=2)
        U = B * HT

        def rounds(eng, body):
            for u in range(2):
                body(u, u % 2, u // 2)
            with eng.Fori(0, (U - 4) // 2) as i:
                for j in range(2):
                    body(i * 2 + (2 + j), j, i + 1)
            for u in range(U - 2, U + 2):
                body(u, u % 2, u // 2)

        def there(u, off):
            return not isinstance(u, int) or 0 <= u + off < U

        def tiles_of(v, b, a, e):
            return v[:, b:b + 1, bass.ds(a * 4 + e, 1), :, :].rearrange("p a o k c -> p (a o k) c")

        def order_of(o, b, a, e, t):
            chunk = a + t * (CHUNKS // 2) if o < 2 else a * -1 + (CHUNKS // 2 - 1 + t * (CHUNKS // 2))
            at = e * P if o < 2 else (3 - e) * P
            return xn[b + o * B:b + o * B + 1, bass.ds(chunk, 1), :, :, at:at + P].rearrange("s h p k n -> p (s h k) n")

        @block.sync
        def _(sp):
            sp.dma_start(w1_sb[:, :, :], w1T.rearrange("(k p) o -> p k o", p=P)).then_inc(s_w, 16)
            for dst, src in ((w2_sb, w2T), (fu_sb, fuT), (lfu_sb, lfuT), (bn1_col, bn1[0]), (dft_sb, dft),
                             (dftl_sb, dftl), (idft_sb, idft), (idftl_sb, idftl), (ident_sb, ident), (rms_sb, rms1),
                             (thirds_sb, thirds)):
                sl = tuple(slice(None) for _ in src.shape)
                sp.dma_start(dst[sl], src).then_inc(s_w, 16)
            at = 0
            for src in (bn1[1], bnf, bnl):
                n = src.shape[1]
                sp.dma_start(bn_sb[:, :, at:at + n], src[None, :, :].broadcast_to([P, 4, n])).then_inc(s_w, 16)
                at += n
            for i in range(2):
                sp.sem_inc(s_x1st[i], 16)
                sp.sem_inc(s_xnst[i], 128)

            def load(b, a, e):
                sp.dma_start(xin[:, e, :, :], tiles_of(x0v, b, a, e)).then_inc(s_in[e], 16)

            def four_steps(b, a, next_b, next_a):
                for e in range(4):
                    u = a * 4 + (b * HT + e)
                    if next_b < B:
                        sp.wait_ge(S["xt_ps"], u + 1)
                        sp.sem_inc(s_sp_passed, 1)
                        load(next_b, next_a, e)
                    sp.wait_ge(S["x1"], u + 1)
                    sp.sem_inc(s_sp_passed, 1)
                    sp.dma_start(tiles_of(x1v, b, a, e), x1_sb[:, e % 2, :, :]).then_inc(s_x1st[e % 2], 16)
                    sp.wait_ge(S["xn23"], u * 2 + 2)
                    sp.sem_inc(s_sp_passed, 1)
                    for o in range(4):
                        for t in range(2):
                            sp.dma_start(order_of(o, b, a, e, t), xn_sb[:, e % 2, o, :, t, :]).then_inc(s_xnst[e % 2], 16)

            for e in range(4):
                load(0, 0, e)
            for b in range(B):
                with sp.Fori(0, HT // 4 - 1) as a:
                    four_steps(b, a, b, a + 1)
                four_steps(b, HT // 4 - 1, b + 1, 0)
            for i in range(2):
                sp.wait_ge(s_x1st[i], 16 + 16 * U // 2)
                sp.wait_ge(s_xnst[i], 128 + 128 * U // 2)

        @block.gpsimd
        def _(pool):
            with pool.Fori(0, U // 2) as i:
                for par in range(2):
                    u = i * 2 + par
                    pool.wait_ge(S["xn0"], u * 2 + 4)
                    pool.wait_ge(S["xn1"], u + 1)
                    pool.sem_inc(s_passed, 1)
                    for o in range(2):
                        nc.gpsimd.tensor_copy(xn_sb[:, par, 2 + o, :, :, :],
                                              xn_sb[:, par, 1 - o, :, ::-1, ::-1]).then_inc(S["xn23"], 1)

        @block.scalar
        def _(act):
            act.wait_ge(s_fold, 2)
            nc.scalar.activation(scale[:, :], bn_sb[:, 3, :], ACT.Sqrt).then_inc(s_fsc, 1)
            nc.scalar.activation(shift_col[:, 0:1], bn1_col[:, 3:4], ACT.Sqrt).then_inc(s_fsc, 1)

            def turned(u):
                act.wait_ge(S["xt_ps"], u + 1)
                nc.scalar.copy(xt_sb[:, :, :, :], pT[:, :].rearrange("p (k t n) -> p k t n", k=KC, t=2)).then_inc(S["xt"], 1)

            turned(0)

            def body(u, par, half):
                if there(u, 0):
                    act.wait_ge(S["yt_ps"], u + 1)
                    nc.scalar.activation(yt_sb[:, par, :, :], pYT[:, 0:256].rearrange("p (t n) -> p t n", t=2), ACT.Relu,
                                         bias=shift_col[:, 3:4]).then_inc(S["yt"], 1)
                if there(u, -2):
                    act.wait_ge(S["xnt_ps"], u + -1)
                    act.wait_ge(s_xnst[par], half * 128)
                    pv = pT[:, :].rearrange("p (k t n) -> p k t n", k=KC, t=2)
                    for kc in range(KC):
                        nc.scalar.activation(xn_sb[:, par, 0, kc, :, :], pv[:, kc, :, :], ACT.Copy,
                                             scale=rms_sb[:, kc:kc + 1]).then_inc(S["xn0"], 1)
                if there(u, 0):
                    act.wait_ge(S["f_ps"], u + 1)
                    nc.scalar.copy(f_sb[:, :, :], pF[:, 0:4 * Z1].rearrange("p (t n) -> p t n", t=2)).then_inc(S["f"], 1)
                if there(u, -1):
                    act.wait_ge(S["x1_ps"], u)
                    act.wait_ge(s_x1st[1 - par], (half if par else half + -1) * 16 + 16)
                    nc.scalar.copy(x1_sb[:, 1 - par, :, :], pX[:, :].rearrange("p (t n) -> p t n", t=2)).then_inc(S["x1"], 1)
                    for t in range(2):
                        nc.scalar.activation(sq[:, t, :], pX[:, t * C:(t + 1) * C], ACT.Square,
                                             accum_out=ss[:, t:t + 1]).then_inc(S["ss"], 1)
                if there(u, 1):
                    turned(u + 1)
                if there(u, -1):
                    act.wait_ge(S["ms"], u)
                    nc.scalar.activation(rt[:, :], ms[:, :], ACT.Sqrt).then_inc(S["rt"], 1)
                if there(u, 0):
                    act.wait_ge(S["z_ps"], u + 1)
                    nc.scalar.activation(z_sb[:, :, :], pZ[0:Z1, :].rearrange("p (t n) -> p t n", t=2), ACT.Relu
                                         ).then_inc(S["z"], 1)

            rounds(act, body)

        @block.vector
        def _(dve):
            done = [0]

            def step(ins):
                done[0] += 1
                ins.then_inc(s_fold, 1)
                dve.wait_ge(s_fold, done[0])

            nc.vector.memset(ones_rows[:, :], 1.0).then_inc(s_ready, 1)
            dve.wait_ge(s_w, 16 * NW)
            nc.vector.tensor_scalar(bn1_col[:, 3:4], bn1_col[:, 3:4], 1e-3, None, ALU.add).then_inc(s_fold, 1)
            done[0] += 1
            step(nc.vector.tensor_scalar(bn_sb[:, 3, :], bn_sb[:, 3, :], 1e-3, None, ALU.add))
            dve.wait_ge(s_fsc, 2)
            step(nc.vector.reciprocal(scale[:, :], scale[:, :]))
            step(nc.vector.tensor_tensor(scale[:, :], scale[:, :], bn_sb[:, 0, :], ALU.mult))
            step(nc.vector.tensor_tensor(shift[:, :], scale[:, :], bn_sb[:, 2, :], ALU.mult))
            step(nc.vector.tensor_tensor(shift[:, :], bn_sb[:, 1, :], shift[:, :], ALU.subtract))
            step(nc.vector.tensor_copy(part16[:, :], shift[0:3, :]))
            step(nc.vector.scalar_tensor_tensor(shift_rest[:, :], part16[:, :], thirds_sb[:, 0:1], shift[0:3, :], ALU.mult, ALU.add))
            step(nc.vector.tensor_copy(part16[:, :], shift_rest[:, :]))
            step(nc.vector.scalar_tensor_tensor(shift3[:, :], part16[:, :], thirds_sb[:, 1:2], shift_rest[:, :], ALU.mult, ALU.add))
            step(nc.vector.reciprocal(shift_col[:, 1:2], shift_col[:, 0:1]))
            step(nc.vector.tensor_tensor(shift_col[:, 2:3], shift_col[:, 1:2], bn1_col[:, 0:1], ALU.mult))
            step(nc.vector.tensor_tensor(shift_col[:, 0:1], shift_col[:, 2:3], bn1_col[:, 2:3], ALU.mult))
            step(nc.vector.tensor_tensor(shift_col[:, 3:4], bn1_col[:, 1:2], shift_col[:, 0:1], ALU.subtract))
            for w, at, n in ((w1_sb, 0, HC), (fu_sb, HC, C), (lfu_sb, HC + C, C)):
                for k in range(2):
                    nc.vector.tensor_tensor(w[:, k, :], w[:, k, :], scale[:, at:at + n], ALU.mult).then_inc(s_ready, 1)

            def body(u, par, half):
                if there(u, 0):
                    dve.wait_ge(S["y_ps"], u + 1)
                    nc.vector.tensor_scalar(y_sb[:, :, :], pY[:, 0:256].rearrange("p (t n) -> p t n", t=2), 0.0, None,
                                            ALU.max).then_inc(S["y"], 1)
                if there(u, -1):
                    dve.wait_ge(S["o_ps"], u)
                    dve.wait_ge(S["yt"], u)
                    nc.vector.tensor_tensor(s_sb[:, :, :], yt_sb[:, 1 - par, :, :], pO[:, 0:256].rearrange("p (t n) -> p t n", t=2),
                                            ALU.add).then_inc(S["s"], 1)
                if there(u, 0):
                    dve.wait_ge(S["f_ps"], u + 1)
                    nc.vector.tensor_copy(fl_sb[:, :], pZL[:, C:C + 2 * Z2]).then_inc(S["fl"], 1)
                if there(u, -2):
                    dve.wait_ge(S["xn0"], u * 2)
                    nc.vector.tensor_copy(xn_sb[:, par, 1, :, :, :].rearrange("p k t (h n) -> p (k t h) n", n=W),
                                          xn_sb[:, par, 0, :, :, :].rearrange("p k t (h n) -> p (k t h) n", n=W)[:, :, ::-1]
                                          ).then_inc(S["xn1"], 1)
                if there(u, -1):
                    dve.wait_ge(S["ss"], u * 2)
                    nc.vector.tensor_scalar(ms[:, :], ss[:, :], 1.0 / C, 1e-5, ALU.mult, ALU.add).then_inc(S["ms"], 1)
                    dve.wait_ge(S["rt"], u)
                    nc.vector.reciprocal(rstd[:, :], rt[:, :]).then_inc(S["rstd"], 1)
                if there(u, 0):
                    dve.wait_ge(S["zl_ps"], u + 1)
                    nc.vector.tensor_scalar(zl_sb[:, :], pZL[0:Z2, 0:C], 0.0, None, ALU.max).then_inc(S["zl"], 1)
                if there(u, -1):
                    dve.wait_ge(S["rstd"], u)
                    dve.wait_ge(S["x1"], u)
                    for t in range(2):
                        nc.vector.tensor_scalar(xs_sb[:, t, :], x1_sb[:, 1 - par, t, :], rstd[:, t:t + 1], None, ALU.mult
                                                ).then_inc(S["xs"], 1)

            rounds(dve, body)

        @block.tensor
        def _(pe):
            pe.wait_ge(s_w, 16 * NW)
            pe.wait_ge(s_ready, 7)
            pe.sem_inc(S["xn0"], 2)

            def turn(u, buf, turns):
                pe.wait_ge(s_in[buf], turns * 16 + 16)
                for kc in range(KC):
                    for t in range(2):
                        at = (2 * kc + t) * P
                        mm = nc.tensor.transpose(pT[:, at:at + P], xin[:, buf, t, kc * P:(kc + 1) * P], ident_sb[:, :])
                mm.then_inc(S["xt_ps"], 1)

            def conv1(u):
                pe.wait_ge(S["xt"], u + 1)
                for t in range(2):
                    o = pY[:, t * HC:(t + 1) * HC]
                    for kc in range(KC):
                        nc.tensor.matmul(o, xt_sb[:, kc, t, :], w1_sb[:, kc, :], start=(kc == 0), stop=False)
                    mm = nc.tensor.matmul(o, ones_rows[:, :], shift3[:, 0:HC], start=False, stop=True)
                mm.then_inc(S["y_ps"], 1)
                if there(u, -1):
                    pe.wait_ge(S["yt"], u)
                for kc in range(KC):
                    mm = nc.tensor.matmul(pYT[:, 0:256].rearrange("p (t n) -> p t n", t=2), w1_sb[:, kc, :], xt_sb[:, kc, :, :],
                                          start=(kc == 0), stop=(kc == KC - 1))
                mm.then_inc(S["yt_ps"], 1)

            def turn_xn(n):
                pe.wait_ge(S["xs"], n * 2)
                for kc in range(KC):
                    for t in range(2):
                        at = (2 * kc + t) * P
                        mm = nc.tensor.transpose(pT[:, at:at + P], xs_sb[:, t, kc * P:(kc + 1) * P], ident_sb[:, :])
                mm.then_inc(S["xnt_ps"], 1)

            def inverse(n):
                pe.wait_ge(S["z"], n)
                pe.wait_ge(S["zl"], n)
                for t in range(2):
                    o = pO[:, t * P:(t + 1) * P]
                    for ri in range(2):
                        nc.tensor.matmul(o, z_sb[:, t, ri * HC:(ri + 1) * HC], idft_sb[:, ri, :], start=(ri == 0), stop=False)
                    for ri in range(2):
                        mm = nc.tensor.matmul(o, zl_sb[:, ri * HC:(ri + 1) * HC], idftl_sb[:, ri, :], start=False, stop=(ri == 1))
                mm.then_inc(S["o_ps"], 1)

            def transforms(u):
                pe.wait_ge(S["y"], u + 1)
                for t in range(2):
                    nc.tensor.matmul(pF[:, t * 2 * Z1:(t + 1) * 2 * Z1], y_sb[:, t, :], dft_sb[:, :], start=True, stop=True)
                for wq in range(2):
                    for hq in range(2):
                        r = 64 * wq + 32 * hq
                        mm = nc.tensor.matmul(pZL[r:r + HC // 4, C:C + 2 * Z2], y_sb[:, hq, 0:HC // 4],
                                              dftl_sb[:, wq, :], start=True, stop=True)
                mm.then_inc(S["f_ps"], 1)

            def conv2(n):
                pe.wait_ge(S["s"], n)
                for t in range(2):
                    mm = nc.tensor.matmul(pX[:, t * C:(t + 1) * C], s_sb[:, t, :], w2_sb[:, :], start=True, stop=True)
                mm.then_inc(S["x1_ps"], 1)

            def units(u):
                pe.wait_ge(S["f"], u + 1)
                for t in range(2):
                    o = pZ[0:Z1, t * C:(t + 1) * C]
                    for ri in range(2):
                        nc.tensor.matmul(o, f_sb[:, t, ri * Z1:(ri + 1) * Z1], fu_sb[:, ri, :], start=(ri == 0), stop=False)
                    mm = nc.tensor.matmul(o, ones_rows[:, 0:Z1], shift3[:, HC:HC + C], start=False, stop=True)
                mm.then_inc(S["z_ps"], 1)
                pe.wait_ge(S["fl"], u + 1)
                for ri in range(2):
                    nc.tensor.matmul(pZL[0:Z2, 0:C], fl_sb[:, ri * Z2:(ri + 1) * Z2], lfu_sb[:, ri, :], start=(ri == 0), stop=False)
                nc.tensor.matmul(pZL[0:Z2, 0:C], ones_rows[:, 0:Z2], shift3[:, HC + C:HC + 2 * C], start=False, stop=True
                                 ).then_inc(S["zl_ps"], 1)

            turn(0, 0, 0)

            def body(u, buf, turns):
                if there(u, 0):
                    conv1(u)
                if there(u, -2):
                    turn_xn(u + -1)
                if there(u, -1):
                    inverse(u)
                if there(u, 0):
                    transforms(u)
                if there(u, -1):
                    conv2(u)
                if there(u, 1):
                    if there(u, -2):
                        pe.wait_ge(S["xn0"], u * 2)
                    turn(u + 1, buf, turns)
                if there(u, 0):
                    units(u)

            def round_of(u):
                body(u, (u + 1) % 4, (u + 1) // 4)

            for u in range(2):
                round_of(u)
            with pe.Fori(0, (U - 4) // 4) as i:
                for j in range(4):
                    body(i * 4 + (2 + j), (3 + j) % 4, i + (3 + j) // 4)
            for u in range(U - 2, U + 2):
                round_of(u)


def mamba(nc, xn, w_inT, conv_w, conv_b, w_xT, split, w_dtT, b_dt, a_log, d_skip, w_outT, ident, pick, keep, out):
    NC = SEQS * CHUNKS
    STEPS = 2 * NS
    BCR = 96
    HS0, CONV0, OUT0, XP, GATE_A, DT0, GATE_B = 0, 4, 8, 10, 11, 12, 16
    G, GO = 19, 2
    FIRST = G - GO
    PIECES = {g: at for g, at in ([(HS0 + i, (i, 1)) for i in range(4)] + [(CONV0 + i, (4 + 2 * i, 2)) for i in range(4)]
                                  + [(OUT0 + i, (12 + 2 * i, 2)) for i in range(2)] + [(XP, (16, 2)), (GATE_A, (18, 1))]
                                  + [(DT0 + i, (19 + i, 1)) for i in range(4)] + [(GATE_B + i, (23 + 2 * i, 2)) for i in range(3)])}
    SILU_GATE_AT, SILU_AT, LN_AT, READ_AT = 6, 13, 24, 3
    DT_STEPS = (25, 26, 27, 28, 29, 30, 31, 31)
    AHEAD, CARRY_LAG = 3, 1
    SPREAD_AHEAD = 2
    HB, Y_LAG = 4, 3
    JOINED = (2, 5, 8, 11, 14)

    def adds(c, k):
        return c * (STEPS - len(JOINED)) + (k - sum(j <= k for j in JOINED))

    def joins(c, k):
        return c * len(JOINED) + sum(j < k for j in JOINED)


    def count(c, g):
        if isinstance(c, int) and c == 0:
            return FIRST + (g if g <= OUT0 else g - GO)
        return c * G + (g + 2 * FIRST - G)

    def issue_order(first, last):
        return [(at + i, g, i, n) for g, (at, n) in PIECES.items() for i in range(n)
                if not (first and OUT0 <= g < OUT0 + GO) and not (last and not OUT0 <= g < OUT0 + GO)]

    with ExitStack() as ctx:
        m = Pool_(nc, ctx, "mm")
        w_in = m.sb("w_in", [P, KC, 2 * I])
        taps, cw = m.sb("taps", [P, IB * TAPS, P]), m.sb("cw", [P, IB * TAPS])
        w_x, w_dt, w_out = m.sb("w_x", [P, IB, BCR + RK]), m.sb("w_dt", [P, I]), m.sb("w_out", [P, IB, C])
        cb_sb, bdt_sb, d_sb, ab_sb = m.sb("cb", [P, IB]), m.sb("bdt", [P, IB]), m.sb("d", [P, IB]), m.sb("ab", [P, 2])
        alog, a_sb = m.sb("alog", [P, IB * NS]), m.sb("a", [P, IB * NS])
        ident_sb, keep_sb = m.sb("ident", [P, P]), m.sb("keep", [P, NC + 1])
        keep_now = m.sb("keep_now", [P, 2])
        pick_sb = m.sb("pick", [BCR, 2 * NS, P], BF16)
        xn_sb = m.sb("xn", [P, 2, KC, T])
        hs = m.sb("hs", [P, IB, TAPS - 1 + T])
        u, gate = m.sb("u", [P, 2, IB, T]), m.sb("gate", [P, 2, IB, T])
        hi, mid, parts = m.sb("hi", [BCR, T], BF16), m.sb("mid", [BCR, T], BF16), m.sb("parts", [BCR, 2, T], BF16)
        rest = m.sb("rest", [BCR + RK, T])
        sp_e = m.sb("sp_e", [P, IB, T])
        dt, du = m.sb("dt", [P, 2, IB, T]), m.sb("du", [P, 2, IB, T])
        da = m.sb("da", [P, 4, 2, T])
        c_sb, bu, h, hc = m.sb("c", [P, 4, T]), m.sb("bu", [P, 2, 2, T]), m.sb("h", [P, 4, 2, T]), m.sb("hc", [P, HB, 2, T])
        carry = m.sb("carry", [P, 2, STEPS, 2])
        yg, out_sb = m.sb("yg", [P, IB, T]), m.sb("out", [P, 2, 2, C])
        p_b, p_c = m.ps("b", [P, 2, T]), m.ps("c", [P, 2, T])
        p_y, p_w = m.ps("y", [P, 2, T]), m.ps("w", [P, 2, T])

        s_w, s_prep, s_a, s_taps = m.sem("weights"), m.sem("a_exp"), m.sem("a"), m.sem("taps")
        s_zero = m.sem("zeroed")
        s_xn, s_st = ([m.sem(f"{k}{i}") for i in range(2)] for k in ("xn", "stored"))
        s_wk, s_wkf = m.sem("work_group"), m.sem("work_emptied")
        s_xpf, s_silu_gate = m.sem("bc_read"), m.sem("silu_gate")
        s_silu, s_parts, s_hi, s_softplus = m.sem("silu"), m.sem("parts"), m.sem("hi"), m.sem("softplus")
        s_tail, s_keep, s_sp1 = m.sem("tail"), m.sem("keep"), m.sem("softplus_exp")
        s_dt, s_du = m.sem("dt"), m.sem("du")
        s_bb, s_cb, s_cc, s_da = m.sem("b_spread"), m.sem("c_spread"), m.sem("c_copied"), m.sem("da")
        s_bu, s_scan, s_carry, s_hc, s_ys = m.sem("bu"), m.sem("scanned"), m.sem("carried"), m.sem("hc"), m.sem("y_added")
        s_join = m.sem("joined")
        s_yev, s_yg = m.sem("y_read"), m.sem("yg")
        block = ctx.enter_context(nc.Block())

        xnf = xn.rearrange("s h p k t -> p (s h) k t")
        outf = out.rearrange("s (h g p) c -> p (s h) g c", p=P, g=4)
        LOADS = ((w_in, w_inT.rearrange("(k p) o -> p k o", p=P)), (cw, conv_w), (w_x, w_xT.rearrange("(k p) o -> p k o", p=P)),
                 (w_out, w_outT.rearrange("(k p) o -> p k o", p=P)), (cb_sb, conv_b), (bdt_sb, b_dt), (d_sb, d_skip),
                 (ab_sb, split), (alog, a_log), (ident_sb, ident), (keep_sb, keep))

        NLOADS = len(LOADS) + 3

        def every_chunk(eng, body):
            body(0, 0, 0, True, False)
            with eng.Fori(0, (NC - 2) // 2) as i:
                body(i * 2 + 1, 1, i, False, False)
                body(i * 2 + 2, 0, i + 1, False, False)
            body(NC - 1, 1, NC // 2 - 1, False, True)

        def at_least(eng, sem, v):
            if not isinstance(v, int) or v > 0:
                eng.wait_ge(sem, v)

        @block.sync
        def _(sp):
            for dst, src in LOADS:
                sl = tuple(slice(None) for _ in src.shape)
                sp.dma_start(dst[sl], src).then_inc(s_w, 16)
            sp.dma_start(w_dt[BCR:BCR + RK, :], w_dtT).then_inc(s_w, 16)
            for i in range(2):
                sp.dma_start(du[0:BCR, i, :, :].rearrange("p a n -> p (a n)"), pick[:, i * NS:(i + 1) * NS, :].rearrange("p a n -> p (a n)")
                             ).then_inc(s_w, 16)
            for i in range(2):
                sp.sem_inc(s_st[i], 16)

            def load(c, par):
                src = xnf[:, bass.ds(c, 1), :, :].rearrange("p s k t -> p (s k) t")
                sp.dma_start(xn_sb[:, par, :, :], src).then_inc(s_xn[par], 16)

            def store(c):
                for g in range(2):
                    sp.wait_ge(s_wkf, count(NC - 1, 0) + (GO + g + 1) if isinstance(c, int) and c == NC - 1 else
                               count(NC - 1, 0) + (g + 1) if isinstance(c, int) and c == NC - 2 else count(c + 1, OUT0 + g + 1))
                    dst = outf[:, bass.ds(c, 1), 2 * g:2 * g + 2, :].rearrange("p s g c -> p (s g) c")
                    sp.dma_start(dst, out_sb[:, g, :, :]).then_inc(s_st[g], 16)

            load(0, 0)
            load(1, 1)
            sp.wait_ge(s_wk, FIRST)
            load(2, 0)
            sp.wait_ge(s_wk, count(0, G))
            load(3, 1)
            with sp.Fori(0, (NC - 4) // 2) as i:
                for j in range(2):
                    c = i * 2 + (1 + j)
                    store(i * 2 + j)
                    sp.wait_ge(s_wk, count(c, G))
                    load(i * 2 + (4 + j), j)
            for c in range(NC - 4, NC):
                store(c)
            for g in range(2):
                sp.wait_ge(s_st[g], 16 + 16 * NC)

        @block.tensor
        def _(pe):
            pe.wait_ge(s_w, 16 * NLOADS)
            pe.wait_ge(s_taps, IB * TAPS + 2)

            def wait_bank(c, g):
                if c is None:
                    n = g if g < OUT0 else g - GO
                    if n >= 2:
                        pe.wait_ge(s_wkf, n - 1)
                    if g >= XP + 2:
                        pe.wait_ge(s_xpf, 1)
                elif isinstance(c, int) and c == NC - 1:
                    pe.wait_ge(s_wkf, count(c, 0))
                else:
                    first = isinstance(c, int) and c == 0
                    n = count(c, 0) if g < 2 else count(c, OUT0) if first and g in (XP, XP + 1) else count(c, g - 2) + 1
                    pe.wait_ge(s_wkf, n)
                    if g >= XP + 2:
                        pe.wait_ge(s_xpf, c + 2)

            def products(c, pn, half, g):
                w = p_w[:, g % 2, :]
                if g < CONV0 or g == GATE_A or g >= GATE_B:
                    o = g if g < CONV0 else IB if g == GATE_A else IB + 1 + (g - GATE_B)
                    if g == 0:
                        pe.wait_ge(s_xn[pn], half * 16 + 16)
                    return [(w, w_in[:, kc, o * P:(o + 1) * P], xn_sb[:, pn, kc, :], kc == 0, kc == KC - 1) for kc in range(KC)]
                if g < OUT0:
                    cb = g - CONV0
                    if c is None:
                        pe.wait_ge(s_wkf, cb + 1)
                    else:
                        pe.wait_ge(s_wkf, count(c, cb) + 1)
                    return [(w, taps[:, cb * TAPS + k, :], hs[:, cb, k:k + T], k == 0, k == TAPS - 1) for k in range(TAPS)]
                if g < XP:
                    pe.wait_ge(s_yg, c * IB)
                    return [(w[:, t * C:(t + 1) * C], yg[:, cb, (2 * (g - OUT0) + t) * P:(2 * (g - OUT0) + t + 1) * P],
                             w_out[:, cb, :], cb == 0, cb == IB - 1) for t in range(2) for cb in range(IB)]
                if g == XP:
                    pe.wait_ge(s_silu, 1 if c is None else c + 2)
                    return [(w[0:BCR + RK, :], w_x[:, cb, :], u[:, pn, cb, :], cb == 0, cb == IB - 1) for cb in range(IB)]
                if g == DT0:
                    pe.wait_ge(s_wkf, XP - GO + 1 if c is None else count(c, XP) + 1)
                cb = g - DT0
                return [(w, w_dt[BCR:BCR + RK, cb * P:(cb + 1) * P], rest[BCR:BCR + RK, :], True, True)]

            def piece(c, pn, half, g, i, n):
                if i == 0:
                    wait_bank(c, g)
                todo = products(c, pn, half, g)
                per = len(todo) // n
                for o, a, b, start, stop in todo[i * per:(i + 1) * per]:
                    mm = nc.tensor.matmul(o, a, b, start=start, stop=stop)
                if i == n - 1:
                    mm.then_inc(s_wk, 1)

            def spread(c, p, k):
                K = c * STEPS + k
                n = k % NS
                if k == 0:
                    pe.wait_ge(s_parts, c + 1)
                pe.wait_ge(s_bu, K + 1)
                nc.tensor.matmul(p_b[:, k % 2, :], pick_sb[:, n, :], parts[:, p, :], start=True, stop=True).then_inc(s_bb, 1)
                pe.wait_ge(s_cc, K + 1)
                nc.tensor.matmul(p_c[:, k % 2, :], pick_sb[:, NS + n, :], parts[:, p, :], start=True, stop=True).then_inc(s_cb, 1)

            def add_y(c, k):
                if k + 1 in JOINED:
                    return
                K = c * STEPS + k
                if k % NS == 0:
                    pe.wait_ge(s_yev, c * 4 + (2 * (k // NS) + 2))
                if k in JOINED:
                    pe.wait_ge(s_join, joins(c, k) + 1)
                else:
                    pe.wait_ge(s_hc, K + 3)
                for j in range(2):
                    mm = nc.tensor.matmul(p_y[:, j, :], ident_sb[:, :], hc[:, k % HB, j, :],
                                          start=(k % NS == 0), stop=(k % NS == NS - 1))
                mm.then_inc(s_ys, 1)

            for g in PIECES:
                if not OUT0 <= g < XP:
                    piece(None, 0, 0, g, 0, 1)
            for k in range(SPREAD_AHEAD):
                spread(0, 0, k)

            def body(c, p, half, first, last):
                nhalf = half + 1 if p == 1 else half
                for k in range(STEPS):
                    if k + SPREAD_AHEAD < STEPS:
                        spread(c, p, k + SPREAD_AHEAD)
                    elif not last:
                        spread(c + 1, 1 - p, k + SPREAD_AHEAD - STEPS)
                    if k >= Y_LAG:
                        add_y(c, k - Y_LAG)
                    elif not first:
                        add_y(c + -1, STEPS + k - Y_LAG)
                    for at, g, i, n in issue_order(first, last):
                        if at == k:
                            piece(c, 1 - p, nhalf, g, i, n)

            every_chunk(pe, body)
            for k in range(Y_LAG):
                add_y(NC - 1, STEPS + k - Y_LAG)
            for g in range(GO):
                pe.wait_ge(s_wkf, count(NC - 1, 0) + GO)
                pe.wait_ge(s_yg, NC * IB)
                for o, a, b, start, stop in products(NC, 0, 0, OUT0 + g):
                    mm = nc.tensor.matmul(o, a, b, start=start, stop=stop)
                mm.then_inc(s_wk, 1)

        @block.scalar
        def _(act):
            act.wait_ge(s_w, 16 * NLOADS)
            act.sem_inc(s_cc, 2)
            nc.scalar.activation(alog[:, :], alog[:, :], ACT.Exp).then_inc(s_prep, 1)
            act.wait_ge(s_prep, 1)
            nc.scalar.mul(a_sb[:, :], alog[:, :], -1.0).then_inc(s_a, 1)
            act.wait_ge(s_a, 1)

            def empty(c, pn, g):
                act.wait_ge(s_wk, (g if g < OUT0 else g - GO) + 1 if c is None else count(c, g) + 1)
                w = p_w[:, g % 2, :]
                if g < CONV0:
                    nc.scalar.copy(hs[:, g, TAPS - 1:], w).then_inc(s_wkf, 1)
                elif g == GATE_A or g >= GATE_B:
                    cb = 0 if g == GATE_A else g - GATE_B + 1
                    nc.scalar.copy(gate[:, pn, cb, :], w).then_inc(s_wkf, 1)
                elif g < OUT0:
                    cb = g - CONV0
                    nc.scalar.activation(u[:, pn, cb, :], w, ACT.Identity, bias=cb_sb[:, cb:cb + 1]).then_inc(s_wkf, 1)
                elif g == XP:
                    nc.scalar.copy(rest[BCR:BCR + RK, :], p_w[BCR:BCR + RK, g % 2, :]).then_inc(s_wkf, 1)
                else:
                    cb = g - DT0
                    if cb == 0 and c is not None:
                        act.wait_ge(s_dt, c * IB + IB)
                    nc.scalar.activation(dt[:, pn, cb, :], w, ACT.Relu, bias=bdt_sb[:, cb:cb + 1])
                    nc.scalar.activation(sp_e[:, cb, :], w, ACT.Abs, bias=bdt_sb[:, cb:cb + 1]).then_inc(s_wkf, 1)

            def empty_output(c, g, n):
                act.wait_ge(s_wk, n + 1)
                act.wait_ge(s_st[g], c * 16 + 16)
                nc.scalar.copy(out_sb[:, g, :, :], p_w[:, g % 2, :].rearrange("p (t n) -> p t n", t=2)).then_inc(s_wkf, 1)

            def tail(c, pn):
                nc.scalar.activation(hs[:, :, 0:TAPS - 1], hs[:, :, T:T + TAPS - 1], ACT.Copy,
                                     scale=keep_now[:, pn:pn + 1]).then_inc(s_tail, 1)
                act.wait_ge(s_tail, c + 1)

            def silu_u(c, pn):
                act.wait_ge(s_wkf, OUT0 if c is None else count(c, OUT0))
                nc.scalar.activation(u[:, pn, :, :], u[:, pn, :, :], ACT.Silu).then_inc(s_silu, 1)

            def silu_gate(c, p):
                act.wait_ge(s_wkf, count(c, 0))
                nc.scalar.activation(gate[:, p, :, :], gate[:, p, :, :], ACT.Silu).then_inc(s_silu_gate, 1)

            def softplus_exp(c, cb):
                act.wait_ge(s_wkf, DT0 - GO + cb + 1 if c is None else count(c, DT0 + cb) + 1)
                nc.scalar.activation(sp_e[:, cb, :], sp_e[:, cb, :], ACT.Exp, scale=-1.0).then_inc(s_sp1, 1)

            def softplus_ln(c):
                act.wait_ge(s_sp1, IB if c is None else c * IB + 2 * IB)
                nc.scalar.activation(sp_e[:, :, :], sp_e[:, :, :], ACT.Ln, bias=1.0).then_inc(s_softplus, 1)

            def copy_c(c, k):
                K = c * STEPS + k
                act.wait_ge(s_cb, K + 1)
                at_least(act, s_hc, K + -1)
                nc.scalar.copy(c_sb[:, k % 4, :], p_c[:, k % 2, :]).then_inc(s_cc, 1)

            def decay(c, p, k):
                K = c * STEPS + k
                if k % NS == 0:
                    act.wait_ge(s_dt, c * IB + (2 if k == 0 else 4))
                at_least(act, s_scan, K * 2 + -4)
                for j in range(2):
                    cb = 2 * (k // NS) + j
                    nc.scalar.activation(da[:, k % 4, j, :], dt[:, p, cb, :], ACT.Exp,
                                         scale=a_sb[:, cb * NS + k % NS:cb * NS + k % NS + 1]).then_inc(s_da, 1)

            def carry_on(c, p, k):
                act.wait_ge(s_scan, (c * STEPS + k) * 2 + 4)
                nc.scalar.activation(carry[:, 1 - p, k, :], h[:, k % 4, :, T - 1], ACT.Copy,
                                     scale=keep_now[:, 1 - p:2 - p]).then_inc(s_carry, 1)

            act.wait_ge(s_zero, 2)
            for g in PIECES:
                if not OUT0 <= g < XP:
                    empty(None, 0, g)
                if g == OUT0 - 1:
                    silu_u(None, 0)
            for cb in range(IB):
                softplus_exp(None, cb)
            softplus_ln(None)
            for k in range(SPREAD_AHEAD):
                copy_c(0, k)
            for k in range(AHEAD):
                decay(0, 0, k)

            def body(c, p, half, first, last):
                nc.scalar.copy(keep_now[:, 1 - p:2 - p], keep_sb[:, bass.ds(c + 1, 1)]).then_inc(s_keep, 1)
                act.wait_ge(s_keep, c + 1)
                for k in range(STEPS):
                    if k + SPREAD_AHEAD < STEPS:
                        copy_c(c, k + SPREAD_AHEAD)
                    elif not last:
                        copy_c(c + 1, k + SPREAD_AHEAD - STEPS)
                    if k + AHEAD < STEPS:
                        decay(c, p, k + AHEAD)
                    elif not last:
                        decay(c + 1, 1 - p, k + AHEAD - STEPS)
                    if k >= CARRY_LAG:
                        carry_on(c, p, k - CARRY_LAG)
                    elif not first:
                        carry_on(c + -1, 1 - p, STEPS + k - CARRY_LAG)
                    if k == 0 and not last:
                        tail(c, 1 - p)
                    for at, g, i, n in issue_order(first, last):
                        if at + 1 == k and i == n - 1:
                            if OUT0 <= g < XP:
                                empty_output(c + -1, g - OUT0, count(c, 0) + (g - OUT0) if last else count(c, g))
                            else:
                                empty(c, 1 - p, g)
                            if DT0 < g < GATE_B:
                                softplus_exp(c, g - DT0 - 1)
                    if k == SILU_GATE_AT:
                        silu_gate(c, p)
                    if not last:
                        if k == SILU_AT:
                            silu_u(c, 1 - p)
                        if k == LN_AT:
                            softplus_exp(c, IB - 1)
                            softplus_ln(c)

            every_chunk(act, body)
            for g in range(GO):
                empty_output(NC - 1, g, count(NC - 1, 0) + (GO + g))

        @block.vector
        def _(dve):
            dve.wait_ge(s_w, 16 * NLOADS)
            for i in range(IB * TAPS):
                nc.vector.tensor_scalar(taps[:, i, :], ident_sb[:, :], cw[:, i:i + 1], None, ALU.mult).then_inc(s_taps, 1)
            for i in range(2):
                nc.vector.tensor_copy(pick_sb[:, i * NS:(i + 1) * NS, :].rearrange("p a n -> p (a n)"),
                                      du[0:BCR, i, :, :].rearrange("p a n -> p (a n)")).then_inc(s_taps, 1)
            nc.vector.memset(hs[:, :, 0:TAPS - 1], 0.0).then_inc(s_zero, 1)
            nc.vector.memset(carry[:, 0, :, :], 0.0).then_inc(s_zero, 1)
            dve.wait_ge(s_zero, 2)
            dve.sem_inc(s_bu, 2)
            dve.sem_inc(s_scan, 2)
            dve.sem_inc(s_yev, 2)
            dve.sem_inc(s_carry, STEPS)

            def split_bc(c, pn):
                dve.wait_ge(s_wk, XP - GO + 1 if c is None else count(c, XP) + 1)
                w = p_w[0:BCR, XP % 2, :]
                nc.vector.tensor_copy(hi[:, :], w).then_inc(s_hi, 1)
                n = 0 if c is None else c * 2 + 2
                dve.wait_ge(s_hi, n + 1)
                nc.vector.scalar_tensor_tensor(rest[0:BCR, :], hi[:, :], ab_sb[0:BCR, 0:1], w, ALU.mult, ALU.add).then_inc(s_xpf, 1)
                dve.wait_ge(s_xpf, 1 if c is None else c + 2)
                nc.vector.tensor_copy(mid[:, :], rest[0:BCR, :]).then_inc(s_hi, 1)
                dve.wait_ge(s_hi, n + 2)
                nc.vector.scalar_tensor_tensor(parts[:, pn, :], mid[:, :], ab_sb[0:BCR, 1:2], rest[0:BCR, :], ALU.mult, ALU.add
                                               ).then_inc(s_parts, 1)

            def times_b(c, p, k):
                K = c * STEPS + k
                if k % NS == 0:
                    dve.wait_ge(s_du, c * IB + (2 if k == 0 else 4))
                q = k // NS
                dve.wait_ge(s_bb, K + 1)
                at_least(dve, s_scan, K * 2)
                nc.vector.tensor_tensor(bu[:, k % 2, :, :], du[:, p, 2 * q:2 * q + 2, :],
                                        p_b[:, k % 2:k % 2 + 1, :].broadcast_to([P, 2, T]), ALU.mult).then_inc(s_bu, 1)

            def scan(c, p, k):
                K = c * STEPS + k
                dve.wait_ge(s_bu, K + 3)
                dve.wait_ge(s_carry, K + (STEPS - 3))
                at_least(dve, s_hc, K + -1)
                for j in range(2):
                    dve.wait_ge(s_da, K * 2 + (j + 1))
                    nc.vector.tensor_tensor_scan(h[:, k % 4, j, :], da[:, k % 4, j, :], bu[:, k % 2, j, :], carry[:, p, k, j:j + 1],
                                                 ALU.mult, ALU.add).then_inc(s_scan, 1)

            def read_y(c, p, q):
                dve.wait_ge(s_ys, adds(c, NS * (q + 1)) + 2)
                if q == 0 and not (isinstance(c, int) and c == 0):
                    dve.wait_ge(s_wk, count(c, 0) + GO if isinstance(c, int) and c == NC - 1 else count(c, XP))
                for j in range(2):
                    cb = 2 * q + j
                    nc.vector.scalar_tensor_tensor(yg[:, cb, :], u[:, p, cb, :], d_sb[:, cb:cb + 1], p_y[:, j, :],
                                                   ALU.mult, ALU.add).then_inc(s_yev, 1)

            split_bc(None, 0)
            times_b(0, 0, 0)

            def body(c, p, half, first, last):
                for k in range(STEPS):
                    if k == READ_AT and not first:
                        read_y(c + -1, 1 - p, 1)
                    if k == NS + READ_AT:
                        read_y(c, p, 0)
                    if k + 1 < STEPS:
                        times_b(c, p, k + 1)
                    elif not last:
                        times_b(c + 1, 1 - p, 0)
                    scan(c, p, k)
                    if k == PIECES[XP][0] + PIECES[XP][1] and not last:
                        split_bc(c, 1 - p)

            every_chunk(dve, body)
            read_y(NC - 1, 1, 1)

        @block.gpsimd
        def _(pool):
            pool.sem_inc(s_hc, 2)
            pool.sem_inc(s_ys, 2)

            def dt_step(c, par, i):
                cb = i // 2
                if i % 2 == 0:
                    pool.wait_ge(s_softplus, c + 1)
                    nc.gpsimd.tensor_tensor(dt[:, par, cb, :], dt[:, par, cb, :], sp_e[:, cb, :], ALU.add).then_inc(s_dt, 1)
                else:
                    pool.wait_ge(s_dt, c * IB + (cb + 1))
                    nc.gpsimd.tensor_tensor(du[:, par, cb, :], dt[:, par, cb, :], u[:, par, cb, :], ALU.mult).then_inc(s_du, 1)

            def times_c(c, k):
                K = c * STEPS + k
                pool.wait_ge(s_scan, K * 2 + 4)
                pool.wait_ge(s_cc, K + 3)
                before = k - HB
                if (before + 1) % STEPS in JOINED:
                    pool.wait_ge(s_join, joins(c, before + 2) if before + 2 > 0 else c * len(JOINED))
                elif before >= 0 or not (isinstance(c, int) and c == 0):
                    pool.wait_ge(s_ys, adds(c, before + 1) + 2)
                nc.gpsimd.tensor_tensor(hc[:, k % HB, :, :], h[:, k % 4, :, :],
                                        c_sb[:, k % 4:k % 4 + 1, :].broadcast_to([P, 2, T]), ALU.mult).then_inc(s_hc, 1)
                if k in JOINED:
                    pool.wait_ge(s_hc, K + 3)
                    nc.gpsimd.tensor_tensor(hc[:, k % HB, :, :], hc[:, k % HB, :, :], hc[:, (k - 1) % HB, :, :], ALU.add).then_inc(s_join, 1)

            def gate_y(c, p, q, j):
                pool.wait_ge(s_silu_gate, c + 1)
                pool.wait_ge(s_yev, c * 4 + (2 * q + 4))
                cb = 2 * q + j
                nc.gpsimd.tensor_tensor(yg[:, cb, :], yg[:, cb, :], gate[:, p, cb, :], ALU.mult).then_inc(s_yg, 1)

            for i in range(len(DT_STEPS)):
                dt_step(0, 0, i)

            def body(c, p, half, first, last):
                for k in range(STEPS):
                    times_c(c, k)
                    for j in range(2):
                        if k == READ_AT + 1 + j and not first:
                            gate_y(c + -1, 1 - p, 1, j)
                        if k == NS + READ_AT + 1 + j:
                            gate_y(c, p, 0, j)
                    for i, at in enumerate(DT_STEPS):
                        if at == k and not last:
                            dt_step(c + 1, 1 - p, i)

            every_chunk(pool, body)
            for j in range(2):
                gate_y(NC - 1, 1, 1, j)


def combine_and_whiten(nc, mix, x1, flips, wf, ln_w, ln_b, ident, blocks, gamma, beta, out):
    NT = B * TILES
    ORD = 4
    ITERS = 26
    ROWS = float(B * N)
    with ExitStack() as outer:
        mo = Pool_(nc, outer, "cw")
        x2 = mo.sb("x2", [P, NT, C])
        ident_sb, ones = mo.sb("ident", [P, P]), mo.sb("ones", [P, P])
        mean_sb = mo.sb("mean", [P, C])
        p_sum = mo.ps("sum", [P, 512])
        with ExitStack() as ctx:
            m = Pool_(nc, ctx, "co")
            flip_sb, wf_sb, wf4 = m.sb("flips", [P, ORD - 1, P]), m.sb("wf", [P, C]), m.sb("wf4", [P, C])
            lw_sb, lb_sb = m.sb("lw", [P, C]), m.sb("lb", [P, C])
            xo = m.sb("xo", [P, 4, ORD + 1, C])
            h0, acc, y = m.sb("h0", [P, 2, C]), m.sb("acc", [P, 4, C]), m.sb("y", [P, 4, C])
            sq, ss, ms, rt, rs = (m.sb(k, [P, 4, 4] if k != "sq" else [P, 4, C]) for k in ("sq", "ss", "ms", "rt", "rs"))
            stats, mv = m.sb("stats", [P, 4, 6]), m.sb("mv", [P, 4, 2])
            ve, rt2, rs2, cen = m.sb("ve", [P, 4]), m.sb("rt2", [P, 4]), m.sb("rs2", [P, 4]), m.sb("cen", [P, 2, C])
            p_h = m.ps("h", [P, 2, 4, C])

            s_w, s_prep, s_passed = m.sem("weights"), m.sem("prepared"), m.sem("dve_passed")
            s_in = [m.sem(f"loaded{i}") for i in range(4)]
            s_g, s_h0, s_ss, s_ms, s_rt, s_rs = (m.sem(k) for k in ("h_summed", "h0", "squares", "ms", "root", "recip"))
            s_acc, s_y, s_bn, s_mv, s_ve = (m.sem(k) for k in ("acc", "y", "stats", "mean_var", "var_eps"))
            s_rt2, s_rs2, s_cen, s_x2, s_sum = (m.sem(k) for k in ("root2", "recip2", "centred", "x2", "summed"))
            block = ctx.enter_context(nc.Block())

            mv_dram = mix.rearrange("(o b) (t p) c -> p o (b t) c", p=P, b=B)
            x1_dram = x1.rearrange("b (t p) c -> p (b t) c", p=P)
            LOADS = ((flip_sb, flips), (wf_sb, wf), (lw_sb, ln_w), (lb_sb, ln_b), (ident_sb, ident))

            def every_tile(body):
                def run(eng):
                    body(0, 0, 0)
                    body(1, 1, 0)
                    with eng.Fori(0, (NT - 4) // 4) as i:
                        for j in range(4):
                            body(i * 4 + (2 + j), (2 + j) % 4, i + (2 + j) // 4)
                    body(NT - 2, 2, NT // 4 - 1)
                    body(NT - 1, 3, NT // 4 - 1)
                return run

            def inside(n, lo, hi):
                return not isinstance(n, int) or (n - lo >= 0 and n + hi < NT)

            @block.sync
            def _(sp):
                for dst, src in LOADS:
                    sl = tuple(slice(None) for _ in src.shape)
                    sp.dma_start(dst[sl], src).then_inc(s_w, 16)
                sp.sem_inc(s_g, 4)
                sp.sem_inc(s_h0, 4)
                with sp.Fori(0, B) as b:
                    with sp.Fori(0, TILES // 4) as i:
                        for j in range(4):
                            n = b * TILES + i * 4 + j
                            back = b * TILES + i * -4 + (TILES - 1 - j)
                            sp.wait_ge(s_g, n + 1)
                            sp.wait_ge(s_h0, n + 1)
                            for o, t in ((0, n), (2, back)):
                                sp.dma_start(xo[:, j, o:o + 2, :], mv_dram[:, o:o + 2, bass.ds(t, 1), :].rearrange("p o t c -> p o (t c)")
                                             ).then_inc(s_in[j], 16)
                            sp.dma_start(xo[:, j, 4, :], x1_dram[:, bass.ds(n, 1), :].rearrange("p t c -> p (t c)")
                                         ).then_inc(s_in[j], 16)

            @block.tensor
            def _(pe):
                pe.wait_ge(s_w, 16 * len(LOADS))
                pe.wait_ge(s_prep, 2)

                def gather(n, r, quarter):
                    pe.wait_ge(s_in[r], quarter * 48 + 48)
                    pe.wait_ge(s_acc, n * 4 + 4)
                    for o in range(1, ORD):
                        dst = p_h[:, r % 2, o - 1, :]
                        nc.tensor.matmul(dst, flip_sb[:, o - 1, :], xo[:, r, o, :], start=True, stop=False)
                        mm = nc.tensor.matmul(dst, ident_sb[:, :], xo[:, r, 4, :], start=False, stop=True)
                    mm.then_inc(s_g, 1)

                def column_sums(n, first, last):
                    pe.wait_ge(s_x2, n + 1)
                    nc.tensor.matmul(p_sum[:, 0:C], ones[:, :], x2[:, bass.ds(n, 1), :].rearrange("p t c -> p (t c)"),
                                     start=first, stop=last, skip_group_check=True).then_inc(s_sum, 1)

                gather(0, 0, 0)

                def body(n, r, quarter):
                    if inside(n, 0, 1):
                        gather(n + 1, (r + 1) % 4, quarter + (r + 1) // 4)
                    if inside(n, 3, 0):
                        column_sums(n + -3, isinstance(n, int) and n == 3, False)

                for n in range(4):
                    body(n, n % 4, 0)
                with pe.Fori(0, (NT - 8) // 4) as i:
                    for j in range(4):
                        body(i * 4 + (4 + j), j, i + 1)
                for n in range(NT - 4, NT):
                    body(n, n % 4, NT // 4 - 1)
                for n in range(NT - 3, NT):
                    column_sums(n, False, n == NT - 1)

            @block.vector
            def _(dve):
                nc.vector.memset(ones[:, :], 1.0).then_inc(s_prep, 1)
                dve.wait_ge(s_w, 16 * len(LOADS))
                nc.vector.tensor_scalar(wf4[:, :], wf_sb[:, :], 1.0 / ORD, None, ALU.mult).then_inc(s_prep, 1)
                dve.sem_inc(s_acc, 8)

                def scale_sum(n, r, o):
                    if o == 0:
                        dve.wait_ge(s_rt, n + 1)
                        nc.vector.reciprocal(rs[:, r, :], rt[:, r, :]).then_inc(s_rs, 1)
                        dve.wait_ge(s_rs, n + 1)
                        dve.wait_ge(s_h0, n + 5)
                        dve.wait_ge(s_g, n + 5)
                        nc.vector.tensor_scalar(acc[:, r, :], h0[:, r % 2, :], rs[:, r, 0:1], None, ALU.mult).then_inc(s_acc, 1)
                    else:
                        dve.wait_ge(s_acc, n * 4 + (8 + o))
                        nc.vector.scalar_tensor_tensor(acc[:, r, :], p_h[:, r % 2, o - 1, :], rs[:, r, o:o + 1], acc[:, r, :],
                                                       ALU.mult, ALU.add).then_inc(s_acc, 1)

                def statistics(n, r):
                    dve.wait_ge(s_y, n + 1)
                    nc.vector.bn_stats(stats[:, r, :], y[:, r, :]).then_inc(s_bn, 1)

                def mean_variance(n, r):
                    dve.wait_ge(s_bn, n + 1)
                    dve.sem_inc(s_passed, 1)
                    nc.vector.bn_aggr(mv[:, r, :], stats[:, r, :]).then_inc(s_mv, 1)

                def variance_eps(n, r):
                    dve.wait_ge(s_mv, n + 1)
                    nc.vector.tensor_scalar(ve[:, r:r + 1], mv[:, r, 1:2], 1e-5, None, ALU.add).then_inc(s_ve, 1)

                def centre(n, r):
                    dve.wait_ge(s_rt2, n + 1)
                    nc.vector.reciprocal(rs2[:, r:r + 1], rt2[:, r:r + 1]).then_inc(s_rs2, 1)
                    nc.vector.scalar_tensor_tensor(cen[:, r % 2, :], y[:, r, :], mv[:, r, 0:1], lw_sb[:, :], ALU.subtract, ALU.mult
                                                   ).then_inc(s_cen, 1)

                def layer_norm(n, r):
                    dve.wait_ge(s_rs2, n + 1)
                    dve.wait_ge(s_cen, n + 1)
                    nc.vector.scalar_tensor_tensor(x2[:, bass.ds(n, 1), :].rearrange("p t c -> p (t c)"), cen[:, r % 2, :],
                                                   rs2[:, r:r + 1], lb_sb[:, :], ALU.mult, ALU.add).then_inc(s_x2, 1)

                def mean_square(n, r):
                    dve.wait_ge(s_ss, n * 4 + 4)
                    nc.vector.tensor_scalar(ms[:, r, :], ss[:, r, :], 1.0 / C, 1e-5, ALU.mult, ALU.add).then_inc(s_ms, 1)

                mean_square(0, 0)

                def body(n, r, quarter):
                    scale_sum(n, r, 0)
                    if inside(n, 1, 0):
                        statistics(n + -1, (r - 1) % 4)
                    scale_sum(n, r, 1)
                    if inside(n, 2, 0):
                        centre(n + -2, (r - 2) % 4)
                    scale_sum(n, r, 2)
                    if inside(n, 1, 0):
                        mean_variance(n + -1, (r - 1) % 4)
                    scale_sum(n, r, 3)
                    if inside(n, 1, 0):
                        variance_eps(n + -1, (r - 1) % 4)
                    if inside(n, 0, 1):
                        mean_square(n + 1, (r + 1) % 4)
                    if inside(n, 2, 0):
                        layer_norm(n + -2, (r - 2) % 4)

                every_tile(body)(dve)
                statistics(NT - 1, 3)
                mean_variance(NT - 1, 3)
                variance_eps(NT - 1, 3)
                for n in (NT - 2, NT - 1):
                    centre(n, n % 4)
                    layer_norm(n, n % 4)
                dve.wait_ge(s_sum, NT)
                nc.vector.tensor_scalar(mean_sb[:, :], p_sum[:, 0:C], 1.0 / ROWS, None, ALU.mult).then_inc(s_sum, 1)

            @block.scalar
            def _(act):
                def squares(n, r):
                    act.wait_ge(s_h0, n + 5)
                    act.wait_ge(s_g, n + 5)
                    for o in range(ORD):
                        src = h0[:, r % 2, :] if o == 0 else p_h[:, r % 2, o - 1, :]
                        nc.scalar.activation(sq[:, o, :], src, ACT.Square, accum_out=ss[:, r, o:o + 1]).then_inc(s_ss, 1)

                def root(n, r):
                    act.wait_ge(s_ms, n + 1)
                    nc.scalar.activation(rt[:, r, :], ms[:, r, :], ACT.Sqrt).then_inc(s_rt, 1)

                def root2(n, r):
                    act.wait_ge(s_ve, n + 1)
                    nc.scalar.activation(rt2[:, r:r + 1], ve[:, r:r + 1], ACT.Sqrt).then_inc(s_rt2, 1)

                squares(0, 0)
                root(0, 0)

                def body(n, r, quarter):
                    if inside(n, 0, 1):
                        squares(n + 1, (r + 1) % 4)
                    if inside(n, 1, 0):
                        root2(n + -1, (r - 1) % 4)
                    if inside(n, 0, 1):
                        root(n + 1, (r + 1) % 4)

                every_tile(body)(act)
                root2(NT - 1, 3)

            @block.gpsimd
            def _(pool):
                pool.wait_ge(s_prep, 2)

                def add_residual(n, r, quarter):
                    pool.wait_ge(s_in[r], quarter * 48 + 48)
                    pool.wait_ge(s_acc, n * 4 + 4)
                    nc.gpsimd.tensor_tensor(h0[:, r % 2, :], xo[:, r, 0, :], xo[:, r, 4, :], ALU.add).then_inc(s_h0, 1)

                add_residual(0, 0, 0)
                add_residual(1, 1, 0)

                def body(n, r, quarter):
                    pool.wait_ge(s_acc, n * 4 + 12)
                    nc.gpsimd.tensor_tensor(y[:, r, :], acc[:, r, :], wf4[:, :], ALU.mult).then_inc(s_y, 1)
                    if inside(n, 0, 2):
                        add_residual(n + 2, (r + 2) % 4, quarter + (r + 2) // 4)

                every_tile(body)(pool)

        with ExitStack() as ctx:
            m = Pool_(nc, ctx, "wh")
            mask_sb, g_sb, b_sb = m.sb("mask", [P, P]), m.sb("gamma", [P, C]), m.sb("beta", [P, C])
            cov, diag = m.sb("cov", [P, KC, P]), m.sb("diag", [P, KC])
            tr, itr, rtr = m.sb("trace", [P, KC]), m.sb("itrace", [P, KC]), m.sb("rtrace", [P, KC])
            i15 = m.sb("i15", [P, P])
            Y, Z, Wm = m.sb("Y", [P, 2, KC, 2, P]), m.sb("Z", [P, 2, KC, 2, P]), m.sb("W", [P, KC, 2, P])
            proj = m.sb("proj", [P, KC, P])
            cT = m.sb("cT", [P, 2, 2, KC, P])
            o_sb = m.sb("o", [P, 4, 2, C])
            p_cov = [m.ps(f"cov{i}", [P, 512]) for i in range(2)]
            p_t, p_o = m.ps("t", [P, 2, 512]), m.ps("o", [P, 2, 512])

            s_w, s_c, s_cov, s_prep = m.sem("weights"), m.sem("centred"), m.sem("covariance"), m.sem("step")
            s_tr, s_rt = m.sem("trace"), m.sem("root")
            s_zy, s_wm, s_yz, s_new = ([m.sem(f"{k}{i}") for i in range(KC)] for k in ("zy", "w", "yz", "new"))
            s_t, s_ct, s_o, s_ob = m.sem("turned"), m.sem("turned_copied"), m.sem("whitened"), m.sem("out_ready")
            s_proj = m.sem("proj")
            s_st = [m.sem(f"stored{i}") for i in range(4)]
            block = ctx.enter_context(nc.Block())
            LOADS = ((mask_sb, blocks), (g_sb, gamma), (b_sb, beta))
            CH = 8
            out_dram = out.rearrange("b (t p) c -> p (b t) c", p=P)

            @block.sync
            def _(sp):
                for dst, src in LOADS:
                    sp.dma_start(dst[:, :], src).then_inc(s_w, 16)
                for n in range(NT // 2):
                    sp.wait_ge(s_ob, n + 1)
                    sp.dma_start(out_dram[:, 2 * n:2 * n + 2, :], o_sb[:, n % 4, :, :]).then_inc(s_st[n % 4], 16)
                for i in range(4):
                    sp.wait_ge(s_st[i], 16 * NT // 8)

            @block.tensor
            def _(pe):
                for t in range(NT):
                    pe.wait_ge(s_c, t // CH + 1)
                    for kc in range(KC):
                        blk = x2[:, t, kc * P:(kc + 1) * P]
                        mm = nc.tensor.matmul(p_cov[kc][:, 0:P], blk, blk, start=(t == 0), stop=(t == NT - 1))
                mm.then_inc(s_cov, 1)
                pe.wait_ge(s_prep, 8)
                nc.tensor.matmul(p_t[:, 0, 0:KC], mask_sb[:, :], diag[:, :], start=True, stop=True).then_inc(s_tr, 1)
                for it in range(ITERS):
                    a = it % 2
                    for kc in range(KC):
                        pe.wait_ge(s_new[kc], 2 * it + 2)
                        nc.tensor.matmul(p_cov[kc][:, 0:P], Z[:, a, kc, 1, :], Y[:, a, kc, 0, :], start=True, stop=True)
                        nc.tensor.matmul(p_cov[kc][:, P:2 * P], Y[:, a, kc, 0, :], Z[:, a, kc, 1, :], start=True, stop=True).then_inc(s_zy[kc], 1)
                    for kc in range(KC):
                        pe.wait_ge(s_wm[kc], it + 1)
                        nc.tensor.matmul(p_t[:, kc, 0:P], Y[:, a, kc, 1, :], Wm[:, kc, 0, :], start=True, stop=True)
                        nc.tensor.matmul(p_t[:, kc, P:2 * P], Wm[:, kc, 0, :], Y[:, a, kc, 1, :], start=True, stop=True).then_inc(s_yz[kc], 1)
                        nc.tensor.matmul(p_o[:, kc, 0:P], Wm[:, kc, 1, :], Z[:, a, kc, 0, :], start=True, stop=True)
                        nc.tensor.matmul(p_o[:, kc, P:2 * P], Z[:, a, kc, 0, :], Wm[:, kc, 1, :], start=True, stop=True).then_inc(s_yz[kc], 1)
                pe.wait_ge(s_proj, KC)

                def turn(n):
                    if n >= 2:
                        pe.wait_ge(s_ct, n - 1)
                    for t in range(2):
                        for kc in range(KC):
                            at = (2 * t + kc) * P
                            mm = nc.tensor.transpose(p_t[:, n % 2, at:at + P], x2[:, 2 * n + t, kc * P:(kc + 1) * P], ident_sb[:, :])
                    mm.then_inc(s_t, 1)

                turn(0)
                for n in range(NT // 2):
                    if n + 1 < NT // 2:
                        turn(n + 1)
                    pe.wait_ge(s_ct, n + 1)
                    if n >= 2:
                        pe.wait_ge(s_ob, n - 1)
                    for t in range(2):
                        for kc in range(KC):
                            at = (2 * t + kc) * P
                            mm = nc.tensor.matmul(p_o[:, n % 2, at:at + P], cT[:, n % 2, t, kc, :], proj[:, kc, :], start=True, stop=True)
                    mm.then_inc(s_o, 1)

            @block.scalar
            def _(act):
                act.wait_ge(s_prep, 10)
                nc.scalar.activation(rtr[:, :], tr[:, :], ACT.Sqrt).then_inc(s_rt, 1)
                for it in range(ITERS):
                    for kc in range(KC):
                        act.wait_ge(s_yz[kc], 2 * it + 2)
                        nc.scalar.copy(Z[:, (it + 1) % 2, kc, :, :], p_o[:, kc, 0:2 * P].rearrange("p (a n) -> p a n", a=2)).then_inc(s_new[kc], 1)
                for n in range(NT // 2):
                    act.wait_ge(s_t, n + 1)
                    if n >= 2:
                        act.wait_ge(s_o, n - 1)
                    nc.scalar.copy(cT[:, n % 2, :, :, :], p_t[:, n % 2, :].rearrange("p (t k n) -> p t k n", t=2, k=KC)
                                   ).then_inc(s_ct, 1)

            @block.vector
            def _(dve):
                mean_b = mean_sb[:, None, :].broadcast_to([P, CH, C])
                for i in range(NT // CH):
                    nc.vector.tensor_tensor(x2[:, i * CH:(i + 1) * CH, :], x2[:, i * CH:(i + 1) * CH, :], mean_b, ALU.subtract
                                            ).then_inc(s_c, 1)
                done = [0]

                def step(ins):
                    done[0] += 1
                    ins.then_inc(s_prep, 1)
                    dve.wait_ge(s_prep, done[0])

                dve.wait_ge(s_w, 16 * len(LOADS))
                dve.wait_ge(s_cov, 1)
                for kc in range(KC):
                    step(nc.vector.scalar_tensor_tensor(cov[:, kc, :], p_cov[kc][:, 0:P], 1.0 / ROWS, mask_sb[:, :], ALU.mult, ALU.mult))
                    step(nc.vector.scalar_tensor_tensor(cov[:, kc, :], ident_sb[:, :], 1e-5, cov[:, kc, :], ALU.mult, ALU.add))
                for kc in range(KC):
                    step(nc.vector.tensor_tensor(Wm[:, kc, 0, :], cov[:, kc, :], ident_sb[:, :], ALU.mult))
                    step(nc.vector.tensor_reduce(diag[:, kc:kc + 1], Wm[:, kc, 0, :], AX.X, ALU.add))
                step(nc.vector.tensor_scalar(i15[:, :], ident_sb[:, :], 1.5, None, ALU.mult))
                dve.wait_ge(s_tr, 1)
                step(nc.vector.tensor_copy(tr[:, :], p_t[:, 0, 0:KC]))
                step(nc.vector.reciprocal(itr[:, :], tr[:, :]))
                for kc in range(KC):
                    two = [P, 2, P]
                    nc.vector.tensor_scalar(Y[:, 0, kc, :, :], cov[:, kc:kc + 1, :].broadcast_to(two), itr[:, kc:kc + 1], None,
                                            ALU.mult).then_inc(s_new[kc], 1)
                    nc.vector.tensor_copy(Z[:, 0, kc, :, :], ident_sb[:, None, :].broadcast_to(two)).then_inc(s_new[kc], 1)
                for it in range(ITERS):
                    for kc in range(KC):
                        dve.wait_ge(s_zy[kc], it + 1)
                        nc.vector.scalar_tensor_tensor(Wm[:, kc, :, :], p_cov[kc][:, 0:2 * P].rearrange("p (a n) -> p a n", a=2), -0.5,
                                                       i15[:, None, :].broadcast_to(two), ALU.mult, ALU.add
                                                       ).then_inc(s_wm[kc], 1)
                    for kc in range(KC):
                        dve.wait_ge(s_yz[kc], 2 * it + 2)
                        nc.vector.tensor_copy(Y[:, (it + 1) % 2, kc, :, :], p_t[:, kc, 0:2 * P].rearrange("p (a n) -> p a n", a=2)).then_inc(s_new[kc], 1)
                dve.wait_ge(s_rt, 1)
                step(nc.vector.reciprocal(rtr[:, :], rtr[:, :]))
                for kc in range(KC):
                    dve.wait_ge(s_new[kc], 2 * ITERS + 2)
                    nc.vector.scalar_tensor_tensor(proj[:, kc, :], Z[:, ITERS % 2, kc, 0, :], rtr[:, kc:kc + 1],
                                                   g_sb[:, kc * P:(kc + 1) * P], ALU.mult, ALU.mult).then_inc(s_proj, 1)
                for n in range(NT // 2):
                    dve.wait_ge(s_o, n + 1)
                    if n >= 4:
                        dve.wait_ge(s_st[n % 4], 16 * (n // 4))
                    nc.vector.tensor_tensor(o_sb[:, n % 4, :, :], p_o[:, n % 2, :].rearrange("p (t c) -> p t c", t=2),
                                            b_sb[:, None, :].broadcast_to([P, 2, C]), ALU.add).then_inc(s_ob, 1)


def network(nc, a, out):
    def scratch(name, shape):
        return nc.dram_tensor(name, shape, F32, kind="Internal").ap()

    x0, x1 = scratch("x0", (B, N, C)), scratch("x1", (B, N, C))
    xn = scratch("xn", (SEQS, CHUNKS, P, KC, T))
    mix = scratch("mix", (SEQS, N, C))
    attention(nc, a["xT"], a["x"], a["wqT"], a["wkT"], a["bq"], a["bk"], a["wvT"], a["bv"], a["gamma"], a["ident"],
              a["halves"], x0)
    fourier_conv(nc, x0, a["w1T"], (a["bn1c"], a["bn1"]), a["fuT"], a["bnf"], a["lfuT"], a["bnl"], a["w2T"], a["dft"],
                 a["dftl"], a["idft"], a["idftl"], a["ident"], a["rms1"], a["thirds"], x1, xn)
    mamba(nc, xn, a["w_inT"], a["conv_w"], a["conv_b"], a["w_xT"], a["split"], a["w_dtT"], a["b_dt"], a["a_log"],
          a["d_skip"], a["w_outT"], a["ident"], a["pick"], a["keep"], mix)
    combine_and_whiten(nc, mix, x1, a["flips"], a["wf"], a["ln_w"], a["ln_b"], a["ident"], a["blocks"], a["gamma3"],
                       a["beta3"], out)


def fourier_matrices(np):
    def pair(n):
        w, k = np.arange(n)[:, None], np.arange(n // 2 + 1)[None]
        ang = 2 * np.pi * w * k / n
        weight = np.full((1, n // 2 + 1), 2.0)
        weight[0, 0] = weight[0, -1] = 1
        im = (-weight * np.sin(ang) / np.sqrt(n)).T
        im[0] = im[-1] = 0
        return np.cos(ang) / np.sqrt(n), -np.sin(ang) / np.sqrt(n), (weight * np.cos(ang) / np.sqrt(n)).T, im

    fr, fi, ir, ii = pair(W)
    dft, idft = np.zeros((P, 2, 2, FR)), np.zeros((2, FR, 2, P))
    for r in range(2):
        at = slice(r * W, (r + 1) * W)
        dft[at, 0, r], dft[at, 1, r], idft[r, :, 0, at], idft[r, :, 1, at] = fr, fi, ir, ii
    fr, fi, ir, ii = pair(W // 2)
    dftl, idftl = np.zeros((P, 2, 2, 2, FL)), np.zeros((2, FL, 2, P))
    for r in range(2):
        for half in range(2):
            at = slice(r * W + half * W // 2, r * W + (half + 1) * W // 2)
            dftl[at, half, 0, r], dftl[at, half, 1, r], idftl[r, :, 0, at], idftl[r, :, 1, at] = fr, fi, ir, ii
    f32 = np.float32
    return (dft.reshape(P, 4 * FR).astype(f32), idft.reshape(2 * FR, 2, P).astype(f32),
            dftl.reshape(P, 2, 4 * FL).astype(f32), idftl.reshape(2 * FL, 2, P).astype(f32))


def layouts(np, i):
    d = {}
    x = i["x"].reshape(B, N, C)
    d["x"], d["xT"] = x, x.transpose(0, 2, 1)

    d["wqT"], d["wkT"] = np.tile(i["L0_conv_Wq"].T, (1, 4)), np.tile(i["L0_conv_Wk"].T, (1, 4))
    d["bq"], d["bk"] = np.tile(i["L0_conv_bq"], 4)[:, None], np.tile(i["L0_conv_bk"], 4)[:, None]
    halves = np.array([[0, 0, 0, -1], [0, -1, -1, 0], [-1, 0, 0, 0], [-1, -1, 0, 0]], np.float32)
    d["halves"] = np.repeat(halves, CQ, 0)
    d["wvT"], d["bv"] = i["L0_conv_Wv"].T, np.broadcast_to(i["L0_conv_bv"], (P, C))
    d["gamma"] = np.broadcast_to(i["L0_conv_gamma"], (P, 1))
    d["ident"] = np.eye(P, dtype=np.float32)

    def parts(v):
        return np.concatenate([v[..., 0::2], v[..., 1::2]], -1)

    def bn(*names):
        return np.stack([i["L1_conv_" + n] for n in names])

    d["w1T"], d["w2T"] = i["L1_conv_w1"].T, i["L1_conv_w2"].T
    d["bn1"] = bn("g1", "b1", "m1", "v1")
    d["bn1c"] = d["bn1"].T
    d["bnf"] = parts(bn("fu_g", "fu_b", "fu_m", "fu_v"))
    d["bnl"] = parts(bn("lfu_g", "lfu_b", "lfu_m", "lfu_v"))
    d["fuT"] = parts(i["L1_conv_fu_w"].T.reshape(HC, 2, C))
    d["lfuT"] = parts(i["L1_conv_lfu_w"].T.reshape(HC, 2, C))
    d["dft"], d["idft"], d["dftl"], d["idftl"] = fourier_matrices(np)

    d["thirds"] = np.array([[0, 0], [-1, 0], [-1, -1]], np.float32)

    m = {k[len("L2_conv_"):]: v for k, v in i.items() if k.startswith("L2_conv_")}
    d["rms1"] = m["rms_w1"].reshape(KC, P).T

    def by_block(v):
        return v.reshape(IB, P, -1).transpose(1, 0, 2).reshape(P, -1)

    d["w_inT"], d["w_dtT"], d["w_outT"] = m["W_in"].T, m["W_dt"].T, m["W_out"].T
    d["conv_w"], d["conv_b"] = by_block(m["conv_w"]), by_block(m["conv_b"])
    wx = m["W_x"].T
    d["w_xT"] = np.concatenate([wx[:, RK:]] * 3 + [wx[:, :RK]], 1)
    d["b_dt"], d["a_log"], d["d_skip"] = by_block(m["b_dt"]), by_block(m["A_log"]), by_block(m["Dp"])
    copy = np.arange(P)[:, None] // (2 * NS)
    d["split"] = np.concatenate([np.where(copy >= 1, -1, 0), np.where(copy >= 2, -1, 0)], 1).astype(np.float32)
    d["pick"] = np.repeat(np.tile(np.eye(2 * NS, dtype=np.float32), (3, 1))[:, :, None], P, 2)
    d["keep"] = np.repeat((np.arange(SEQS * CHUNKS + 1)[None] % CHUNKS != 0).astype(np.float32), P, 0)

    def on_all(v):
        return np.broadcast_to(v.reshape(1, C), (P, C))

    d["wf"], d["ln_w"], d["ln_b"] = on_all(m["rms_wf"]), on_all(m["ln_w"]), on_all(m["ln_b"])
    d["gamma3"], d["beta3"] = on_all(i["L3_conv_gamma"]), on_all(i["L3_conv_beta"])
    t = np.arange(P)
    r, w = t // W, t % W
    sources = (r * W + W - 1 - w, (1 - r) * W + w, P - 1 - t)
    d["flips"] = np.stack([np.eye(P, dtype=np.float32)[:, s] for s in sources], 1)
    d["blocks"] = np.kron(np.eye(P // M), np.ones((M, M))).astype(np.float32)
    return {k: np.ascontiguousarray(v) for k, v in d.items()}


def kernel(**inputs):
    import numpy as np
    import concourse.bacc as bacc
    from concourse import mybir as mb
    from concourse.bass_utils import run_bass_kernel_spmd

    nc = bacc.Bacc("TRN2", target_bir_lowering=False, num_devices=1)
    arrays = {f"in_{k}": v for k, v in layouts(np, {k: np.asarray(v) for k, v in inputs.items()}).items()}
    a = {k[3:]: nc.dram_tensor(k, v.shape, mb.dt.from_np(v.dtype), kind="ExternalInput").ap() for k, v in arrays.items()}
    out = nc.dram_tensor("out_0", (B, N, C), F32, kind="ExternalOutput").ap()
    network(nc, a, out)
    r = run_bass_kernel_spmd(nc, [arrays], core_ids=[0])
    return r.results[0]["out_0"].reshape(B, H, W, C)
```
